# Optimizing a Trainium2 kernel written in Bass

```python
import numpy as np
import jax
import jax.numpy as jnp

def _softmax(x, axis=-1):
    return jax.nn.softmax(x, axis=axis)

def _gelu(x):
    return jax.nn.gelu(x, approximate=True)

def _silu(x):
    return jax.nn.silu(x)

def _sigmoid(x):
    return jax.nn.sigmoid(x)

def _layernorm(x, axis=-1, eps=1e-05):
    m = jnp.mean(x, axis=axis, keepdims=True)
    v = jnp.var(x, axis=axis, keepdims=True)
    return (x - m) / jnp.sqrt(v + eps)

def _scatter_add(tgt, idx, src, axis=0):
    return tgt.at[idx].add(src)

def _segment_sum(src, seg, n):
    return jax.ops.segment_sum(src, seg, n)
kernel_name = 'mk_prb_d1_jaxref_r8_56cd9b'

def setup_inputs(seed: int=0):
    np.random.seed(seed)
    _w = jnp.asarray

    def _L0_attn_setup():
        import jax, jax.numpy as jnp
        import numpy as np
        EMBED_DIM = 128
        NUM_HEADS = 8
        HEAD_DIM = EMBED_DIM // NUM_HEADS
        NUM_QUBITS = 8
        CIRCUITS = 4
        DEPTH = 3
        WAVELENGTHS = 16
        SCALING = HEAD_DIM ** (-0.5)
        ERR_MIN = 1e-06
        TWO_PI = 2.0 * np.pi

        def _quantum_encode(x, photonic_phases):
            hd = x.shape[-1]
            norm = jnp.sqrt(jnp.sum(x * x, axis=-1, keepdims=True))
            normed = x / jnp.maximum(norm, 1e-12)
            ch = jnp.arange(hd)
            phases = photonic_phases[ch % WAVELENGTHS, ch]
            return normed * jnp.exp(1j * phases)

        def _entangle(state, gates):
            for depth in range(DEPTH):
                g = gates[depth, :NUM_HEADS - 1]
                theta = g[:, 0][None, None, :, None]
                phi = g[:, 1][None, None, :, None]
                s1 = state[:, :, :-1]
                s2 = state[:, :, 1:]
                cos_t = jnp.cos(theta / 2)
                sin_t = jnp.sin(theta / 2)
                ctrl = jnp.abs(s1) ** 2
                rot = cos_t * s2 + sin_t * jnp.exp(1j * phi) * jnp.conj(s2)
                new = ctrl * rot + (1.0 - ctrl) * s2
                state = jnp.concatenate([new, state[:, :, -1:]], axis=2)
            return state

        def _forward(query, W_qkv, b_qkv, W_out, b_out, quantum_weights, photonic_phases, entanglement_gates, superposition_logits):
            B, S, E = query.shape
            qkv = query @ W_qkv.T + b_qkv
            q, k, v = jnp.split(qkv, 3, axis=-1)
            q = q.reshape(B, S, NUM_HEADS, HEAD_DIM)
            k = k.reshape(B, S, NUM_HEADS, HEAD_DIM)
            v = v.reshape(B, S, NUM_HEADS, HEAD_DIM)
            qq = _quantum_encode(q, photonic_phases)
            kq = _quantum_encode(k, photonic_phases)
            vq = _quantum_encode(v, photonic_phases)
            q_ent = _entangle(qq, entanglement_gates)
            k_ent = _entangle(kq, entanglement_gates)
            coh = jnp.exp(1j * jnp.angle(jnp.sum(vq, axis=2, keepdims=True)))
            sup_w = jax.nn.softmax(superposition_logits)
            final = None
            for c in range(CIRCUITS):
                ratio = 0.5 + 0.3 * jnp.sin(quantum_weights[c, 0, 0])
                qa = jnp.sqrt(ratio) * q_ent
                ka = jnp.sqrt(1.0 - ratio) * k_ent
                pattern = jnp.einsum('bsid,bsjd->bsij', jnp.conj(qa), ka)
                mod = pattern * jnp.exp(1j * quantum_weights[c, 1, :])
                scores = jnp.abs(mod) ** 2 * SCALING
                probs = jax.nn.softmax(scores, axis=-1)
                amps = jnp.sqrt(probs + 1e-12)
                coh_phase = jnp.angle(jnp.sum(scores, axis=-1, keepdims=True))
                w = amps * jnp.cos(coh_phase)
                weighted = jnp.einsum('bsij,bsjd->bsid', w.astype(jnp.complex64), vq)
                co = weighted * coh
                amp = jnp.clip(jnp.abs(co), ERR_MIN, 1.0)
                ph = jnp.mod(jnp.angle(co), TWO_PI)
                corrected = amp * jnp.exp(1j * ph)
                contrib = sup_w[c] * corrected
                final = contrib if final is None else final + contrib
            measured = jnp.real(final).reshape(B, S, E)
            return measured @ W_out.T + b_out
        key = jax.random.key(seed)
        ks = jax.random.split(key, 8)
        B, S, E = (2, 256, EMBED_DIM)
        return {'query': jax.random.normal(ks[0], (B, S, E), jnp.float32), 'W_qkv': jax.random.normal(ks[1], (3 * E, E), jnp.float32) / np.sqrt(E).astype(np.float32), 'b_qkv': jnp.zeros((3 * E,), jnp.float32), 'W_out': jax.random.normal(ks[2], (E, E), jnp.float32) / np.sqrt(E).astype(np.float32), 'b_out': jnp.zeros((E,), jnp.float32), 'quantum_weights': jax.random.normal(ks[3], (CIRCUITS, NUM_QUBITS, NUM_QUBITS), jnp.float32) * 0.1, 'photonic_phases': jax.random.normal(ks[4], (WAVELENGTHS, E), jnp.float32) * np.float32(np.pi), 'entanglement_gates': jax.random.normal(ks[5], (DEPTH, NUM_HEADS, 4), jnp.float32) * 0.1, 'superposition_logits': jax.random.normal(ks[6], (CIRCUITS,), jnp.float32)}
    _L0_attn_in = _L0_attn_setup()

    def _L0_ffn_setup():
        import jax, jax.numpy as jnp
        import numpy as np
        B, T, C = (8, 128, 128)
        H = 4 * C
        E = 8
        K = 2
        key = jax.random.key(seed)
        ks = jax.random.split(key, 7)
        s_in = 1.0 / np.sqrt(C)
        s_h = 1.0 / np.sqrt(H)
        x = jax.random.normal(ks[0], (B, T, C), dtype=jnp.float32)
        Wg = jax.random.normal(ks[1], (C, E), dtype=jnp.float32) * s_in
        W1 = jax.random.normal(ks[2], (E, C, H), dtype=jnp.float32) * s_in
        b1 = jax.random.normal(ks[3], (E, H), dtype=jnp.float32) * s_in
        W2 = jax.random.normal(ks[4], (E, H, C), dtype=jnp.float32) * s_h
        b2 = jax.random.normal(ks[5], (E, C), dtype=jnp.float32) * s_h
        return {'x': x, 'Wg': Wg, 'W1': W1, 'b1': b1, 'W2': W2, 'b2': b2}
    _L0_ffn_in = _L0_ffn_setup()
    _d = {'L0_attn_query': _L0_attn_in['query'], 'L0_attn_W_qkv': _L0_attn_in['W_qkv'], 'L0_attn_b_qkv': _L0_attn_in['b_qkv'], 'L0_attn_W_out': _L0_attn_in['W_out'], 'L0_attn_b_out': _L0_attn_in['b_out'], 'L0_attn_quantum_weights': _L0_attn_in['quantum_weights'], 'L0_attn_photonic_phases': _L0_attn_in['photonic_phases'], 'L0_attn_entanglement_gates': _L0_attn_in['entanglement_gates'], 'L0_attn_superposition_logits': _L0_attn_in['superposition_logits'], 'L0_ffn_Wg': _L0_ffn_in['Wg'], 'L0_ffn_W1': _L0_ffn_in['W1'], 'L0_ffn_b1': _L0_ffn_in['b1'], 'L0_ffn_W2': _L0_ffn_in['W2'], 'L0_ffn_b2': _L0_ffn_in['b2']}
    _x0 = _d['L0_attn_query']
    _d['L0_attn_query'] = jax.random.normal(jax.random.fold_in(jax.random.key(seed), 1), (16, 512, 128), dtype=_x0.dtype)
    del _x0
    return _d

def reference(L0_attn_query, L0_attn_W_qkv, L0_attn_b_qkv, L0_attn_W_out, L0_attn_b_out, L0_attn_quantum_weights, L0_attn_photonic_phases, L0_attn_entanglement_gates, L0_attn_superposition_logits, L0_ffn_Wg, L0_ffn_W1, L0_ffn_b1, L0_ffn_W2, L0_ffn_b2):

    def _L0_attn_ref(query, W_qkv, b_qkv, W_out, b_out, quantum_weights, photonic_phases, entanglement_gates, superposition_logits):
        import jax, jax.numpy as jnp
        import numpy as np
        EMBED_DIM = 128
        NUM_HEADS = 8
        HEAD_DIM = EMBED_DIM // NUM_HEADS
        NUM_QUBITS = 8
        CIRCUITS = 4
        DEPTH = 3
        WAVELENGTHS = 16
        SCALING = HEAD_DIM ** (-0.5)
        ERR_MIN = 1e-06
        TWO_PI = 2.0 * np.pi

        def _quantum_encode(x, photonic_phases):
            hd = x.shape[-1]
            norm = jnp.sqrt(jnp.sum(x * x, axis=-1, keepdims=True))
            normed = x / jnp.maximum(norm, 1e-12)
            ch = jnp.arange(hd)
            phases = photonic_phases[ch % WAVELENGTHS, ch]
            return normed * jnp.exp(1j * phases)

        def _entangle(state, gates):
            for depth in range(DEPTH):
                g = gates[depth, :NUM_HEADS - 1]
                theta = g[:, 0][None, None, :, None]
                phi = g[:, 1][None, None, :, None]
                s1 = state[:, :, :-1]
                s2 = state[:, :, 1:]
                cos_t = jnp.cos(theta / 2)
                sin_t = jnp.sin(theta / 2)
                ctrl = jnp.abs(s1) ** 2
                rot = cos_t * s2 + sin_t * jnp.exp(1j * phi) * jnp.conj(s2)
                new = ctrl * rot + (1.0 - ctrl) * s2
                state = jnp.concatenate([new, state[:, :, -1:]], axis=2)
            return state

        def _forward(query, W_qkv, b_qkv, W_out, b_out, quantum_weights, photonic_phases, entanglement_gates, superposition_logits):
            B, S, E = query.shape
            qkv = query @ W_qkv.T + b_qkv
            q, k, v = jnp.split(qkv, 3, axis=-1)
            q = q.reshape(B, S, NUM_HEADS, HEAD_DIM)
            k = k.reshape(B, S, NUM_HEADS, HEAD_DIM)
            v = v.reshape(B, S, NUM_HEADS, HEAD_DIM)
            qq = _quantum_encode(q, photonic_phases)
            kq = _quantum_encode(k, photonic_phases)
            vq = _quantum_encode(v, photonic_phases)
            q_ent = _entangle(qq, entanglement_gates)
            k_ent = _entangle(kq, entanglement_gates)
            coh = jnp.exp(1j * jnp.angle(jnp.sum(vq, axis=2, keepdims=True)))
            sup_w = jax.nn.softmax(superposition_logits)
            final = None
            for c in range(CIRCUITS):
                ratio = 0.5 + 0.3 * jnp.sin(quantum_weights[c, 0, 0])
                qa = jnp.sqrt(ratio) * q_ent
                ka = jnp.sqrt(1.0 - ratio) * k_ent
                pattern = jnp.einsum('bsid,bsjd->bsij', jnp.conj(qa), ka)
                mod = pattern * jnp.exp(1j * quantum_weights[c, 1, :])
                scores = jnp.abs(mod) ** 2 * SCALING
                probs = jax.nn.softmax(scores, axis=-1)
                amps = jnp.sqrt(probs + 1e-12)
                coh_phase = jnp.angle(jnp.sum(scores, axis=-1, keepdims=True))
                w = amps * jnp.cos(coh_phase)
                weighted = jnp.einsum('bsij,bsjd->bsid', w.astype(jnp.complex64), vq)
                co = weighted * coh
                amp = jnp.clip(jnp.abs(co), ERR_MIN, 1.0)
                ph = jnp.mod(jnp.angle(co), TWO_PI)
                corrected = amp * jnp.exp(1j * ph)
                contrib = sup_w[c] * corrected
                final = contrib if final is None else final + contrib
            measured = jnp.real(final).reshape(B, S, E)
            return measured @ W_out.T + b_out
        return _forward(query, W_qkv, b_qkv, W_out, b_out, quantum_weights, photonic_phases, entanglement_gates, superposition_logits)

    def _L0_ffn_ref(x, Wg, W1, b1, W2, b2):
        import jax, jax.numpy as jnp
        import numpy as np
        B, T, C = (8, 128, 128)
        H = 4 * C
        E = 8
        K = 2
        Bb, Tt, Cc = x.shape
        x_flat = x.reshape(-1, Cc)
        scores = x_flat @ Wg
        topk_scores, topk_idx = jax.lax.top_k(scores, K)
        topk_w = jax.nn.softmax(topk_scores, axis=-1)
        cw = (jax.nn.one_hot(topk_idx, E, dtype=x.dtype) * topk_w[..., None]).sum(axis=1)
        y = jnp.zeros_like(x_flat)
        for e in range(E):
            h = jax.nn.gelu(x_flat @ W1[e] + b1[e], approximate=False)
            out_e = h @ W2[e] + b2[e]
            y = y + cw[:, e:e + 1] * out_e
        return y.reshape(Bb, Tt, Cc)
    x = L0_attn_query
    xn = _layernorm(x, axis=-1)
    x = x + _L0_attn_ref(xn, L0_attn_W_qkv, L0_attn_b_qkv, L0_attn_W_out, L0_attn_b_out, L0_attn_quantum_weights, L0_attn_photonic_phases, L0_attn_entanglement_gates, L0_attn_superposition_logits) + _L0_ffn_ref(xn, L0_ffn_Wg, L0_ffn_W1, L0_ffn_b1, L0_ffn_W2, L0_ffn_b2)
    return x

_drawn_inputs = setup_inputs


def setup_inputs(seed=0):
    import zlib

    import numpy as np

    out = dict(_drawn_inputs(seed))
    spreads = {'L0_attn_b_qkv': (0.0, 0.552), 'L0_attn_b_out': (0.0, 0.1)}
    factors = {'L0_attn_quantum_weights': 8.0,
     'L0_attn_entanglement_gates': 8.0,
     'L0_attn_superposition_logits': 8.0}
    for name, (base, spread) in spreads.items():
        noise = np.random.default_rng([zlib.crc32(name.encode()), seed]).standard_normal(out[name].shape)
        drawn = base * np.exp(spread * noise) if base else spread * noise
        out[name] = jnp.asarray(drawn.astype(out[name].dtype))
    for name, factor in factors.items():
        out[name] = (out[name] * factor).astype(out[name].dtype)
    return out
```

```python
import math
from contextlib import ExitStack

import concourse.bass as bass
from concourse import mybir

ALU = mybir.AluOpType
ACT = mybir.ActivationFunctionType
F32 = mybir.dt.float32
AX_X = mybir.AxisListType.X

P = 128
T = 4
BT = P * T
C = 128
NH = 8
HD = C // NH
NT = NH - 1
NC = 4
DEPTH = 3
E = 8
HID = 512
HC = HID // P
QKV = 3 * C
PROJ = QKV + E
GQ = 2 * T

ANGLES = dict(gamma=(0, 128), eta=(128, 112), theta=(240, 21), turn=(261, 8), twop=(269, 16), p=(285, 16), qw=(301, 4))
NANG = 305
TWO_PI = 2.0 * math.pi
PI_HI = 6.28125
PI_MID = 0.0019350051879882812
PI_LO = TWO_PI - PI_HI - PI_MID
ROUND = 1.5 * 2.0 ** 23
PI_IN = 3.1415925


class Blk:

    def __init__(self, pair, slot):
        self.pair, self.slot = pair, slot
        self.value = pair * 2 + slot
        self.number = self.value if type(pair) is int else None

    def plus(self, n):
        return Blk(self.pair + (self.slot + n) // 2, (self.slot + n) % 2)

    def older(self, n):
        return self.number is None or self.number >= n

    def exists(self, nblocks):
        return self.number is None or 0 <= self.number < nblocks


class Signal:

    def __init__(self, sem, per):
        self.sem, self.per = sem, per

    def value(self, k, n=None):
        return k.value * self.per + (self.per if n is None else n)


class SlotSignal:

    def __init__(self, sems):
        self.sems = sems

    def of(self, k):
        return self.sems[k.slot]

    def value(self, k):
        return k.pair * 16 + 16


def bc_mid(ap, n):
    return ap.unsqueeze(1).to_broadcast([ap.shape[0], n, ap.shape[1]])


def bc_last(ap, n):
    return ap.unsqueeze(2).to_broadcast([ap.shape[0], ap.shape[1], n])


def build(nc, query, W_qkv, b_qkv, W_out, b_out, quantum_weights, photonic_phases, entanglement_gates,
          superposition_logits, Wg, W1, b1, W2, b2, out):
    B, S, _ = query.shape
    NB = B * S // BT
    LOOP_FROM, LOOP_TO = 1, NB // 2 - 1

    x_dram = query.rearrange("b s c -> (b s) c")
    out_dram = out.rearrange("b s c -> (b s) c")

    with ExitStack() as ctx:
        def sb(name, shape):
            return ctx.enter_context(nc.sbuf_tensor(name, shape, F32))

        def psum(name, shape):
            return ctx.enter_context(nc.psum_tensor(name, shape, F32))

        def sem(name):
            return ctx.enter_context(nc.semaphore(name))

        def signal(name, per=1):
            return Signal(sem(name), per)

        ident = sb("ident", [P, P])
        ones = sb("ones", [P, P])
        w_proj = sb("w_proj", [P, PROJ])
        b_proj = sb("b_proj", [1, PROJ])
        w_outT = sb("w_outT", [P, C])
        w1 = sb("w1", [P, E, HID])
        w2 = sb("w2", [P, E, HC, C])
        b1_rows = sb("b1_rows", [E * HC, P])
        b1_cols = sb("b1_cols", [P, E * HC])
        b_rows = sb("b_rows", [E + 1, C])
        prow = sb("prow", [1, 120])
        par = sb("par", [P, 120])
        half = sb("half", [P, 96])
        psi = sb("psi", [P, NH])
        phi_psi = sb("phi_psi", [P, NT])
        fr1 = sb("fr1", [P, NH])
        fr2 = sb("fr2", [P, NH])
        ang = sb("ang", [P, NANG])
        kk = sb("kk", [P, NANG])
        rem = sb("rem", [P, NANG])
        sin_t = sb("sin_t", [P, NANG])
        cos_t = sb("cos_t", [P, NANG])
        alpha = sb("alpha", [P, DEPTH * NT])
        a_plus = sb("a_plus", [P, DEPTH * NT])
        a_minus = sb("a_minus", [P, DEPTH * NT])
        k1x = sb("k1x", [P, NT * HD])
        k1y = sb("k1y", [P, NT * HD])
        k_tmp = sb("k_tmp", [P, 4, NT * HD])
        ratio = sb("ratio", [P, 2, NC])
        gain = sb("gain", [P, NC])
        sup = sb("sup", [P, NC])
        sup_tmp = sb("sup_tmp", [P, 8])
        eps_ln = sb("eps_ln", [P, 1])
        eps_amp = sb("eps_amp", [P, 1])
        tiny = sb("tiny", [P, 1])
        rank = sb("rank", [P, E])

        x_sb = sb("x_sb", [P, 2, T, C])
        stats = sb("stats", [P, T, 6])
        moments = sb("moments", [P, 3, T])
        sd = sb("sd", [P, T])
        rstd = sb("rstd", [P, T])
        xn = sb("xn", [P, T, C])
        xnT = sb("xnT", [P, 2, BT])
        qkv = sb("qkv", [P, T, PROJ])
        ss = sb("ss", [P, 2, T * 3 * NH])
        norm = sb("norm", [P, T * 3 * NH])
        rnorm = sb("rnorm", [P, T * 3 * NH])
        a0 = sb("a0", [P, GQ, C])
        vT = sb("vT", [P, 2, T, HD, NH])
        vsum = sb("vsum", [P, T, HD])
        f_tmp = sb("f_tmp", [P, 3, T, HD])
        phase = sb("phase", [P, 2, T, HD])
        r_tmp = sb("r_tmp", [P, 4, T, E])
        r_one = sb("r_one", [P, 8, T])
        cw = sb("cw", [P, 2, T, E + 1])
        cwT = sb("cwT", [E + 1, 2, BT])
        sqx = sb("sqx", [P, GQ, NT * HD])
        sqy = sb("sqy", [P, GQ, NT * HD])
        x1 = sb("x1", [P, GQ, C])
        y1 = sb("y1", [P, GQ, C])
        xy2 = sb("xy2", [P, 2, GQ, C])
        x2, y2 = xy2[:, 0], xy2[:, 1]
        sq = xy2.rearrange("p a g c -> p (a g c)")[:, 0:T * QKV].rearrange("p (t c) -> p t c", t=T)
        m1 = sb("m1", [P, GQ, C])
        m2 = sb("m2", [P, GQ, C])
        zp, zm = m1[:, :, 0:NT * HD], m2[:, :, 0:NT * HD]
        fx = sb("fx", [P, 2, GQ, C])
        fy = sb("fy", [P, 2, GQ, C])
        qsum = sb("qsum", [P, T, C])
        kdif = sb("kdif", [P, T, C])
        prod = sb("prod", [P, 2, 2048])
        pat = sb("pat", [P, T, 3, NH * NH])
        pr = sb("pr", [P, 3, T, NH * NH])
        power = sb("power", [P, T, NH * NH])
        rowmax = sb("rowmax", [P, T * NH])
        below = sb("below", [P, T, NH * NH])
        expo = sb("expo", [P, T, NC, NH * NH])
        zsum = sb("zsum", [P, T * NC * NH])
        rz = sb("rz", [P, T * NC * NH])
        u = sb("u", [P, T, NC, C])
        u_sgn = sb("u_sgn", [P, T, NC, C])
        msum = sb("msum", [P, T, C])
        meas = sb("meas", [P, T, C])
        measT = sb("measT", [P, BT])
        hid = sb("hid", [P, 2, HC, BT])
        wqkv_rows = hid[:, 0, 0, 0:QKV].rearrange("p (r c) -> p r c", r=3)
        wout_rows = hid[:, 0, 0, QKV:QKV + C]
        gated = sb("gated", [P, 2, T, C])
        yacc = sb("yacc", [P, 2, T, C])

        ps_h = psum("ps_h", [P, 2, 512])
        ps_y = psum("ps_y", [P, 2, 512])
        ps_proj = psum("ps_proj", [P, 2, 512])
        ps_t = psum("ps_t", [P, 512])
        ps_o = psum("ps_o", [P, 512])

        weights_in = sem("weights_in")
        params_in = sem("params_in")
        small_in = sem("small_in")
        experts_in = sem("experts_in")
        ident_made = sem("ident_made")
        ones_made = sem("ones_made")
        setup_psum = sem("setup_psum")
        setup_copied = sem("setup_copied")
        const_step = sem("const_step")
        angles_reduced = sem("angles_reduced")
        angles_folded = sem("angles_folded")
        logits_shifted = sem("logits_shifted")
        const_act = sem("const_act")
        entangle_consts = sem("entangle_consts")
        consts_ready = sem("consts_ready")
        x_loaded = SlotSignal([sem("x_loaded_0"), sem("x_loaded_1")])
        ln_step = signal("ln_step", T + 7)
        sd_ready = signal("sd_ready")
        xn_ready = signal("xn_ready", T)
        xT_psum = signal("xT_psum")
        xnT_ready = signal("xnT_ready")
        proj_psum = signal("proj_psum", T)
        qkv_ready = signal("qkv_ready", T)
        sq_ready = signal("sq_ready", T)
        ss_step = signal("ss_step", 2)
        norm_ready = signal("norm_ready")
        rnorm_step = signal("rnorm_step", 2)
        a0_ready = signal("a0_ready")
        v_ready = signal("v_ready")
        phase_step = signal("phase_step", 5)
        router_step = signal("router_step", 16)
        phase_ready = signal("phase_ready")
        router_diff = signal("router_diff")
        router_exp = signal("router_exp")
        cw_ready = signal("cw_ready")
        ctrl0_ready = signal("ctrl0_ready")
        depth0 = signal("depth0", 8)
        sq1_ready = signal("sq1_ready", 4)
        depth1 = signal("depth1", 13)
        sq2_ready = signal("sq2_ready", 4)
        depth2 = signal("depth2", 7)
        mixed_ready = signal("mixed_ready", 2)
        prod_ready = signal("prod_ready", 3 * T)
        pat_ready = signal("pat_ready", T + T // 2)
        power_step = signal("power_step", 6)
        below_step = signal("below_step", 2)
        exp_ready = signal("exp_ready", NC)
        probs_step = signal("probs_step", 3)
        amp_ready = signal("amp_ready")
        wprod_ready = signal("wprod_ready", 2 * T)
        u_ready = signal("u_ready", 2 * T)
        hidden_psum = signal("hidden_psum", E * HC)
        hidden_ready = signal("hidden_ready", E * HC)
        expert_psum = signal("expert_psum", E)
        gated_ready = signal("gated_ready", E)
        y_added = signal("y_added", E)
        cwT_psum = signal("cwT_psum")
        cwT_ready = signal("cwT_ready")
        abs_ready = signal("abs_ready", T)
        sgn_ready = signal("sgn_ready", T)
        clip_ready = signal("clip_ready")
        mix_ready = signal("mix_ready", NC)
        msum_step = signal("msum_step", NC - 1)
        meas_ready = signal("meas_ready")
        mT_psum = signal("mT_psum")
        mT_ready = signal("mT_ready")
        o_psum = signal("o_psum")
        out_ready = signal("out_ready")
        stored = SlotSignal([sem("stored_0"), sem("stored_1")])

        block = ctx.enter_context(nc.Block())

        def run_steps(eng, step):
            for n in range(-2, 2 * LOOP_FROM):
                step(Blk(n // 2, n % 2))
            with eng.Fori(LOOP_FROM, LOOP_TO) as pair:
                for slot in range(2):
                    step(Blk(pair, slot))
            for n in range(2 * LOOP_TO, NB + 1):
                step(Blk(n // 2, n % 2))

        def ang_of(table, name):
            at, n = ANGLES[name]
            return table[:, at:at + n]

        def heads(ap):
            return ap.rearrange("p g (h d) -> p g h d", d=HD)

        @block.sync
        def _(sp):
            def load_x(k):
                if k.older(2):
                    sp.wait_ge(y_added.sem, y_added.value(k.plus(-2), 1))
                src = x_dram[bass.ds(k.value * BT, BT), :].rearrange("(t p) c -> p t c", p=P)
                sp.dma_start(x_sb[:, k.slot], src).then_inc(x_loaded.of(k), 16)

            def store(k):
                sp.wait_ge(out_ready.sem, out_ready.value(k))
                dst = out_dram[bass.ds(k.value * BT, BT), :].rearrange("(t p) c -> p t c", p=P)
                sp.dma_start(dst, yacc[:, k.slot]).then_inc(stored.of(k), 16)

            load_x(Blk(0, 0))
            sp.dma_start(wqkv_rows, W_qkv.rearrange("(r p) c -> p r c", p=P)).then_inc(weights_in, 16)
            sp.dma_start(wout_rows, W_out).then_inc(weights_in, 16)
            sp.dma_start(w_proj[:, QKV:PROJ], Wg).then_inc(weights_in, 16)
            flat = photonic_phases.rearrange("a b -> (a b)")
            diag = flat[0:(HD - 1) * (C + 1) + 1:C + 1]
            sp.dma_start(prow[:, 0:16], diag.unsqueeze(0), allow_slow_non_contiguous=True).then_inc(params_in, 16)
            sp.dma_start(prow[:, 16:112], entanglement_gates.rearrange("a b c -> (a b c)").unsqueeze(0)).then_inc(params_in, 16)
            sp.dma_start(prow[:, 112:116], quantum_weights[:, 0, 0].unsqueeze(0), allow_slow_non_contiguous=True).then_inc(params_in, 16)
            sp.dma_start(prow[:, 116:120], superposition_logits.unsqueeze(0)).then_inc(params_in, 16)
            sp.dma_start(b_proj[:, 0:QKV], b_qkv.unsqueeze(0)).then_inc(small_in, 16)
            sp.dma_start(b1_rows[:], b1.rearrange("e (c p) -> (e c) p", p=P)).then_inc(small_in, 16)
            sp.dma_start(b_rows[0:E, :], b2).then_inc(small_in, 16)
            sp.dma_start(b_rows[E:E + 1, :], b_out.unsqueeze(0)).then_inc(small_in, 16)
            sp.dma_start(w1[:], W1.rearrange("e c h -> c e h")).then_inc(experts_in, 16)
            sp.dma_start(w2[:], W2.rearrange("e (c p) n -> p e c n", p=P)).then_inc(experts_in, 16)

            def step(k):
                if k.plus(-2).exists(NB):
                    store(k.plus(-2))
                if k.plus(2).exists(NB) and not (k.number is not None and k.number < -1):
                    load_x(k.plus(2))

            run_steps(sp, step)
            store(Blk((NB - 1) // 2, (NB - 1) % 2))
            for last in (NB - 2, NB - 1):
                sp.wait_ge(stored.of(Blk(last // 2, last % 2)), stored.value(Blk(last // 2, last % 2)))

        @block.tensor
        def _(pe):
            pe.wait_ge(ident_made, 2)
            pe.wait_ge(weights_in, 48)
            for r in range(3):
                last = nc.tensor.transpose(ps_h[:, 0, r * P:(r + 1) * P], wqkv_rows[:, r, :], ident[:])
            last = nc.tensor.transpose(ps_h[:, 0, 3 * P:4 * P], wout_rows, ident[:])
            last.then_inc(setup_psum, 1)
            pe.wait_ge(params_in, 64)
            pe.wait_ge(ones_made, 1)
            nc.tensor.matmul(ps_y[:, 0, 0:120], ones[0:1, :], prow[:], start=True, stop=True).then_inc(setup_psum, 1)
            pe.wait_ge(small_in, 64)
            nc.tensor.transpose(ps_y[:, 1, 0:E * HC], b1_rows[:], ident[0:E * HC, 0:E * HC]).then_inc(setup_psum, 1)

            def experts(k, e):
                if e == 0:
                    pe.wait_ge(xnT_ready.sem, xnT_ready.value(k))
                    if k.number == 0:
                        pe.wait_ge(experts_in, 32)
                        pe.wait_ge(setup_copied, 3)
                for c in range(HC):
                    n = e * HC + c
                    if n >= 2:
                        pe.wait_ge(hidden_ready.sem, hidden_ready.value(k, n - 1))
                    elif k.older(1):
                        pe.wait_ge(hidden_ready.sem, hidden_ready.value(k.plus(-1), E * HC + n - 1))
                    nc.tensor.matmul(ps_h[:, n % 2, :], w1[:, e, c * P:(c + 1) * P], xnT[:, k.slot, :],
                                     start=True, stop=True).then_inc(hidden_psum.sem, 1)
                    if e > 0:
                        expert_out(k, e - 1, c)

            def expert_out(k, e, t):
                if t == 0:
                    if e >= 2:
                        pe.wait_ge(gated_ready.sem, gated_ready.value(k, e - 1))
                    elif k.older(1):
                        pe.wait_ge(gated_ready.sem, gated_ready.value(k.plus(-1), E + e - 1))
                    elif e == 0:
                        pe.wait_ge(setup_copied, 4)
                    pe.wait_ge(hidden_ready.sem, hidden_ready.value(k, (e + 1) * HC))
                for c in range(HC):
                    last = nc.tensor.matmul(ps_y[:, e % 2, t * P:(t + 1) * P], hid[:, e % 2, c, t * P:(t + 1) * P],
                                            w2[:, e, c, :], start=(c == 0), stop=(c == HC - 1))
                if t == T - 1:
                    last.then_inc(expert_psum.sem, 1)

            def turn_x(k):
                pe.wait_ge(xn_ready.sem, xn_ready.value(k))
                if k.older(2):
                    pe.wait_ge(cwT_ready.sem, cwT_ready.value(k.plus(-2)))
                elif k.older(1):
                    pe.wait_ge(xnT_ready.sem, xnT_ready.value(k.plus(-1)))
                for t in range(T):
                    last = nc.tensor.transpose(ps_t[:, t * P:(t + 1) * P], xn[:, t, :], ident[:])
                last.then_inc(xT_psum.sem, 1)

            def project(k):
                pe.wait_ge(xnT_ready.sem, xnT_ready.value(k))
                if k.number == 0:
                    pe.wait_ge(setup_copied, 3)
                    pe.wait_ge(small_in, 64)
                for t in range(T):
                    if t >= 2:
                        pe.wait_ge(sq_ready.sem, sq_ready.value(k, t - 1))
                    elif k.older(1):
                        pe.wait_ge(sq_ready.sem, sq_ready.value(k.plus(-1), T + t - 1))
                    nc.tensor.matmul(ps_proj[:, t % 2, 0:PROJ], xnT[:, k.slot, t * P:(t + 1) * P], w_proj[:],
                                     start=True, stop=False)
                    nc.tensor.matmul(ps_proj[:, t % 2, 0:PROJ], ones[0:1, :], b_proj[:],
                                     start=False, stop=True).then_inc(proj_psum.sem, 1)

            def turn_cw(k):
                pe.wait_ge(cw_ready.sem, cw_ready.value(k))
                if k.older(1):
                    pe.wait_ge(mT_ready.sem, mT_ready.value(k.plus(-1)))
                else:
                    pe.wait_ge(xnT_ready.sem, xnT_ready.value(k.plus(1)))
                for t in range(T):
                    last = nc.tensor.transpose(ps_t[0:E + 1, t * P:(t + 1) * P], cw[:, k.slot, t, :], ident[:])
                last.then_inc(cwT_psum.sem, 1)

            def turn_m(k):
                pe.wait_ge(meas_ready.sem, meas_ready.value(k))
                if k.plus(2).exists(NB):
                    pe.wait_ge(xnT_ready.sem, xnT_ready.value(k.plus(2)))
                else:
                    pe.wait_ge(cwT_ready.sem, cwT_ready.value(k))
                for t in range(T):
                    last = nc.tensor.transpose(ps_t[:, t * P:(t + 1) * P], meas[:, t, :], ident[:])
                last.then_inc(mT_psum.sem, 1)

            def project_out(k):
                pe.wait_ge(mT_ready.sem, mT_ready.value(k))
                pe.wait_ge(cwT_ready.sem, cwT_ready.value(k))
                if k.older(1):
                    pe.wait_ge(out_ready.sem, out_ready.value(k.plus(-1)))
                for t in range(T):
                    cols = slice(t * P, (t + 1) * P)
                    nc.tensor.matmul(ps_o[:, cols], measT[:, cols], w_outT[:], start=True, stop=False)
                    last = nc.tensor.matmul(ps_o[:, cols], cwT[:, k.slot, cols], b_rows[:], start=False, stop=True)
                last.then_inc(o_psum.sem, 1)

            def step(k):
                n, o, far = k.plus(1), k.plus(-1), k.plus(2)
                front, main, tail = n.exists(NB), k.exists(NB), o.exists(NB)
                if front:
                    project(n)
                if main:
                    experts(k, 0)
                    experts(k, 1)
                    experts(k, 2)
                if tail:
                    turn_m(o)
                if main:
                    experts(k, 3)
                if tail:
                    project_out(o)
                if main:
                    experts(k, 4)
                    turn_cw(k)
                    for e in range(5, E):
                        experts(k, e)
                    for t in range(T):
                        expert_out(k, E - 1, t)
                if far.exists(NB):
                    turn_x(far)

            run_steps(pe, step)

        @block.scalar
        def _(act):
            act.wait_ge(setup_psum, 1)
            act.activation(w_proj[:, 0:QKV], ps_h[:, 0, 0:QKV], ACT.Copy).then_inc(setup_copied, 1)
            act.activation(w_outT[:], ps_h[:, 0, QKV:QKV + C], ACT.Copy).then_inc(setup_copied, 1)
            act.wait_ge(setup_psum, 2)
            act.activation(par[:], ps_y[:, 0, 0:120], ACT.Copy).then_inc(setup_copied, 1)
            act.wait_ge(setup_psum, 3)
            act.activation(b1_cols[:], ps_y[:, 1, 0:E * HC], ACT.Copy).then_inc(setup_copied, 1)
            act.wait_ge(angles_reduced, 1)
            act.activation(sin_t[:], rem[:], ACT.Sin).then_inc(const_act, 1)
            act.activation(kk[:], rem[:], ACT.Abs).then_inc(const_act, 1)
            act.wait_ge(angles_folded, 1)
            act.activation(cos_t[:], kk[:], ACT.Sin).then_inc(const_act, 1)
            act.wait_ge(logits_shifted, 1)
            act.activation(sup_tmp[:, 4:8], sup_tmp[:, 0:4], ACT.Exp).then_inc(const_act, 1)

            def ln_sd(k):
                act.wait_ge(ln_step.sem, ln_step.value(k, T + 6))
                if k.older(1):
                    act.wait_ge(ln_step.sem, ln_step.value(k.plus(-1)))
                if k.number == 0:
                    act.wait_ge(consts_ready, 1)
                act.activation(sd[:], moments[:, 2], ACT.Sqrt, bias=eps_ln[:, 0:1], scale=1.0 / C).then_inc(sd_ready.sem, 1)

            def copy_xT(k):
                act.wait_ge(xT_psum.sem, xT_psum.value(k))
                if k.older(2):
                    o = k.plus(-2)
                    act.wait_ge(hidden_psum.sem, hidden_psum.value(o))
                act.activation(xnT[:, k.slot, :], ps_t[:], ACT.Copy).then_inc(xnT_ready.sem, 1)

            def copy_proj(k):
                if k.older(1):
                    o = k.plus(-1)
                    act.wait_ge(v_ready.sem, v_ready.value(o))
                    act.wait_ge(a0_ready.sem, a0_ready.value(o))
                    act.wait_ge(router_step.sem, router_step.value(o, 6))
                    act.wait_ge(ss_step.sem, ss_step.value(o, 1))
                    act.wait_ge(depth1.sem, depth1.value(o))
                for t in range(T):
                    act.wait_ge(proj_psum.sem, proj_psum.value(k, t + 1))
                    act.activation(qkv[:, t, :], ps_proj[:, t % 2, 0:PROJ], ACT.Copy).then_inc(qkv_ready.sem, 1)
                    act.activation(sq[:, t, :], ps_proj[:, t % 2, 0:QKV], ACT.Square).then_inc(sq_ready.sem, 1)

            def norm_sqrt(k):
                act.wait_ge(ss_step.sem, ss_step.value(k))
                if k.older(1):
                    act.wait_ge(rnorm_step.sem, rnorm_step.value(k.plus(-1), 1))
                act.activation(norm[:], ss[:, 1, :], ACT.Sqrt).then_inc(norm_ready.sem, 1)

            def control0(k):
                act.wait_ge(a0_ready.sem, a0_ready.value(k))
                if k.older(1):
                    act.wait_ge(depth2.sem, depth2.value(k.plus(-1), 3))
                act.activation(sqx[:], a0[:, :, 0:NT * HD], ACT.Square).then_inc(ctrl0_ready.sem, 1)

            def control1(k):
                act.wait_ge(depth0.sem, depth0.value(k))
                act.activation(sqx[:], x1[:, :, 0:NT * HD], ACT.Square).then_inc(sq1_ready.sem, 1)
                act.activation(sqy[:], y1[:, :, 0:NT * HD], ACT.Square).then_inc(sq1_ready.sem, 1)
                act.activation(x2[:, :, NT * HD:C], x1[:, :, NT * HD:C], ACT.Copy).then_inc(sq1_ready.sem, 1)
                act.activation(y2[:, :, NT * HD:C], y1[:, :, NT * HD:C], ACT.Copy).then_inc(sq1_ready.sem, 1)

            def control2(k):
                act.wait_ge(depth1.sem, depth1.value(k))
                if k.older(2):
                    act.wait_ge(pat_ready.sem, pat_ready.value(k.plus(-2)))
                act.activation(sqx[:], x1[:, :, 0:NT * HD], ACT.Square).then_inc(sq2_ready.sem, 1)
                act.activation(sqy[:], y1[:, :, 0:NT * HD], ACT.Square).then_inc(sq2_ready.sem, 1)
                act.activation(fx[:, k.slot, :, NT * HD:C], x1[:, :, NT * HD:C], ACT.Copy).then_inc(sq2_ready.sem, 1)
                act.activation(fy[:, k.slot, :, NT * HD:C], y1[:, :, NT * HD:C], ACT.Copy).then_inc(sq2_ready.sem, 1)

            def router_softmax(k):
                act.wait_ge(router_diff.sem, router_diff.value(k))
                if k.older(1):
                    act.wait_ge(cw_ready.sem, cw_ready.value(k.plus(-1)))
                act.activation(r_one[:, 3, :], r_one[:, 2, :], ACT.Exp).then_inc(router_exp.sem, 1)

            def score_exp(k):
                act.wait_ge(below_step.sem, below_step.value(k))
                if k.older(1):
                    act.wait_ge(wprod_ready.sem, wprod_ready.value(k.plus(-1)))
                for c in range(NC):
                    act.activation(expo[:, :, c, :], below[:], ACT.Exp,
                                   scale=gain[:, c:c + 1]).then_inc(exp_ready.sem, 1)

            def amplitude(k):
                act.wait_ge(probs_step.sem, probs_step.value(k))
                act.activation(expo[:], expo[:], ACT.Sqrt, bias=eps_amp[:, 0:1]).then_inc(amp_ready.sem, 1)

            def abs_sign(k, t):
                act.wait_ge(u_ready.sem, u_ready.value(k, 2 * (t + 1)))
                if k.older(1):
                    act.wait_ge(msum_step.sem, msum_step.value(k.plus(-1)))
                act.activation(u_sgn[:, t], u[:, t], ACT.Sign, bias=tiny[:, 0:1]).then_inc(sgn_ready.sem, 1)
                act.wait_ge(sgn_ready.sem, sgn_ready.value(k, t + 1))
                act.activation(u[:, t], u[:, t], ACT.Abs).then_inc(abs_ready.sem, 1)

            def gelu(k, e):
                for c in range(HC):
                    n = e * HC + c
                    act.wait_ge(hidden_psum.sem, hidden_psum.value(k, n + 1))
                    if c == 0:
                        if e >= 2:
                            act.wait_ge(expert_psum.sem, expert_psum.value(k, e - 1))
                        elif k.older(1):
                            act.wait_ge(expert_psum.sem, expert_psum.value(k.plus(-1), E + e - 1))
                    act.activation(hid[:, e % 2, c, :], ps_h[:, n % 2, :], ACT.Gelu,
                                   bias=b1_cols[:, n:n + 1]).then_inc(hidden_ready.sem, 1)

            def gate(k, e):
                act.wait_ge(expert_psum.sem, expert_psum.value(k, e + 1))
                if e == 0:
                    act.wait_ge(cw_ready.sem, cw_ready.value(k))
                if e >= 2:
                    act.wait_ge(y_added.sem, y_added.value(k, e - 1))
                elif k.older(1):
                    act.wait_ge(y_added.sem, y_added.value(k.plus(-1), E + e - 1))
                for t in range(T):
                    last = act.activation(gated[:, e % 2, t, :], ps_y[:, e % 2, t * P:(t + 1) * P], ACT.Copy,
                                          scale=cw[:, k.slot, t, e:e + 1])
                last.then_inc(gated_ready.sem, 1)

            def copy_cwT(k):
                act.wait_ge(cwT_psum.sem, cwT_psum.value(k))
                if k.older(2):
                    act.wait_ge(o_psum.sem, o_psum.value(k.plus(-2)))
                act.activation(cwT[:, k.slot, :], ps_t[0:E + 1, :], ACT.Copy).then_inc(cwT_ready.sem, 1)

            def copy_mT(k):
                act.wait_ge(mT_psum.sem, mT_psum.value(k))
                if k.older(1):
                    act.wait_ge(o_psum.sem, o_psum.value(k.plus(-1)))
                act.activation(measT[:], ps_t[:], ACT.Copy).then_inc(mT_ready.sem, 1)

            def step(k):
                n, o, far = k.plus(1), k.plus(-1), k.plus(2)
                front, main, tail = n.exists(NB), k.exists(NB), o.exists(NB)
                if front:
                    copy_proj(n)
                    norm_sqrt(n)
                if main:
                    gelu(k, 0)
                if front:
                    control0(n)
                if tail:
                    abs_sign(o, T - 1)
                if main:
                    gelu(k, 1)
                    gate(k, 0)
                if front:
                    control1(n)
                if main:
                    gelu(k, 2)
                    gate(k, 1)
                if tail:
                    copy_mT(o)
                if main:
                    gelu(k, 3)
                    gate(k, 2)
                    score_exp(k)
                if front:
                    router_softmax(n)
                if main:
                    amplitude(k)
                    gelu(k, 4)
                    gate(k, 3)
                if front:
                    control2(n)
                if main:
                    copy_cwT(k)
                    gelu(k, 5)
                    gate(k, 4)
                    abs_sign(k, 0)
                if far.exists(NB):
                    ln_sd(far)
                if main:
                    gelu(k, 6)
                    gate(k, 5)
                    abs_sign(k, 1)
                    gelu(k, 7)
                    gate(k, 6)
                    gate(k, 7)
                if far.exists(NB):
                    copy_xT(far)
                if main:
                    abs_sign(k, 2)

            run_steps(act, step)

        @block.gpsimd
        def _(pool):
            pool.memset(ident[:], 0.0).then_inc(ident_made, 1)
            pool.memset(ones[:], 1.0).then_inc(ones_made, 1)
            pool.wait_ge(ident_made, 1)
            pool.affine_select(out=ident[:], in_=ident[:], compare_op=ALU.not_equal, fill=1.0, base=0,
                               pattern=[[-1, P]], channel_multiplier=1).then_inc(ident_made, 1)

            def tt(out_, a, b, op, sig):
                pool.tensor_tensor(out_, a, b, op).then_inc(sig.sem, 1)

            def const_hd(ap):
                return bc_mid(ap, GQ)

            def const_h(ap):
                n = ap.shape[1]
                return ap.unsqueeze(1).unsqueeze(3).to_broadcast([P, GQ, n, HD])

            low, high = slice(0, NT * HD), slice(HD, C)

            def entangle0(k):
                if k.number == 0:
                    pool.wait_ge(entangle_consts, 1)
                pool.wait_ge(ctrl0_ready.sem, ctrl0_ready.value(k))
                tt(zp, sqx[:], const_hd(k1x[:]), ALU.mult, depth0)
                tt(zm, sqx[:], const_hd(k1y[:]), ALU.mult, depth0)
                gx, gy = ang_of(cos_t, "gamma"), ang_of(sin_t, "gamma")
                tt(x1[:, :, NT * HD:C], a0[:, :, NT * HD:C], const_hd(gx[:, NT * HD:C]), ALU.mult, depth0)
                tt(y1[:, :, NT * HD:C], a0[:, :, NT * HD:C], const_hd(gy[:, NT * HD:C]), ALU.mult, depth0)
                pool.wait_ge(depth0.sem, depth0.value(k, 4))
                tt(zp, zp, const_hd(gx[:, low]), ALU.add, depth0)
                tt(zm, zm, const_hd(gy[:, low]), ALU.add, depth0)
                pool.wait_ge(depth0.sem, depth0.value(k, 6))
                tt(x1[:, :, low], zp, a0[:, :, high], ALU.mult, depth0)
                tt(y1[:, :, low], zm, a0[:, :, high], ALU.mult, depth0)

            def grow(k, sig, base, depth, dst_x, dst_y):
                tt(sqx[:], sqx[:], sqy[:], ALU.add, sig)
                pool.wait_ge(sig.sem, sig.value(k, base + 1))
                ap, am = a_plus[:, depth * NT:(depth + 1) * NT], a_minus[:, depth * NT:(depth + 1) * NT]
                tt(heads(zp), heads(sqx[:]), const_h(ap), ALU.mult, sig)
                tt(heads(zm), heads(sqx[:]), const_h(am), ALU.mult, sig)
                pool.wait_ge(sig.sem, sig.value(k, base + 3))
                tt(zp, zp, x1[:, :, high], ALU.mult, sig)
                tt(zm, zm, y1[:, :, high], ALU.mult, sig)
                pool.wait_ge(sig.sem, sig.value(k, base + 5))
                tt(dst_x, zp, x1[:, :, high], ALU.add, sig)
                tt(dst_y, zm, y1[:, :, high], ALU.add, sig)

            def entangle1(k):
                pool.wait_ge(depth0.sem, depth0.value(k))
                pool.wait_ge(sq1_ready.sem, sq1_ready.value(k))
                grow(k, depth1, 0, 1, x2[:, :, low], y2[:, :, low])
                pool.wait_ge(depth1.sem, depth1.value(k, 7))
                ct, st = const_h(ang_of(cos_t, "turn")), const_h(ang_of(sin_t, "turn"))
                tt(heads(m1[:]), heads(x2), ct, ALU.mult, depth1)
                tt(heads(m2[:]), heads(y2), st, ALU.mult, depth1)
                pool.wait_ge(depth1.sem, depth1.value(k, 9))
                tt(x1[:], m1[:], m2[:], ALU.subtract, depth1)
                pool.wait_ge(depth1.sem, depth1.value(k, 10))
                tt(heads(m1[:]), heads(x2), st, ALU.mult, depth1)
                tt(heads(m2[:]), heads(y2), ct, ALU.mult, depth1)
                pool.wait_ge(depth1.sem, depth1.value(k, 12))
                tt(y1[:], m1[:], m2[:], ALU.add, depth1)

            def entangle2(k):
                pool.wait_ge(depth1.sem, depth1.value(k))
                pool.wait_ge(sq2_ready.sem, sq2_ready.value(k))
                grow(k, depth2, 0, 2, fx[:, k.slot, :, low], fy[:, k.slot, :, low])

            def add_expert(k, e):
                pool.wait_ge(gated_ready.sem, gated_ready.value(k, e + 1))
                if e == 0 and k.older(2):
                    pool.wait_ge(stored.of(k), stored.value(k.plus(-2)))
                if e > 0:
                    pool.wait_ge(y_added.sem, y_added.value(k, e))
                base = x_sb[:, k.slot] if e == 0 else yacc[:, k.slot]
                tt(yacc[:, k.slot], gated[:, e % 2], base, ALU.add, y_added)

            def sum_circuits(k):
                if k.older(1):
                    pool.wait_ge(meas_ready.sem, meas_ready.value(k.plus(-1)))
                for c in range(1, NC):
                    pool.wait_ge(mix_ready.sem, mix_ready.value(k, c + 1))
                    if c > 1:
                        pool.wait_ge(msum_step.sem, msum_step.value(k, c - 1))
                    tt(msum[:], u_sgn[:, :, 0, :] if c == 1 else msum[:], u_sgn[:, :, c, :], ALU.add, msum_step)

            def step(k):
                n, o = k.plus(1), k.plus(-1)
                front, main, tail = n.exists(NB), k.exists(NB), o.exists(NB)
                if front:
                    entangle0(n)
                if main:
                    add_expert(k, 0)
                if tail:
                    sum_circuits(o)
                if front:
                    entangle1(n)
                if main:
                    for e in range(1, 5):
                        add_expert(k, e)
                if front:
                    entangle2(n)
                if main:
                    for e in range(5, E):
                        add_expert(k, e)

            run_steps(pool, step)

        @block.vector
        def _(dve):
            steps = [0]

            def const(ins, named=None):
                if named is None:
                    steps[0] += 1
                    ins.then_inc(const_step, 1)
                    dve.wait_ge(const_step, steps[0])
                else:
                    ins.then_inc(named, 1)
                    dve.wait_ge(named, 1)

            const(dve.memset(eps_ln[:], 1e-5))
            const(dve.memset(eps_amp[:], 1e-12))
            const(dve.memset(tiny[:], 1e-30))
            for j in range(E):
                const(dve.memset(rank[:, j:j + 1], float(E - j)))
            for slot in range(2):
                const(dve.memset(cw[:, slot, :, E:E + 1], 1.0))
            const(dve.memset(b_proj[:, QKV:PROJ], 0.0), consts_ready)

            dve.wait_ge(setup_copied, 3)
            phases = par[:, 0:HD]
            gates = par[:, 16:112].rearrange("p (a h c) -> p a h c", a=DEPTH, h=NH)
            halves = half[:].rearrange("p (a h c) -> p a h c", a=DEPTH, h=NH)
            const(dve.tensor_scalar(half[:], par[:, 16:112], 0.5, None, ALU.mult))
            const(dve.tensor_copy(psi[:, 1:NH], halves[:, 1, 0:NT, 1]))
            const(dve.tensor_copy(psi[:, 0:1], halves[:, 0, 0:1, 1]))
            const(dve.tensor_tensor(phi_psi[:], gates[:, 0, 0:NT, 1], psi[:, 0:NT], ALU.subtract))
            const(dve.tensor_tensor(ang_of(ang, "gamma").rearrange("p (h d) -> p h d", d=HD), bc_mid(phases, NH),
                                    bc_last(psi[:], HD), ALU.subtract))
            const(dve.tensor_tensor(ang_of(ang, "eta").rearrange("p (h d) -> p h d", d=HD), bc_last(phi_psi[:], HD),
                                    bc_mid(phases, NT), ALU.subtract))
            const(dve.tensor_copy(ang_of(ang, "theta").rearrange("p (a h) -> p a h", a=DEPTH), halves[:, :, 0:NT, 0]))
            const(dve.tensor_copy(fr1[:, 0:NT], halves[:, 1, 0:NT, 1]))
            const(dve.tensor_copy(fr1[:, NT:NH], halves[:, 1, NT - 1:NT, 1]))
            const(dve.tensor_copy(fr2[:, 1:NH], halves[:, 2, 0:NT, 1]))
            const(dve.tensor_copy(fr2[:, 0:1], halves[:, 1, 0:1, 1]))
            const(dve.tensor_tensor(ang_of(ang, "turn"), fr1[:], fr2[:], ALU.subtract))
            const(dve.tensor_scalar(ang_of(ang, "twop"), phases, 2.0, None, ALU.mult))
            const(dve.tensor_copy(ang_of(ang, "p"), phases))
            const(dve.tensor_copy(ang_of(ang, "qw"), par[:, 112:116]))
            const(dve.tensor_scalar(kk[:], ang[:], 1.0 / TWO_PI, ROUND, ALU.mult, ALU.add))
            const(dve.tensor_scalar(kk[:], kk[:], ROUND, None, ALU.subtract))
            const(dve.scalar_tensor_tensor(rem[:], kk[:], -PI_HI, ang[:], ALU.mult, ALU.add))
            const(dve.scalar_tensor_tensor(rem[:], kk[:], -PI_MID, rem[:], ALU.mult, ALU.add))
            const(dve.scalar_tensor_tensor(rem[:], kk[:], -PI_LO, rem[:], ALU.mult, ALU.add))
            const(dve.tensor_scalar(rem[:], rem[:], PI_IN, -PI_IN, ALU.min, ALU.max), angles_reduced)
            dve.wait_ge(const_act, 2)
            const(dve.tensor_scalar(kk[:], kk[:], -1.0, math.pi / 2, ALU.mult, ALU.add), angles_folded)
            const(dve.tensor_reduce(ratio[:, 0, 0:1], par[:, 116:120], AX_X, ALU.max))
            const(dve.tensor_scalar(sup_tmp[:, 0:4], par[:, 116:120], ratio[:, 0, 0:1], None, ALU.subtract),
                  logits_shifted)
            dve.wait_ge(const_act, 4)
            const(dve.tensor_reduce(ratio[:, 0, 0:1], sup_tmp[:, 4:8], AX_X, ALU.add))
            const(dve.reciprocal(ratio[:, 0, 1:2], ratio[:, 0, 0:1]))
            const(dve.tensor_scalar(sup[:], sup_tmp[:, 4:8], ratio[:, 0, 1:2], None, ALU.mult))
            const(dve.tensor_scalar(ratio[:, 0, :], ang_of(sin_t, "qw"), 0.3, 0.5, ALU.mult, ALU.add))
            const(dve.tensor_scalar(ratio[:, 1, :], ratio[:, 0, :], -1.0, 1.0, ALU.mult, ALU.add))
            const(dve.scalar_tensor_tensor(gain[:], ratio[:, 0, :], HD ** -0.5, ratio[:, 1, :], ALU.mult, ALU.mult))
            const(dve.tensor_scalar(alpha[:], ang_of(cos_t, "theta"), 1.0, None, ALU.subtract))
            const(dve.tensor_tensor(a_plus[:], alpha[:], ang_of(sin_t, "theta"), ALU.add))
            const(dve.tensor_tensor(a_minus[:], alpha[:], ang_of(sin_t, "theta"), ALU.subtract))
            for n, (table, name, factor) in enumerate(((cos_t, "gamma", alpha[:, 0:NT]),
                                                       (cos_t, "eta", ang_of(sin_t, "theta")[:, 0:NT]),
                                                       (sin_t, "gamma", alpha[:, 0:NT]),
                                                       (sin_t, "eta", ang_of(sin_t, "theta")[:, 0:NT]))):
                const(dve.tensor_tensor(k_tmp[:, n].rearrange("p (h d) -> p h d", d=HD),
                                        ang_of(table, name)[:, 0:NT * HD].rearrange("p (h d) -> p h d", d=HD),
                                        bc_last(factor, HD), ALU.mult))
            const(dve.tensor_tensor(k1x[:], k_tmp[:, 0], k_tmp[:, 1], ALU.add))
            const(dve.tensor_tensor(k1y[:], k_tmp[:, 2], k_tmp[:, 3], ALU.add), entangle_consts)

            def tt(out_, a, b, op, sig):
                dve.tensor_tensor(out_, a, b, op).then_inc(sig.sem, 1)

            def layer_norm_stats(k):
                dve.wait_ge(x_loaded.of(k), x_loaded.value(k))
                for t in range(T):
                    dve.bn_stats(stats[:, t, :], x_sb[:, k.slot, t, :]).then_inc(ln_step.sem, 1)
                dve.wait_ge(ln_step.sem, ln_step.value(k, T))
                tt(moments[:, 0], stats[:, :, 1], stats[:, :, 4], ALU.add, ln_step)
                tt(moments[:, 1], stats[:, :, 1], stats[:, :, 4], ALU.subtract, ln_step)
                tt(moments[:, 2], stats[:, :, 2], stats[:, :, 5], ALU.add, ln_step)
                dve.wait_ge(ln_step.sem, ln_step.value(k, T + 3))
                dve.scalar_tensor_tensor(moments[:, 1], moments[:, 1], C / 4.0, moments[:, 1],
                                         ALU.mult, ALU.mult).then_inc(ln_step.sem, 1)
                dve.tensor_scalar(moments[:, 0], moments[:, 0], 0.5, None, ALU.mult).then_inc(ln_step.sem, 1)
                dve.wait_ge(ln_step.sem, ln_step.value(k, T + 4))
                tt(moments[:, 2], moments[:, 1], moments[:, 2], ALU.add, ln_step)

            def layer_norm(k):
                dve.wait_ge(sd_ready.sem, sd_ready.value(k))
                dve.reciprocal(rstd[:], sd[:]).then_inc(ln_step.sem, 1)
                dve.wait_ge(ln_step.sem, ln_step.value(k))
                if k.older(1):
                    dve.wait_ge(xT_psum.sem, xT_psum.value(k.plus(-1)))
                for t in range(T):
                    dve.tensor_scalar(xn[:, t, :], x_sb[:, k.slot, t, :], moments[:, 0, t:t + 1], rstd[:, t:t + 1],
                                      ALU.subtract, ALU.mult).then_inc(xn_ready.sem, 1)

            def norm_squares(k):
                dve.wait_ge(sq_ready.sem, sq_ready.value(k))
                dve.tensor_reduce(ss[:, 0, :], sq.rearrange("p t (g d) -> p (t g) d", d=HD), AX_X,
                                  ALU.add).then_inc(ss_step.sem, 1)
                dve.wait_ge(ss_step.sem, ss_step.value(k, 1))
                dve.tensor_scalar(ss[:, 1, :], ss[:, 0, :], 1e-24, None, ALU.max).then_inc(ss_step.sem, 1)

            def normalise(k):
                dve.wait_ge(norm_ready.sem, norm_ready.value(k))
                dve.tensor_scalar(rnorm[:], norm[:], 1e-12, None, ALU.max).then_inc(rnorm_step.sem, 1)
                dve.wait_ge(rnorm_step.sem, rnorm_step.value(k, 1))
                dve.reciprocal(rnorm[:], rnorm[:]).then_inc(rnorm_step.sem, 1)
                dve.wait_ge(rnorm_step.sem, rnorm_step.value(k))
                if k.older(1):
                    dve.wait_ge(depth0.sem, depth0.value(k.plus(-1)))
                rn = rnorm[:].rearrange("p (t g) -> p t g", t=T)
                tt(a0[:].rearrange("p (t q) (h d) -> p t (q h) d", t=T, d=HD),
                   qkv[:, :, 0:2 * C].rearrange("p t (g d) -> p t g d", d=HD),
                   rn[:, :, 0:2 * NH].unsqueeze(3).to_broadcast([P, T, 2 * NH, HD]), ALU.mult, a0_ready)
                tt(vT[:, k.slot].rearrange("p t d j -> p t j d"),
                   qkv[:, :, 2 * C:QKV].rearrange("p t (g d) -> p t g d", d=HD),
                   rn[:, :, 2 * NH:3 * NH].unsqueeze(3).to_broadcast([P, T, NH, HD]), ALU.mult, v_ready)

            def value_phase(k):
                dve.wait_ge(v_ready.sem, v_ready.value(k))
                dve.tensor_reduce(vsum[:], vT[:, k.slot], AX_X, ALU.add).then_inc(phase_step.sem, 1)
                dve.wait_ge(phase_step.sem, phase_step.value(k, 1))
                dve.tensor_scalar(f_tmp[:, 0], vsum[:], 0.0, None, ALU.is_gt).then_inc(phase_step.sem, 1)
                dve.scalar_tensor_tensor(f_tmp[:, 2], vsum[:], 0.0, bc_mid(ang_of(cos_t, "p"), T),
                                         ALU.is_equal, ALU.mult).then_inc(phase_step.sem, 1)
                dve.wait_ge(phase_step.sem, phase_step.value(k, 2))
                dve.scalar_tensor_tensor(f_tmp[:, 1], vsum[:], 0.0, f_tmp[:, 0],
                                         ALU.is_lt, ALU.subtract).then_inc(phase_step.sem, 1)
                dve.wait_ge(phase_step.sem, phase_step.value(k, 4))
                tt(f_tmp[:, 1], f_tmp[:, 1], bc_mid(ang_of(cos_t, "twop"), T), ALU.mult, phase_step)
                dve.wait_ge(phase_step.sem, phase_step.value(k))
                tt(phase[:, k.slot], f_tmp[:, 2], f_tmp[:, 1], ALU.subtract, phase_ready)

            def route(k):
                done = [0]

                def link(ins):
                    done[0] += 1
                    ins.then_inc(router_step.sem, 1)
                    dve.wait_ge(router_step.sem, router_step.value(k, done[0]))

                def wide(ap):
                    return bc_last(ap, E)

                dve.wait_ge(qkv_ready.sem, qkv_ready.value(k))
                s = qkv[:, :, QKV:PROJ]
                order = bc_mid(rank[:], T)
                best, second, first_at, second_at = (r_one[:, n, :] for n in (0, 4, 1, 5))
                is_first, is_second, rest, tmp = (r_tmp[:, n] for n in range(4))
                link(dve.tensor_reduce(best, s, AX_X, ALU.max))
                link(dve.tensor_tensor(tmp, s, wide(best), ALU.is_equal))
                link(dve.tensor_tensor(tmp, tmp, order, ALU.mult))
                link(dve.tensor_reduce(first_at, tmp, AX_X, ALU.max))
                link(dve.tensor_tensor(is_first, tmp, wide(first_at), ALU.is_equal))
                link(dve.scalar_tensor_tensor(rest, is_first, -3e38, s, ALU.mult, ALU.add))
                link(dve.tensor_reduce(second, rest, AX_X, ALU.max))
                dve.tensor_tensor(r_one[:, 2, :], second, best, ALU.subtract).then_inc(router_diff.sem, 1)
                link(dve.tensor_tensor(tmp, rest, wide(second), ALU.is_equal))
                link(dve.tensor_tensor(tmp, tmp, order, ALU.mult))
                link(dve.tensor_reduce(second_at, tmp, AX_X, ALU.max))
                link(dve.tensor_tensor(is_second, tmp, wide(second_at), ALU.is_equal))

            def route_weights(k):
                done = [11]

                def link(ins):
                    done[0] += 1
                    ins.then_inc(router_step.sem, 1)
                    dve.wait_ge(router_step.sem, router_step.value(k, done[0]))

                dve.wait_ge(router_exp.sem, router_exp.value(k))
                if k.older(2):
                    dve.wait_ge(gated_ready.sem, gated_ready.value(k.plus(-2)))
                    dve.wait_ge(cwT_psum.sem, cwT_psum.value(k.plus(-2)))
                w_one, w_two = r_one[:, 7, :], r_one[:, 6, :]
                link(dve.tensor_scalar(w_two, r_one[:, 3, :], 1.0, None, ALU.add))
                link(dve.reciprocal(w_one, w_two))
                link(dve.tensor_tensor(w_two, r_one[:, 3, :], w_one, ALU.mult))
                link(dve.tensor_tensor(r_tmp[:, 2], r_tmp[:, 0], bc_last(w_one, E), ALU.mult))
                link(dve.tensor_tensor(r_tmp[:, 3], r_tmp[:, 1], bc_last(w_two, E), ALU.mult))
                tt(cw[:, k.slot, :, 0:E], r_tmp[:, 2], r_tmp[:, 3], ALU.add, cw_ready)

            def mix_parts(k):
                dve.wait_ge(depth2.sem, depth2.value(k))
                dve.wait_ge(sq2_ready.sem, sq2_ready.value(k))
                vx = fx[:, k.slot].rearrange("p (t q) c -> p t q c", t=T)
                vy = fy[:, k.slot].rearrange("p (t q) c -> p t q c", t=T)
                tt(qsum[:], vx[:, :, 0, :], vy[:, :, 0, :], ALU.add, mixed_ready)
                tt(kdif[:], vy[:, :, 1, :], vx[:, :, 1, :], ALU.subtract, mixed_ready)

            UNITS = [[(0, 0), (0, 1)], [(1, 0), (1, 1)], [(0, 2), (1, 2)], [(2, 0), (2, 1)], [(3, 0), (3, 1)],
                     [(2, 2), (3, 2)]]

            def pattern_products(k, m):
                if m == 0:
                    dve.wait_ge(mixed_ready.sem, mixed_ready.value(k))
                if m >= 2:
                    dve.wait_ge(pat_ready.sem, pat_ready.value(k, m - 1))
                for n, (t, kind) in enumerate(UNITS[m]):
                    q, kq = ((fx[:, k.slot, 2 * t, :], fx[:, k.slot, 2 * t + 1, :]),
                             (fy[:, k.slot, 2 * t, :], fy[:, k.slot, 2 * t + 1, :]),
                             (qsum[:, t, :], kdif[:, t, :]))[kind]
                    dst = prod[:, m % 2, n * 1024:(n + 1) * 1024].rearrange("p (i j d) -> p i j d", i=NH, j=NH)
                    tt(dst, q.rearrange("p (i d) -> p i d", d=HD).unsqueeze(2).to_broadcast([P, NH, NH, HD]),
                       kq.rearrange("p (j d) -> p j d", d=HD).unsqueeze(1).to_broadcast([P, NH, NH, HD]),
                       ALU.mult, prod_ready)

            def pattern_sums(k, m):
                dve.wait_ge(prod_ready.sem, prod_ready.value(k, 2 * (m + 1)))
                (t, kind), (t2, _) = UNITS[m]
                dst = pat[:, t, 0:2, :] if t == t2 else pat[:, t:t2 + 1, 2, :]
                dve.tensor_reduce(dst, prod[:, m % 2, :].rearrange("p (n g d) -> p n g d", n=2, d=HD), AX_X,
                                  ALU.add).then_inc(pat_ready.sem, 1)

            def pattern_power(k):
                dve.wait_ge(pat_ready.sem, pat_ready.value(k))
                a, b, c = (pat[:, :, n, :] for n in range(3))
                tt(pr[:, 1], a, b, ALU.subtract, power_step)
                tt(pr[:, 0], a, b, ALU.add, power_step)
                dve.wait_ge(power_step.sem, power_step.value(k, 1))
                tt(pr[:, 2], pr[:, 1], c, ALU.add, power_step)
                dve.wait_ge(power_step.sem, power_step.value(k, 2))
                tt(pr[:, 0], pr[:, 0], pr[:, 0], ALU.mult, power_step)
                dve.wait_ge(power_step.sem, power_step.value(k, 3))
                tt(pr[:, 1], pr[:, 2], pr[:, 2], ALU.mult, power_step)
                dve.wait_ge(power_step.sem, power_step.value(k, 5))
                tt(power[:], pr[:, 0], pr[:, 1], ALU.add, power_step)
                dve.wait_ge(power_step.sem, power_step.value(k))
                rows = power[:].rearrange("p t (i j) -> p (t i) j", j=NH)
                dve.tensor_reduce(rowmax[:], rows, AX_X, ALU.max).then_inc(below_step.sem, 1)
                dve.wait_ge(below_step.sem, below_step.value(k, 1))
                tt(below[:].rearrange("p t (i j) -> p (t i) j", j=NH), rows, bc_last(rowmax[:], NH),
                   ALU.subtract, below_step)

            def probabilities(k):
                dve.wait_ge(exp_ready.sem, exp_ready.value(k))
                rows = expo[:].rearrange("p t c (i j) -> p (t c i) j", j=NH)
                dve.tensor_reduce(zsum[:], rows, AX_X, ALU.add).then_inc(probs_step.sem, 1)
                dve.wait_ge(probs_step.sem, probs_step.value(k, 1))
                dve.reciprocal(rz[:], zsum[:]).then_inc(probs_step.sem, 1)
                dve.wait_ge(probs_step.sem, probs_step.value(k, 2))
                tt(rows, rows, bc_last(rz[:], NH), ALU.mult, probs_step)

            def weighted_products(k, m):
                t, c = m // 2, 2 * (m % 2)
                if m == 0:
                    dve.wait_ge(amp_ready.sem, amp_ready.value(k))
                if m >= 2:
                    dve.wait_ge(u_ready.sem, u_ready.value(k, m - 1))
                w = expo[:, t, c:c + 2, :].rearrange("p c (i j) -> p (c i) j", j=NH)
                tt(prod[:, m % 2, :].rearrange("p (g d j) -> p g d j", d=HD, j=NH),
                   w.unsqueeze(2).to_broadcast([P, 2 * NH, HD, NH]),
                   vT[:, k.slot, t].unsqueeze(1).to_broadcast([P, 2 * NH, HD, NH]), ALU.mult, wprod_ready)

            def weighted_sums(k, m):
                t, c = m // 2, 2 * (m % 2)
                dve.wait_ge(wprod_ready.sem, wprod_ready.value(k, m + 1))
                dve.tensor_reduce(u[:, t, c:c + 2, :].rearrange("p c e -> p (c e)"),
                                  prod[:, m % 2, :].rearrange("p (g j) -> p g j", j=NH), AX_X,
                                  ALU.add).then_inc(u_ready.sem, 1)

            def clip_and_mix(k):
                dve.wait_ge(abs_ready.sem, abs_ready.value(k))
                dve.wait_ge(sgn_ready.sem, sgn_ready.value(k))
                dve.tensor_scalar(u[:], u[:], 1e-6, 1.0, ALU.max, ALU.min).then_inc(clip_ready.sem, 1)
                dve.wait_ge(clip_ready.sem, clip_ready.value(k))
                for c in range(NC):
                    dve.scalar_tensor_tensor(u_sgn[:, :, c, :], u[:, :, c, :], sup[:, c:c + 1], u_sgn[:, :, c, :],
                                             ALU.mult, ALU.mult).then_inc(mix_ready.sem, 1)

            def measure(k):
                dve.wait_ge(msum_step.sem, msum_step.value(k))
                if k.older(1):
                    dve.wait_ge(mT_psum.sem, mT_psum.value(k.plus(-1)))
                tt(meas[:].rearrange("p t (i d) -> p t i d", d=HD), msum[:].rearrange("p t (i d) -> p t i d", d=HD),
                   phase[:, k.slot].unsqueeze(2).to_broadcast([P, T, NH, HD]), ALU.mult, meas_ready)

            def add_out(k):
                dve.wait_ge(o_psum.sem, o_psum.value(k))
                dve.wait_ge(y_added.sem, y_added.value(k))
                tt(yacc[:, k.slot], ps_o[:].rearrange("p (t c) -> p t c", t=T), yacc[:, k.slot], ALU.add, out_ready)

            def step(k):
                n, o, far = k.plus(1), k.plus(-1), k.plus(2)
                front, main, tail = n.exists(NB), k.exists(NB), o.exists(NB)
                if main:
                    mix_parts(k)
                    pattern_products(k, 0)
                    pattern_products(k, 1)
                if front:
                    norm_squares(n)
                if main:
                    pattern_sums(k, 0)
                if front:
                    normalise(n)
                if main:
                    pattern_products(k, 2)
                    pattern_sums(k, 1)
                if tail:
                    clip_and_mix(o)
                if main:
                    pattern_products(k, 3)
                    pattern_sums(k, 2)
                    pattern_products(k, 4)
                    pattern_sums(k, 3)
                if tail:
                    measure(o)
                if main:
                    pattern_products(k, 5)
                    pattern_sums(k, 4)
                    pattern_sums(k, 5)
                    pattern_power(k)
                if front:
                    route(n)
                if main:
                    probabilities(k)
                if front:
                    value_phase(n)
                    route_weights(n)
                if tail:
                    add_out(o)
                if main:
                    weighted_products(k, 0)
                    for m in range(1, 2 * T):
                        weighted_products(k, m)
                        weighted_sums(k, m - 1)
                        if m == 3 and far.exists(NB):
                            layer_norm_stats(far)
                        if m == 5 and far.exists(NB):
                            layer_norm(far)
                    weighted_sums(k, 2 * T - 1)
                elif far.exists(NB):
                    layer_norm_stats(far)
                    layer_norm(far)

            run_steps(dve, step)


_INS = ["query", "W_qkv", "b_qkv", "W_out", "b_out", "quantum_weights", "photonic_phases", "entanglement_gates",
        "superposition_logits"]
_FFN = ["Wg", "W1", "b1", "W2", "b2"]


def kernel(**inputs):
    import numpy as _np
    import concourse.bacc as _bacc
    from concourse import mybir as _mybir
    from concourse.bass_utils import run_bass_kernel_spmd as _run

    nc = _bacc.Bacc("TRN2", target_bir_lowering=False, num_devices=1)
    arrays, args = {}, []
    for name in ["L0_attn_" + n for n in _INS] + ["L0_ffn_" + n for n in _FFN]:
        a = _np.ascontiguousarray(inputs[name])
        arrays[f"in_{name}_dram"] = a
        args.append(nc.dram_tensor(f"in_{name}_dram", a.shape, _mybir.dt.from_np(a.dtype), kind="ExternalInput").ap())
    shape = inputs["L0_attn_query"].shape
    args.append(nc.dram_tensor("out_0_dram", shape, _mybir.dt.float32, kind="ExternalOutput").ap())
    build(nc, *args)
    r = _run(nc, [arrays], core_ids=[0])
    return r.results[0]["out_0_dram"]
```

```python
import math
from contextlib import ExitStack

import concourse.bass as bass
from concourse import mybir

ALU = mybir.AluOpType
ACT = mybir.ActivationFunctionType
F32 = mybir.dt.float32
AX_X = mybir.AxisListType.X

P = 128
T = 4
BT = P * T
C = 128
NH = 8
HD = C // NH
NT = NH - 1
NC = 4
DEPTH = 3
E = 8
HID = 512
HC = HID // P
QKV = 3 * C
PROJ = QKV + E
GQ = 2 * T

ANGLES = dict(gamma=(0, 128), eta=(128, 112), theta=(240, 21), turn=(261, 8), twop=(269, 16), p=(285, 16), qw=(301, 4))
NANG = 305
TWO_PI = 2.0 * math.pi
PI_HI = 6.28125
PI_MID = 0.0019350051879882812
PI_LO = TWO_PI - PI_HI - PI_MID
ROUND = 1.5 * 2.0 ** 23
PI_IN = 3.1415925


PATTERN_SETS = [[(0, 0), (0, 1)], [(1, 0), (1, 1)], [(0, 2), (1, 2)], [(2, 0), (2, 1)], [(3, 0), (3, 1)],
                [(2, 2), (3, 2)]]
POOL_UNITS = [("pattern", 1), ("pattern", 4), ("weighted", 1), ("weighted", 4), ("weighted", 6)]
OWN_UNITS = [u for u in [("pattern", m) for m in range(6)] + [("weighted", m) for m in range(2 * T)]
             if u not in POOL_UNITS]


class Blk:

    def __init__(self, pair, slot):
        self.pair, self.slot = pair, slot
        self.value = pair * 2 + slot
        self.number = self.value if type(pair) is int else None

    def plus(self, n):
        return Blk(self.pair + (self.slot + n) // 2, (self.slot + n) % 2)

    def older(self, n):
        return self.number is None or self.number >= n

    def exists(self, nblocks):
        return self.number is None or 0 <= self.number < nblocks


class Signal:

    def __init__(self, sem, per):
        self.sem, self.per = sem, per

    def value(self, k, n=None):
        return k.value * self.per + (self.per if n is None else n)


class SlotSignal:

    def __init__(self, sems):
        self.sems = sems

    def of(self, k):
        return self.sems[k.slot]

    def value(self, k):
        return k.pair * 16 + 16


def bc_mid(ap, n):
    return ap.unsqueeze(1).to_broadcast([ap.shape[0], n, ap.shape[1]])


def bc_last(ap, n):
    return ap.unsqueeze(2).to_broadcast([ap.shape[0], ap.shape[1], n])


def build(nc, query, W_qkv, b_qkv, W_out, b_out, quantum_weights, photonic_phases, entanglement_gates,
          superposition_logits, Wg, W1, b1, W2, b2, out):
    B, S, _ = query.shape
    NB = B * S // BT
    LOOP_FROM, LOOP_TO = 1, NB // 2 - 1

    x_dram = query.rearrange("b s c -> (b s) c")
    out_dram = out.rearrange("b s c -> (b s) c")

    with ExitStack() as ctx:
        def sb(name, shape):
            return ctx.enter_context(nc.sbuf_tensor(name, shape, F32))

        def psum(name, shape):
            return ctx.enter_context(nc.psum_tensor(name, shape, F32))

        def sem(name):
            return ctx.enter_context(nc.semaphore(name))

        def signal(name, per=1):
            return Signal(sem(name), per)

        ident = sb("ident", [P, P])
        ones = sb("ones", [P, P])
        w_proj = sb("w_proj", [P, PROJ])
        b_proj = sb("b_proj", [1, PROJ])
        w_outT = sb("w_outT", [P, C])
        w1 = sb("w1", [P, E, HID])
        w2 = sb("w2", [P, E, HC, C])
        b1_cols = sb("b1_cols", [P, E * HC])
        b_rows = sb("b_rows", [E + 1, C])
        prow = sb("prow", [1, 120])
        par = sb("par", [P, 120])
        half = sb("half", [P, 96])
        psi = sb("psi", [P, NH])
        phi_psi = sb("phi_psi", [P, NT])
        fr1 = sb("fr1", [P, NH])
        fr2 = sb("fr2", [P, NH])
        sin_t = sb("sin_t", [P, NANG])
        cos_t = sb("cos_t", [P, NANG])
        alpha = sb("alpha", [P, DEPTH * NT])
        a_plus = sb("a_plus", [P, DEPTH * NT])
        a_minus = sb("a_minus", [P, DEPTH * NT])
        k1x = sb("k1x", [P, NT * HD])
        k1y = sb("k1y", [P, NT * HD])
        ratio = sb("ratio", [P, 2, NC])
        gain = sb("gain", [P, NC])
        sup = sb("sup", [P, NC])
        sup_tmp = sb("sup_tmp", [P, 8])
        eps_ln = sb("eps_ln", [P, 1])
        eps_amp = sb("eps_amp", [P, 1])
        tiny = sb("tiny", [P, 1])
        rank = sb("rank", [P, E])

        x_sb = sb("x_sb", [P, 2, T, C])
        stats = sb("stats", [P, T, 6])
        moments = sb("moments", [P, 3, T])
        sd = sb("sd", [P, T])
        rstd = sb("rstd", [P, T])
        xn = sb("xn", [P, T, C])
        xnT = sb("xnT", [P, 2, BT])
        qkv = sb("qkv", [P, T, PROJ])
        ss = sb("ss", [P, 2, T * 3 * NH])
        norm = sb("norm", [P, T * 3 * NH])
        rnorm = sb("rnorm", [P, T * 3 * NH])
        a0 = sb("a0", [P, GQ, C])
        vT = sb("vT", [P, 2, T, HD, NH])
        vsum = sb("vsum", [P, T, HD])
        f_tmp = sb("f_tmp", [P, 3, T, HD])
        phase = sb("phase", [P, 2, T, HD])
        r_tmp = sb("r_tmp", [P, 4, T, E])
        r_one = sb("r_one", [P, 8, T])
        cw = sb("cw", [P, 2, T, E + 1])
        cwT = sb("cwT", [E + 1, 2, BT])
        sqx = sb("sqx", [P, GQ, NT * HD])
        sqy = sb("sqy", [P, GQ, NT * HD])
        x1 = sb("x1", [P, GQ, C])
        y1 = sb("y1", [P, GQ, C])
        xy2 = sb("xy2", [P, 2, GQ, C])
        x2, y2 = xy2[:, 0], xy2[:, 1]
        sq = xy2.rearrange("p a g c -> p (a g c)")[:, 0:T * QKV].rearrange("p (t c) -> p t c", t=T)
        m1 = sb("m1", [P, GQ, C])
        m2 = sb("m2", [P, GQ, C])
        zp, zm = m1[:, :, 0:NT * HD], m2[:, :, 0:NT * HD]
        fx = sb("fx", [P, 2, GQ, C])
        fy = sb("fy", [P, 2, GQ, C])
        qsum = sb("qsum", [P, T, C])
        kdif = sb("kdif", [P, T, C])
        prod = sb("prod", [P, 3, 2048])
        ang, kk, rem = (prod[:, 0, n * NANG:(n + 1) * NANG] for n in range(3))
        k_tmp = prod[:, 1, 0:4 * NT * HD].rearrange("p (n e) -> p n e", n=4)
        pat = sb("pat", [P, T, 3, NH * NH])
        pr = sb("pr", [P, 3, T, NH * NH])
        power = pr[:, 0]
        rowmax = sb("rowmax", [P, T * NH])
        below = sb("below", [P, T, NH * NH])
        expo = sb("expo", [P, T, NC, NH * NH])
        zsum = sb("zsum", [P, T * NC * NH])
        rz = sb("rz", [P, T * NC * NH])
        u = sb("u", [P, T, NC, C])
        u_sgn = sb("u_sgn", [P, T, NC, C])
        msum = sb("msum", [P, T, C])
        meas = sb("meas", [P, T, C])
        measT = sb("measT", [P, BT])
        hid = sb("hid", [P, 2, HC, BT])
        wqkv_rows = hid[:, 0, 0, 0:QKV].rearrange("p (r c) -> p r c", r=3)
        wout_rows = hid[:, 0, 0, QKV:QKV + C]
        b1_rows = hid[0:E * HC, 0, 1, 0:P]
        gated = sb("gated", [P, 2, T, C])
        yacc = sb("yacc", [P, 2, T, C])

        ps_h = psum("ps_h", [P, 2, 512])
        ps_y = psum("ps_y", [P, 2, 512])
        ps_proj = psum("ps_proj", [P, 2, 512])
        ps_t = psum("ps_t", [P, 512])
        ps_o = psum("ps_o", [P, 512])

        weights_in = sem("weights_in")
        params_in = sem("params_in")
        small_in = sem("small_in")
        experts_in = sem("experts_in")
        ident_made = sem("ident_made")
        ones_made = sem("ones_made")
        setup_psum = sem("setup_psum")
        setup_copied = sem("setup_copied")
        const_step = sem("const_step")
        angles_reduced = sem("angles_reduced")
        angles_folded = sem("angles_folded")
        logits_shifted = sem("logits_shifted")
        const_act = sem("const_act")
        entangle_consts = sem("entangle_consts")
        consts_ready = sem("consts_ready")
        x_loaded = SlotSignal([sem("x_loaded_0"), sem("x_loaded_1")])
        ln_step = signal("ln_step", T + 7)
        sd_ready = signal("sd_ready")
        xn_ready = signal("xn_ready", T)
        xT_psum = signal("xT_psum")
        xnT_ready = signal("xnT_ready")
        proj_psum = signal("proj_psum", T)
        qkv_ready = signal("qkv_ready", T)
        sq_ready = signal("sq_ready", T)
        ss_step = signal("ss_step", 2)
        norm_ready = signal("norm_ready")
        rnorm_step = signal("rnorm_step", 2)
        a0_ready = signal("a0_ready")
        v_ready = signal("v_ready")
        phase_step = signal("phase_step", 5)
        router_step = signal("router_step", 16)
        phase_ready = signal("phase_ready")
        router_diff = signal("router_diff")
        router_exp = signal("router_exp")
        cw_ready = signal("cw_ready")
        ctrl0_ready = signal("ctrl0_ready")
        depth0 = signal("depth0", 8)
        sq1_ready = signal("sq1_ready", 4)
        grow1 = signal("grow1", 3)
        grown1 = signal("grown1", 2)
        turned = signal("turned", 6)
        sq2_ready = signal("sq2_ready", 4)
        grow2 = signal("grow2", 3)
        grown2 = signal("grown2", 2)
        mixed_ready = signal("mixed_ready", 2)
        own_prod = signal("own_prod", len(OWN_UNITS))
        own_sum = signal("own_sum", len(OWN_UNITS))
        pool_prod = signal("pool_prod", len(POOL_UNITS))
        pool_sum = signal("pool_sum", len(POOL_UNITS))
        power_step = signal("power_step", 6)
        below_step = signal("below_step", 2)
        exp_ready = signal("exp_ready", NC)
        probs_step = signal("probs_step", 3)
        amp_ready = signal("amp_ready")
        hidden_psum = signal("hidden_psum", E * HC)
        hidden_ready = signal("hidden_ready", E * HC)
        expert_psum = signal("expert_psum", E)
        gated_ready = signal("gated_ready", E)
        y_added = signal("y_added", E)
        cwT_psum = signal("cwT_psum")
        cwT_ready = signal("cwT_ready")
        abs_ready = signal("abs_ready", T)
        sgn_ready = signal("sgn_ready", T)
        clip_ready = signal("clip_ready")
        mix_ready = signal("mix_ready", NC)
        msum_step = signal("msum_step", NC - 1)
        meas_ready = signal("meas_ready")
        mT_psum = signal("mT_psum")
        mT_ready = signal("mT_ready")
        o_psum = signal("o_psum")
        out_ready = signal("out_ready")
        stored = SlotSignal([sem("stored_0"), sem("stored_1")])

        block = ctx.enter_context(nc.Block())

        def run_steps(eng, step):
            for n in range(-2, 2 * LOOP_FROM):
                step(Blk(n // 2, n % 2))
            with eng.Fori(LOOP_FROM, LOOP_TO) as pair:
                for slot in range(2):
                    step(Blk(pair, slot))
            for n in range(2 * LOOP_TO, NB + 1):
                step(Blk(n // 2, n % 2))

        def ang_of(table, name):
            at, n = ANGLES[name]
            return table[:, at:at + n]

        def unit_summed(eng, k, unit):
            if unit in POOL_UNITS:
                eng.wait_ge(pool_sum.sem, pool_sum.value(k, POOL_UNITS.index(unit) + 1))
            else:
                eng.wait_ge(own_sum.sem, own_sum.value(k, OWN_UNITS.index(unit) + 1))

        def pattern_summed(eng, k):
            for units in (POOL_UNITS, OWN_UNITS):
                unit_summed(eng, k, [u for u in units if u[0] == "pattern"][-1])

        def pattern_operands(k, m):
            for n, (t, kind) in enumerate(PATTERN_SETS[m]):
                q, kq = ((fx[:, k.slot, 2 * t, :], fx[:, k.slot, 2 * t + 1, :]),
                         (fy[:, k.slot, 2 * t, :], fy[:, k.slot, 2 * t + 1, :]),
                         (qsum[:, t, :], kdif[:, t, :]))[kind]
                yield (n, q.rearrange("p (i d) -> p i d", d=HD).unsqueeze(2).to_broadcast([P, NH, NH, HD]),
                       kq.rearrange("p (j d) -> p j d", d=HD).unsqueeze(1).to_broadcast([P, NH, NH, HD]))

        def weighted_operands(k, m):
            t, c = m // 2, 2 * (m % 2)
            w = expo[:, t, c:c + 2, :].rearrange("p c (i j) -> p (c i) j", j=NH)
            return (w.unsqueeze(2).to_broadcast([P, 2 * NH, HD, NH]),
                    vT[:, k.slot, t].unsqueeze(1).to_broadcast([P, 2 * NH, HD, NH]))

        def set_of(slot, n):
            return prod[:, slot, n * 1024:(n + 1) * 1024].rearrange("p (i j d) -> p i j d", i=NH, j=NH)

        def weighted_slot(slot):
            return prod[:, slot, :].rearrange("p (g d j) -> p g d j", d=HD, j=NH)

        def heads(ap):
            return ap.rearrange("p g (h d) -> p g h d", d=HD)

        @block.sync
        def _(sp):
            def load_x(k):
                if k.older(2):
                    sp.wait_ge(y_added.sem, y_added.value(k.plus(-2), 1))
                src = x_dram[bass.ds(k.value * BT, BT), :].rearrange("(t p) c -> p t c", p=P)
                sp.dma_start(x_sb[:, k.slot], src).then_inc(x_loaded.of(k), 16)

            def store(k):
                sp.wait_ge(out_ready.sem, out_ready.value(k))
                dst = out_dram[bass.ds(k.value * BT, BT), :].rearrange("(t p) c -> p t c", p=P)
                sp.dma_start(dst, yacc[:, k.slot]).then_inc(stored.of(k), 16)

            load_x(Blk(0, 0))
            sp.dma_start(wqkv_rows, W_qkv.rearrange("(r p) c -> p r c", p=P)).then_inc(weights_in, 16)
            sp.dma_start(wout_rows, W_out).then_inc(weights_in, 16)
            sp.dma_start(w_proj[:, QKV:PROJ], Wg).then_inc(weights_in, 16)
            flat = photonic_phases.rearrange("a b -> (a b)")
            diag = flat[0:(HD - 1) * (C + 1) + 1:C + 1]
            sp.dma_start(prow[:, 0:16], diag.unsqueeze(0), allow_slow_non_contiguous=True).then_inc(params_in, 16)
            sp.dma_start(prow[:, 16:112], entanglement_gates.rearrange("a b c -> (a b c)").unsqueeze(0)).then_inc(params_in, 16)
            sp.dma_start(prow[:, 112:116], quantum_weights[:, 0, 0].unsqueeze(0), allow_slow_non_contiguous=True).then_inc(params_in, 16)
            sp.dma_start(prow[:, 116:120], superposition_logits.unsqueeze(0)).then_inc(params_in, 16)
            sp.dma_start(b_proj[:, 0:QKV], b_qkv.unsqueeze(0)).then_inc(small_in, 16)
            sp.dma_start(b1_rows, b1.rearrange("e (c p) -> (e c) p", p=P)).then_inc(small_in, 16)
            sp.dma_start(b_rows[0:E, :], b2).then_inc(small_in, 16)
            sp.dma_start(b_rows[E:E + 1, :], b_out.unsqueeze(0)).then_inc(small_in, 16)
            sp.dma_start(w1[:], W1.rearrange("e c h -> c e h")).then_inc(experts_in, 16)
            sp.dma_start(w2[:], W2.rearrange("e (c p) n -> p e c n", p=P)).then_inc(experts_in, 16)

            def step(k):
                if k.plus(-2).exists(NB):
                    store(k.plus(-2))
                if k.plus(2).exists(NB) and not (k.number is not None and k.number < -1):
                    load_x(k.plus(2))

            run_steps(sp, step)
            store(Blk((NB - 1) // 2, (NB - 1) % 2))
            for last in (NB - 2, NB - 1):
                sp.wait_ge(stored.of(Blk(last // 2, last % 2)), stored.value(Blk(last // 2, last % 2)))

        @block.tensor
        def _(pe):
            pe.wait_ge(ident_made, 2)
            pe.wait_ge(weights_in, 48)
            for r in range(3):
                last = nc.tensor.transpose(ps_h[:, 0, r * P:(r + 1) * P], wqkv_rows[:, r, :], ident[:])
            last = nc.tensor.transpose(ps_h[:, 0, 3 * P:4 * P], wout_rows, ident[:])
            last.then_inc(setup_psum, 1)
            pe.wait_ge(params_in, 64)
            pe.wait_ge(ones_made, 1)
            nc.tensor.matmul(ps_y[:, 0, 0:120], ones[0:1, :], prow[:], start=True, stop=True).then_inc(setup_psum, 1)
            pe.wait_ge(small_in, 64)
            nc.tensor.transpose(ps_y[:, 1, 0:E * HC], b1_rows, ident[0:E * HC, 0:E * HC]).then_inc(setup_psum, 1)

            def experts(k, e):
                if e == 0:
                    pe.wait_ge(xnT_ready.sem, xnT_ready.value(k))
                    if k.number == 0:
                        pe.wait_ge(experts_in, 32)
                        pe.wait_ge(setup_copied, 3)
                for c in range(HC):
                    n = e * HC + c
                    if n >= 2:
                        pe.wait_ge(hidden_ready.sem, hidden_ready.value(k, n - 1))
                    elif k.older(1):
                        pe.wait_ge(hidden_ready.sem, hidden_ready.value(k.plus(-1), E * HC + n - 1))
                    nc.tensor.matmul(ps_h[:, n % 2, :], w1[:, e, c * P:(c + 1) * P], xnT[:, k.slot, :],
                                     start=True, stop=True).then_inc(hidden_psum.sem, 1)
                    if e > 0:
                        expert_out(k, e - 1, c)

            def expert_out(k, e, t):
                if t == 0:
                    if e >= 2:
                        pe.wait_ge(gated_ready.sem, gated_ready.value(k, e - 1))
                    elif k.older(1):
                        pe.wait_ge(gated_ready.sem, gated_ready.value(k.plus(-1), E + e - 1))
                    elif e == 0:
                        pe.wait_ge(setup_copied, 4)
                    pe.wait_ge(hidden_ready.sem, hidden_ready.value(k, (e + 1) * HC))
                for c in range(HC):
                    last = nc.tensor.matmul(ps_y[:, e % 2, t * P:(t + 1) * P], hid[:, e % 2, c, t * P:(t + 1) * P],
                                            w2[:, e, c, :], start=(c == 0), stop=(c == HC - 1))
                if t == T - 1:
                    last.then_inc(expert_psum.sem, 1)

            def last_expert_out(k):
                for t in range(T):
                    expert_out(k, E - 1, t)

            def turn_x(k):
                pe.wait_ge(xn_ready.sem, xn_ready.value(k))
                if k.older(2):
                    pe.wait_ge(cwT_ready.sem, cwT_ready.value(k.plus(-2)))
                elif k.older(1):
                    pe.wait_ge(xnT_ready.sem, xnT_ready.value(k.plus(-1)))
                for t in range(T):
                    last = nc.tensor.transpose(ps_t[:, t * P:(t + 1) * P], xn[:, t, :], ident[:])
                last.then_inc(xT_psum.sem, 1)

            def project(k):
                pe.wait_ge(xnT_ready.sem, xnT_ready.value(k))
                if k.number == 0:
                    pe.wait_ge(setup_copied, 3)
                    pe.wait_ge(small_in, 64)
                for t in range(T):
                    if t >= 2:
                        pe.wait_ge(sq_ready.sem, sq_ready.value(k, t - 1))
                    elif k.older(1):
                        pe.wait_ge(sq_ready.sem, sq_ready.value(k.plus(-1), T + t - 1))
                    nc.tensor.matmul(ps_proj[:, t % 2, 0:PROJ], xnT[:, k.slot, t * P:(t + 1) * P], w_proj[:],
                                     start=True, stop=False)
                    nc.tensor.matmul(ps_proj[:, t % 2, 0:PROJ], ones[0:1, :], b_proj[:],
                                     start=False, stop=True).then_inc(proj_psum.sem, 1)

            def turn_cw(k):
                pe.wait_ge(cw_ready.sem, cw_ready.value(k))
                if k.older(1):
                    pe.wait_ge(mT_ready.sem, mT_ready.value(k.plus(-1)))
                else:
                    pe.wait_ge(xnT_ready.sem, xnT_ready.value(k.plus(1)))
                for t in range(T):
                    last = nc.tensor.transpose(ps_t[0:E + 1, t * P:(t + 1) * P], cw[:, k.slot, t, :], ident[:])
                last.then_inc(cwT_psum.sem, 1)

            def turn_m(k):
                pe.wait_ge(meas_ready.sem, meas_ready.value(k))
                if k.plus(2).exists(NB):
                    pe.wait_ge(xnT_ready.sem, xnT_ready.value(k.plus(2)))
                else:
                    pe.wait_ge(cwT_ready.sem, cwT_ready.value(k))
                for t in range(T):
                    last = nc.tensor.transpose(ps_t[:, t * P:(t + 1) * P], meas[:, t, :], ident[:])
                last.then_inc(mT_psum.sem, 1)

            def project_out(k):
                pe.wait_ge(mT_ready.sem, mT_ready.value(k))
                pe.wait_ge(cwT_ready.sem, cwT_ready.value(k))
                if k.older(1):
                    pe.wait_ge(out_ready.sem, out_ready.value(k.plus(-1)))
                for t in range(T):
                    cols = slice(t * P, (t + 1) * P)
                    nc.tensor.matmul(ps_o[:, cols], measT[:, cols], w_outT[:], start=True, stop=False)
                    last = nc.tensor.matmul(ps_o[:, cols], cwT[:, k.slot, cols], b_rows[:], start=False, stop=True)
                last.then_inc(o_psum.sem, 1)

            def step(k):
                o, n, far = k.plus(-1), k.plus(1), k.plus(2)
                if n.exists(NB):
                    project(n)
                if k.exists(NB):
                    experts(k, 0)
                    experts(k, 1)
                    experts(k, 2)
                if o.exists(NB):
                    turn_m(o)
                if k.exists(NB):
                    experts(k, 3)
                if o.exists(NB):
                    project_out(o)
                if k.exists(NB):
                    experts(k, 4)
                    turn_cw(k)
                    experts(k, 5)
                    experts(k, 6)
                    experts(k, 7)
                    last_expert_out(k)
                if far.exists(NB):
                    turn_x(far)

            run_steps(pe, step)

        @block.scalar
        def _(act):
            act.wait_ge(setup_psum, 1)
            act.activation(w_proj[:, 0:QKV], ps_h[:, 0, 0:QKV], ACT.Copy).then_inc(setup_copied, 1)
            act.activation(w_outT[:], ps_h[:, 0, QKV:QKV + C], ACT.Copy).then_inc(setup_copied, 1)
            act.wait_ge(setup_psum, 2)
            act.activation(par[:], ps_y[:, 0, 0:120], ACT.Copy).then_inc(setup_copied, 1)
            act.wait_ge(setup_psum, 3)
            act.activation(b1_cols[:], ps_y[:, 1, 0:E * HC], ACT.Copy).then_inc(setup_copied, 1)
            act.wait_ge(angles_reduced, 1)
            act.activation(sin_t[:], rem, ACT.Sin).then_inc(const_act, 1)
            act.activation(kk, rem, ACT.Abs).then_inc(const_act, 1)
            act.wait_ge(angles_folded, 1)
            act.activation(cos_t[:], kk, ACT.Sin).then_inc(const_act, 1)
            act.wait_ge(logits_shifted, 1)
            act.activation(sup_tmp[:, 4:8], sup_tmp[:, 0:4], ACT.Exp).then_inc(const_act, 1)

            def ln_sd(k):
                act.wait_ge(ln_step.sem, ln_step.value(k, T + 6))
                if k.older(1):
                    act.wait_ge(ln_step.sem, ln_step.value(k.plus(-1)))
                if k.number == 0:
                    act.wait_ge(consts_ready, 1)
                act.activation(sd[:], moments[:, 2], ACT.Sqrt, bias=eps_ln[:, 0:1], scale=1.0 / C).then_inc(sd_ready.sem, 1)

            def copy_xT(k):
                act.wait_ge(xT_psum.sem, xT_psum.value(k))
                if k.older(2):
                    o = k.plus(-2)
                    act.wait_ge(hidden_psum.sem, hidden_psum.value(o))
                act.activation(xnT[:, k.slot, :], ps_t[:], ACT.Copy).then_inc(xnT_ready.sem, 1)

            def copy_proj(k):
                if k.older(1):
                    o = k.plus(-1)
                    act.wait_ge(v_ready.sem, v_ready.value(o))
                    act.wait_ge(a0_ready.sem, a0_ready.value(o))
                    act.wait_ge(router_step.sem, router_step.value(o, 6))
                    act.wait_ge(ss_step.sem, ss_step.value(o, 1))
                    act.wait_ge(turned.sem, turned.value(o))
                for t in range(T):
                    act.wait_ge(proj_psum.sem, proj_psum.value(k, t + 1))
                    act.activation(qkv[:, t, :], ps_proj[:, t % 2, 0:PROJ], ACT.Copy).then_inc(qkv_ready.sem, 1)
                    act.activation(sq[:, t, :], ps_proj[:, t % 2, 0:QKV], ACT.Square).then_inc(sq_ready.sem, 1)

            def norm_sqrt(k):
                act.wait_ge(ss_step.sem, ss_step.value(k))
                if k.older(1):
                    act.wait_ge(rnorm_step.sem, rnorm_step.value(k.plus(-1), 1))
                act.activation(norm[:], ss[:, 1, :], ACT.Sqrt).then_inc(norm_ready.sem, 1)

            def control0(k):
                act.wait_ge(a0_ready.sem, a0_ready.value(k))
                if k.older(1):
                    act.wait_ge(grow2.sem, grow2.value(k.plus(-1)))
                act.activation(sqx[:], a0[:, :, 0:NT * HD], ACT.Square).then_inc(ctrl0_ready.sem, 1)

            def control1(k):
                act.wait_ge(depth0.sem, depth0.value(k))
                act.activation(sqx[:], x1[:, :, 0:NT * HD], ACT.Square).then_inc(sq1_ready.sem, 1)
                act.activation(sqy[:], y1[:, :, 0:NT * HD], ACT.Square).then_inc(sq1_ready.sem, 1)
                act.activation(x2[:, :, NT * HD:C], x1[:, :, NT * HD:C], ACT.Copy).then_inc(sq1_ready.sem, 1)
                act.activation(y2[:, :, NT * HD:C], y1[:, :, NT * HD:C], ACT.Copy).then_inc(sq1_ready.sem, 1)

            def control2(k):
                act.wait_ge(turned.sem, turned.value(k))
                if k.older(2):
                    pattern_summed(act, k.plus(-2))
                act.activation(sqx[:], x1[:, :, 0:NT * HD], ACT.Square).then_inc(sq2_ready.sem, 1)
                act.activation(sqy[:], y1[:, :, 0:NT * HD], ACT.Square).then_inc(sq2_ready.sem, 1)
                act.activation(fx[:, k.slot, :, NT * HD:C], x1[:, :, NT * HD:C], ACT.Copy).then_inc(sq2_ready.sem, 1)
                act.activation(fy[:, k.slot, :, NT * HD:C], y1[:, :, NT * HD:C], ACT.Copy).then_inc(sq2_ready.sem, 1)

            def router_softmax(k):
                act.wait_ge(router_diff.sem, router_diff.value(k))
                if k.older(1):
                    act.wait_ge(cw_ready.sem, cw_ready.value(k.plus(-1)))
                act.activation(r_one[:, 3, :], r_one[:, 2, :], ACT.Exp).then_inc(router_exp.sem, 1)

            def score_exp(k):
                act.wait_ge(below_step.sem, below_step.value(k))
                if k.older(1):
                    act.wait_ge(own_prod.sem, own_prod.value(k.plus(-1)))
                    act.wait_ge(pool_prod.sem, pool_prod.value(k.plus(-1)))
                for c in range(NC):
                    act.activation(expo[:, :, c, :], below[:], ACT.Exp,
                                   scale=gain[:, c:c + 1]).then_inc(exp_ready.sem, 1)

            def amplitude(k):
                act.wait_ge(probs_step.sem, probs_step.value(k))
                act.activation(expo[:], expo[:], ACT.Sqrt, bias=eps_amp[:, 0:1]).then_inc(amp_ready.sem, 1)

            def abs_sign(k, t):
                unit_summed(act, k, ("weighted", 2 * t))
                unit_summed(act, k, ("weighted", 2 * t + 1))
                if k.older(1):
                    act.wait_ge(msum_step.sem, msum_step.value(k.plus(-1)))
                act.activation(u_sgn[:, t], u[:, t], ACT.Sign, bias=tiny[:, 0:1]).then_inc(sgn_ready.sem, 1)
                act.wait_ge(sgn_ready.sem, sgn_ready.value(k, t + 1))
                act.activation(u[:, t], u[:, t], ACT.Abs).then_inc(abs_ready.sem, 1)

            def gelu(k, e):
                for c in range(HC):
                    n = e * HC + c
                    act.wait_ge(hidden_psum.sem, hidden_psum.value(k, n + 1))
                    if c == 0:
                        if e >= 2:
                            act.wait_ge(expert_psum.sem, expert_psum.value(k, e - 1))
                        elif k.older(1):
                            act.wait_ge(expert_psum.sem, expert_psum.value(k.plus(-1), E + e - 1))
                    act.activation(hid[:, e % 2, c, :], ps_h[:, n % 2, :], ACT.Gelu,
                                   bias=b1_cols[:, n:n + 1]).then_inc(hidden_ready.sem, 1)

            def gate(k, e):
                act.wait_ge(expert_psum.sem, expert_psum.value(k, e + 1))
                if e == 0:
                    act.wait_ge(cw_ready.sem, cw_ready.value(k))
                if e >= 2:
                    act.wait_ge(y_added.sem, y_added.value(k, e - 1))
                elif k.older(1):
                    act.wait_ge(y_added.sem, y_added.value(k.plus(-1), E + e - 1))
                for t in range(T):
                    last = act.activation(gated[:, e % 2, t, :], ps_y[:, e % 2, t * P:(t + 1) * P], ACT.Copy,
                                          scale=cw[:, k.slot, t, e:e + 1])
                last.then_inc(gated_ready.sem, 1)

            def copy_cwT(k):
                act.wait_ge(cwT_psum.sem, cwT_psum.value(k))
                if k.older(2):
                    act.wait_ge(o_psum.sem, o_psum.value(k.plus(-2)))
                act.activation(cwT[:, k.slot, :], ps_t[0:E + 1, :], ACT.Copy).then_inc(cwT_ready.sem, 1)

            def copy_mT(k):
                act.wait_ge(mT_psum.sem, mT_psum.value(k))
                if k.older(1):
                    act.wait_ge(o_psum.sem, o_psum.value(k.plus(-1)))
                act.activation(measT[:], ps_t[:], ACT.Copy).then_inc(mT_ready.sem, 1)

            def step(k):
                o, n, far = k.plus(-1), k.plus(1), k.plus(2)
                if n.exists(NB):
                    copy_proj(n)
                if o.exists(NB):
                    abs_sign(o, 2)
                if k.exists(NB):
                    gelu(k, 0)
                if o.exists(NB):
                    abs_sign(o, 3)
                if n.exists(NB):
                    norm_sqrt(n)
                if k.exists(NB):
                    gelu(k, 1)
                    gate(k, 0)
                if n.exists(NB):
                    control0(n)
                if k.exists(NB):
                    gelu(k, 2)
                if o.exists(NB):
                    copy_mT(o)
                if k.exists(NB):
                    gelu(k, 3)
                    gate(k, 1)
                if n.exists(NB):
                    control1(n)
                if k.exists(NB):
                    gelu(k, 4)
                    gate(k, 2)
                if n.exists(NB):
                    router_softmax(n)
                if k.exists(NB):
                    score_exp(k)
                if far.exists(NB):
                    ln_sd(far)
                if k.exists(NB):
                    gate(k, 3)
                    amplitude(k)
                    gelu(k, 5)
                if n.exists(NB):
                    control2(n)
                if k.exists(NB):
                    gelu(k, 6)
                    gate(k, 4)
                    abs_sign(k, 0)
                    gelu(k, 7)
                    gate(k, 5)
                    abs_sign(k, 1)
                    copy_cwT(k)
                    gate(k, 6)
                    gate(k, 7)
                if far.exists(NB):
                    copy_xT(far)

            run_steps(act, step)

        @block.gpsimd
        def _(pool):
            pool.memset(ident[:], 0.0).then_inc(ident_made, 1)
            pool.memset(ones[:], 1.0).then_inc(ones_made, 1)
            pool.wait_ge(ident_made, 1)
            pool.affine_select(out=ident[:], in_=ident[:], compare_op=ALU.not_equal, fill=1.0, base=0,
                               pattern=[[-1, P]], channel_multiplier=1).then_inc(ident_made, 1)

            def tt(out_, a, b, op, sig):
                pool.tensor_tensor(out_, a, b, op).then_inc(sig.sem, 1)

            def const_hd(ap):
                return bc_mid(ap, GQ)

            def const_h(ap):
                n = ap.shape[1]
                return ap.unsqueeze(1).unsqueeze(3).to_broadcast([P, GQ, n, HD])

            low, high = slice(0, NT * HD), slice(HD, C)

            def entangle0(k):
                if k.number == 0:
                    pool.wait_ge(entangle_consts, 1)
                pool.wait_ge(ctrl0_ready.sem, ctrl0_ready.value(k))
                if k.older(1):
                    pool.wait_ge(grown2.sem, grown2.value(k.plus(-1)))
                tt(zp, sqx[:], const_hd(k1x[:]), ALU.mult, depth0)
                tt(zm, sqx[:], const_hd(k1y[:]), ALU.mult, depth0)
                gx, gy = ang_of(cos_t, "gamma"), ang_of(sin_t, "gamma")
                tt(x1[:, :, NT * HD:C], a0[:, :, NT * HD:C], const_hd(gx[:, NT * HD:C]), ALU.mult, depth0)
                tt(y1[:, :, NT * HD:C], a0[:, :, NT * HD:C], const_hd(gy[:, NT * HD:C]), ALU.mult, depth0)
                pool.wait_ge(depth0.sem, depth0.value(k, 4))
                tt(zp, zp, const_hd(gx[:, low]), ALU.add, depth0)
                tt(zm, zm, const_hd(gy[:, low]), ALU.add, depth0)
                pool.wait_ge(depth0.sem, depth0.value(k, 6))
                tt(x1[:, :, low], zp, a0[:, :, high], ALU.mult, depth0)
                tt(y1[:, :, low], zm, a0[:, :, high], ALU.mult, depth0)

            def grow(k, sig, depth):
                tt(sqx[:], sqx[:], sqy[:], ALU.add, sig)
                pool.wait_ge(sig.sem, sig.value(k, 1))
                ap, am = a_plus[:, depth * NT:(depth + 1) * NT], a_minus[:, depth * NT:(depth + 1) * NT]
                tt(heads(zp), heads(sqx[:]), const_h(ap), ALU.mult, sig)
                tt(heads(zm), heads(sqx[:]), const_h(am), ALU.mult, sig)

            def entangle1(k):
                pool.wait_ge(depth0.sem, depth0.value(k))
                pool.wait_ge(sq1_ready.sem, sq1_ready.value(k))
                grow(k, grow1, 1)

            def turn(k):
                pool.wait_ge(grown1.sem, grown1.value(k))
                ct, st = const_h(ang_of(cos_t, "turn")), const_h(ang_of(sin_t, "turn"))
                tt(heads(m1[:]), heads(x2), ct, ALU.mult, turned)
                tt(heads(m2[:]), heads(y2), st, ALU.mult, turned)
                pool.wait_ge(turned.sem, turned.value(k, 2))
                tt(x1[:], m1[:], m2[:], ALU.subtract, turned)
                pool.wait_ge(turned.sem, turned.value(k, 3))
                tt(heads(m1[:]), heads(x2), st, ALU.mult, turned)
                tt(heads(m2[:]), heads(y2), ct, ALU.mult, turned)
                pool.wait_ge(turned.sem, turned.value(k, 5))
                tt(y1[:], m1[:], m2[:], ALU.add, turned)

            def entangle2(k):
                pool.wait_ge(turned.sem, turned.value(k))
                pool.wait_ge(sq2_ready.sem, sq2_ready.value(k))
                grow(k, grow2, 2)

            def products(k, unit):
                n = POOL_UNITS.index(unit)
                if n > 0:
                    pool.wait_ge(pool_sum.sem, pool_sum.value(k, n))
                elif k.older(1):
                    pool.wait_ge(pool_sum.sem, pool_sum.value(k.plus(-1)))
                if unit[0] == "pattern":
                    if n == 0:
                        pool.wait_ge(grown2.sem, grown2.value(k))
                        pool.wait_ge(sq2_ready.sem, sq2_ready.value(k))
                    for part, q, kq in pattern_operands(k, unit[1]):
                        last = pool.tensor_tensor(set_of(2, part), q, kq, ALU.mult)
                else:
                    pool.wait_ge(amp_ready.sem, amp_ready.value(k))
                    w, v = weighted_operands(k, unit[1])
                    last = pool.tensor_tensor(weighted_slot(2), w, v, ALU.mult)
                last.then_inc(pool_prod.sem, 1)

            def add_expert(k, e):
                pool.wait_ge(gated_ready.sem, gated_ready.value(k, e + 1))
                if e == 0 and k.older(2):
                    pool.wait_ge(stored.of(k), stored.value(k.plus(-2)))
                if e > 0:
                    pool.wait_ge(y_added.sem, y_added.value(k, e))
                base = x_sb[:, k.slot] if e == 0 else yacc[:, k.slot]
                tt(yacc[:, k.slot], gated[:, e % 2], base, ALU.add, y_added)

            def sum_circuits(k):
                if k.older(1):
                    pool.wait_ge(meas_ready.sem, meas_ready.value(k.plus(-1)))
                for c in range(1, NC):
                    pool.wait_ge(mix_ready.sem, mix_ready.value(k, c + 1))
                    if c > 1:
                        pool.wait_ge(msum_step.sem, msum_step.value(k, c - 1))
                    tt(msum[:], u_sgn[:, :, 0, :] if c == 1 else msum[:], u_sgn[:, :, c, :], ALU.add, msum_step)

            def step(k):
                o, n = k.plus(-1), k.plus(1)
                if k.exists(NB):
                    products(k, ("pattern", 1))
                if o.exists(NB):
                    sum_circuits(o)
                if k.exists(NB):
                    products(k, ("pattern", 4))
                if n.exists(NB):
                    entangle0(n)
                if k.exists(NB):
                    add_expert(k, 0)
                if n.exists(NB):
                    entangle1(n)
                if k.exists(NB):
                    add_expert(k, 1)
                    add_expert(k, 2)
                if n.exists(NB):
                    turn(n)
                if k.exists(NB):
                    products(k, ("weighted", 1))
                    add_expert(k, 3)
                if n.exists(NB):
                    entangle2(n)
                if k.exists(NB):
                    products(k, ("weighted", 4))
                    add_expert(k, 4)
                    add_expert(k, 5)
                    products(k, ("weighted", 6))
                    add_expert(k, 6)
                    add_expert(k, 7)

            run_steps(pool, step)

        @block.vector
        def _(dve):
            steps = [0]

            def const(ins, named=None):
                if named is None:
                    steps[0] += 1
                    ins.then_inc(const_step, 1)
                    dve.wait_ge(const_step, steps[0])
                else:
                    ins.then_inc(named, 1)
                    dve.wait_ge(named, 1)

            const(dve.memset(eps_ln[:], 1e-5))
            const(dve.memset(eps_amp[:], 1e-12))
            const(dve.memset(tiny[:], 1e-30))
            for j in range(E):
                const(dve.memset(rank[:, j:j + 1], float(E - j)))
            for slot in range(2):
                const(dve.memset(cw[:, slot, :, E:E + 1], 1.0))
            const(dve.memset(b_proj[:, QKV:PROJ], 0.0), consts_ready)

            dve.wait_ge(setup_copied, 3)
            phases = par[:, 0:HD]
            gates = par[:, 16:112].rearrange("p (a h c) -> p a h c", a=DEPTH, h=NH)
            halves = half[:].rearrange("p (a h c) -> p a h c", a=DEPTH, h=NH)
            const(dve.tensor_scalar(half[:], par[:, 16:112], 0.5, None, ALU.mult))
            const(dve.tensor_copy(psi[:, 1:NH], halves[:, 1, 0:NT, 1]))
            const(dve.tensor_copy(psi[:, 0:1], halves[:, 0, 0:1, 1]))
            const(dve.tensor_tensor(phi_psi[:], gates[:, 0, 0:NT, 1], psi[:, 0:NT], ALU.subtract))
            const(dve.tensor_tensor(ang_of(ang, "gamma").rearrange("p (h d) -> p h d", d=HD), bc_mid(phases, NH),
                                    bc_last(psi[:], HD), ALU.subtract))
            const(dve.tensor_tensor(ang_of(ang, "eta").rearrange("p (h d) -> p h d", d=HD), bc_last(phi_psi[:], HD),
                                    bc_mid(phases, NT), ALU.subtract))
            const(dve.tensor_copy(ang_of(ang, "theta").rearrange("p (a h) -> p a h", a=DEPTH), halves[:, :, 0:NT, 0]))
            const(dve.tensor_copy(fr1[:, 0:NT], halves[:, 1, 0:NT, 1]))
            const(dve.tensor_copy(fr1[:, NT:NH], halves[:, 1, NT - 1:NT, 1]))
            const(dve.tensor_copy(fr2[:, 1:NH], halves[:, 2, 0:NT, 1]))
            const(dve.tensor_copy(fr2[:, 0:1], halves[:, 1, 0:1, 1]))
            const(dve.tensor_tensor(ang_of(ang, "turn"), fr1[:], fr2[:], ALU.subtract))
            const(dve.tensor_scalar(ang_of(ang, "twop"), phases, 2.0, None, ALU.mult))
            const(dve.tensor_copy(ang_of(ang, "p"), phases))
            const(dve.tensor_copy(ang_of(ang, "qw"), par[:, 112:116]))
            const(dve.tensor_scalar(kk, ang, 1.0 / TWO_PI, ROUND, ALU.mult, ALU.add))
            const(dve.tensor_scalar(kk, kk, ROUND, None, ALU.subtract))
            const(dve.scalar_tensor_tensor(rem, kk, -PI_HI, ang, ALU.mult, ALU.add))
            const(dve.scalar_tensor_tensor(rem, kk, -PI_MID, rem, ALU.mult, ALU.add))
            const(dve.scalar_tensor_tensor(rem, kk, -PI_LO, rem, ALU.mult, ALU.add))
            const(dve.tensor_scalar(rem, rem, PI_IN, -PI_IN, ALU.min, ALU.max), angles_reduced)
            dve.wait_ge(const_act, 2)
            const(dve.tensor_scalar(kk, kk, -1.0, math.pi / 2, ALU.mult, ALU.add), angles_folded)
            const(dve.tensor_reduce(ratio[:, 0, 0:1], par[:, 116:120], AX_X, ALU.max))
            const(dve.tensor_scalar(sup_tmp[:, 0:4], par[:, 116:120], ratio[:, 0, 0:1], None, ALU.subtract),
                  logits_shifted)
            dve.wait_ge(const_act, 4)
            const(dve.tensor_reduce(ratio[:, 0, 0:1], sup_tmp[:, 4:8], AX_X, ALU.add))
            const(dve.reciprocal(ratio[:, 0, 1:2], ratio[:, 0, 0:1]))
            const(dve.tensor_scalar(sup[:], sup_tmp[:, 4:8], ratio[:, 0, 1:2], None, ALU.mult))
            const(dve.tensor_scalar(ratio[:, 0, :], ang_of(sin_t, "qw"), 0.3, 0.5, ALU.mult, ALU.add))
            const(dve.tensor_scalar(ratio[:, 1, :], ratio[:, 0, :], -1.0, 1.0, ALU.mult, ALU.add))
            const(dve.scalar_tensor_tensor(gain[:], ratio[:, 0, :], HD ** -0.5, ratio[:, 1, :], ALU.mult, ALU.mult))
            const(dve.tensor_scalar(alpha[:], ang_of(cos_t, "theta"), 1.0, None, ALU.subtract))
            const(dve.tensor_tensor(a_plus[:], alpha[:], ang_of(sin_t, "theta"), ALU.add))
            const(dve.tensor_tensor(a_minus[:], alpha[:], ang_of(sin_t, "theta"), ALU.subtract))
            for n, (table, name, factor) in enumerate(((cos_t, "gamma", alpha[:, 0:NT]),
                                                       (cos_t, "eta", ang_of(sin_t, "theta")[:, 0:NT]),
                                                       (sin_t, "gamma", alpha[:, 0:NT]),
                                                       (sin_t, "eta", ang_of(sin_t, "theta")[:, 0:NT]))):
                const(dve.tensor_tensor(k_tmp[:, n].rearrange("p (h d) -> p h d", d=HD),
                                        ang_of(table, name)[:, 0:NT * HD].rearrange("p (h d) -> p h d", d=HD),
                                        bc_last(factor, HD), ALU.mult))
            const(dve.tensor_tensor(k1x[:], k_tmp[:, 0], k_tmp[:, 1], ALU.add))
            const(dve.tensor_tensor(k1y[:], k_tmp[:, 2], k_tmp[:, 3], ALU.add), entangle_consts)

            def tt(out_, a, b, op, sig):
                dve.tensor_tensor(out_, a, b, op).then_inc(sig.sem, 1)

            def layer_norm_stats(k):
                dve.wait_ge(x_loaded.of(k), x_loaded.value(k))
                for t in range(T):
                    dve.bn_stats(stats[:, t, :], x_sb[:, k.slot, t, :]).then_inc(ln_step.sem, 1)
                dve.wait_ge(ln_step.sem, ln_step.value(k, T))
                tt(moments[:, 0], stats[:, :, 1], stats[:, :, 4], ALU.add, ln_step)
                tt(moments[:, 1], stats[:, :, 1], stats[:, :, 4], ALU.subtract, ln_step)
                tt(moments[:, 2], stats[:, :, 2], stats[:, :, 5], ALU.add, ln_step)
                dve.wait_ge(ln_step.sem, ln_step.value(k, T + 3))
                dve.scalar_tensor_tensor(moments[:, 1], moments[:, 1], C / 4.0, moments[:, 1],
                                         ALU.mult, ALU.mult).then_inc(ln_step.sem, 1)
                dve.tensor_scalar(moments[:, 0], moments[:, 0], 0.5, None, ALU.mult).then_inc(ln_step.sem, 1)
                dve.wait_ge(ln_step.sem, ln_step.value(k, T + 4))
                tt(moments[:, 2], moments[:, 1], moments[:, 2], ALU.add, ln_step)

            def layer_norm(k):
                dve.wait_ge(sd_ready.sem, sd_ready.value(k))
                dve.reciprocal(rstd[:], sd[:]).then_inc(ln_step.sem, 1)
                dve.wait_ge(ln_step.sem, ln_step.value(k))
                if k.older(1):
                    dve.wait_ge(xT_psum.sem, xT_psum.value(k.plus(-1)))
                for t in range(T):
                    dve.tensor_scalar(xn[:, t, :], x_sb[:, k.slot, t, :], moments[:, 0, t:t + 1], rstd[:, t:t + 1],
                                      ALU.subtract, ALU.mult).then_inc(xn_ready.sem, 1)

            def norm_squares(k):
                dve.wait_ge(sq_ready.sem, sq_ready.value(k))
                dve.tensor_reduce(ss[:, 0, :], sq.rearrange("p t (g d) -> p (t g) d", d=HD), AX_X,
                                  ALU.add).then_inc(ss_step.sem, 1)
                dve.wait_ge(ss_step.sem, ss_step.value(k, 1))
                dve.tensor_scalar(ss[:, 1, :], ss[:, 0, :], 1e-24, None, ALU.max).then_inc(ss_step.sem, 1)

            def normalise(k):
                dve.wait_ge(norm_ready.sem, norm_ready.value(k))
                dve.tensor_scalar(rnorm[:], norm[:], 1e-12, None, ALU.max).then_inc(rnorm_step.sem, 1)
                dve.wait_ge(rnorm_step.sem, rnorm_step.value(k, 1))
                dve.reciprocal(rnorm[:], rnorm[:]).then_inc(rnorm_step.sem, 1)
                dve.wait_ge(rnorm_step.sem, rnorm_step.value(k))
                if k.older(1):
                    dve.wait_ge(depth0.sem, depth0.value(k.plus(-1)))
                if k.older(2):
                    dve.wait_ge(pool_prod.sem, pool_prod.value(k.plus(-2)))
                rn = rnorm[:].rearrange("p (t g) -> p t g", t=T)
                tt(a0[:].rearrange("p (t q) (h d) -> p t (q h) d", t=T, d=HD),
                   qkv[:, :, 0:2 * C].rearrange("p t (g d) -> p t g d", d=HD),
                   rn[:, :, 0:2 * NH].unsqueeze(3).to_broadcast([P, T, 2 * NH, HD]), ALU.mult, a0_ready)
                tt(vT[:, k.slot].rearrange("p t d j -> p t j d"),
                   qkv[:, :, 2 * C:QKV].rearrange("p t (g d) -> p t g d", d=HD),
                   rn[:, :, 2 * NH:3 * NH].unsqueeze(3).to_broadcast([P, T, NH, HD]), ALU.mult, v_ready)

            def value_phase(k):
                dve.wait_ge(v_ready.sem, v_ready.value(k))
                dve.tensor_reduce(vsum[:], vT[:, k.slot], AX_X, ALU.add).then_inc(phase_step.sem, 1)
                dve.wait_ge(phase_step.sem, phase_step.value(k, 1))
                dve.tensor_scalar(f_tmp[:, 0], vsum[:], 0.0, None, ALU.is_gt).then_inc(phase_step.sem, 1)
                dve.scalar_tensor_tensor(f_tmp[:, 2], vsum[:], 0.0, bc_mid(ang_of(cos_t, "p"), T),
                                         ALU.is_equal, ALU.mult).then_inc(phase_step.sem, 1)
                dve.wait_ge(phase_step.sem, phase_step.value(k, 2))
                dve.scalar_tensor_tensor(f_tmp[:, 1], vsum[:], 0.0, f_tmp[:, 0],
                                         ALU.is_lt, ALU.subtract).then_inc(phase_step.sem, 1)
                dve.wait_ge(phase_step.sem, phase_step.value(k, 4))
                tt(f_tmp[:, 1], f_tmp[:, 1], bc_mid(ang_of(cos_t, "twop"), T), ALU.mult, phase_step)
                dve.wait_ge(phase_step.sem, phase_step.value(k))
                tt(phase[:, k.slot], f_tmp[:, 2], f_tmp[:, 1], ALU.subtract, phase_ready)

            def route(k):
                done = [0]

                def link(ins):
                    done[0] += 1
                    ins.then_inc(router_step.sem, 1)
                    dve.wait_ge(router_step.sem, router_step.value(k, done[0]))

                def wide(ap):
                    return bc_last(ap, E)

                dve.wait_ge(qkv_ready.sem, qkv_ready.value(k))
                s = qkv[:, :, QKV:PROJ]
                order = bc_mid(rank[:], T)
                best, second, first_at, second_at = (r_one[:, n, :] for n in (0, 4, 1, 5))
                is_first, is_second, rest, tmp = (r_tmp[:, n] for n in range(4))
                link(dve.tensor_reduce(best, s, AX_X, ALU.max))
                link(dve.tensor_tensor(tmp, s, wide(best), ALU.is_equal))
                link(dve.tensor_tensor(tmp, tmp, order, ALU.mult))
                link(dve.tensor_reduce(first_at, tmp, AX_X, ALU.max))
                link(dve.tensor_tensor(is_first, tmp, wide(first_at), ALU.is_equal))
                link(dve.scalar_tensor_tensor(rest, is_first, -3e38, s, ALU.mult, ALU.add))
                link(dve.tensor_reduce(second, rest, AX_X, ALU.max))
                dve.tensor_tensor(r_one[:, 2, :], second, best, ALU.subtract).then_inc(router_diff.sem, 1)
                link(dve.tensor_tensor(tmp, rest, wide(second), ALU.is_equal))
                link(dve.tensor_tensor(tmp, tmp, order, ALU.mult))
                link(dve.tensor_reduce(second_at, tmp, AX_X, ALU.max))
                link(dve.tensor_tensor(is_second, tmp, wide(second_at), ALU.is_equal))

            def route_weights(k):
                done = [11]

                def link(ins):
                    done[0] += 1
                    ins.then_inc(router_step.sem, 1)
                    dve.wait_ge(router_step.sem, router_step.value(k, done[0]))

                dve.wait_ge(router_exp.sem, router_exp.value(k))
                if k.older(2):
                    dve.wait_ge(gated_ready.sem, gated_ready.value(k.plus(-2)))
                    dve.wait_ge(cwT_psum.sem, cwT_psum.value(k.plus(-2)))
                w_one, w_two = r_one[:, 7, :], r_one[:, 6, :]
                link(dve.tensor_scalar(w_two, r_one[:, 3, :], 1.0, None, ALU.add))
                link(dve.reciprocal(w_one, w_two))
                link(dve.tensor_tensor(w_two, r_one[:, 3, :], w_one, ALU.mult))
                link(dve.tensor_tensor(r_tmp[:, 2], r_tmp[:, 0], bc_last(w_one, E), ALU.mult))
                link(dve.tensor_tensor(r_tmp[:, 3], r_tmp[:, 1], bc_last(w_two, E), ALU.mult))
                tt(cw[:, k.slot, :, 0:E], r_tmp[:, 2], r_tmp[:, 3], ALU.add, cw_ready)

            def mix_parts(k):
                dve.wait_ge(grown2.sem, grown2.value(k))
                dve.wait_ge(sq2_ready.sem, sq2_ready.value(k))
                if k.older(1):
                    o = k.plus(-1)
                    dve.wait_ge(own_prod.sem, own_prod.value(o, OWN_UNITS.index(("pattern", 5)) + 1))
                vx = fx[:, k.slot].rearrange("p (t q) c -> p t q c", t=T)
                vy = fy[:, k.slot].rearrange("p (t q) c -> p t q c", t=T)
                tt(qsum[:], vx[:, :, 0, :], vy[:, :, 0, :], ALU.add, mixed_ready)
                tt(kdif[:], vy[:, :, 1, :], vx[:, :, 1, :], ALU.subtract, mixed_ready)

            def products(k, unit):
                n = OWN_UNITS.index(unit)
                slot = n % 2
                if n >= 2:
                    dve.wait_ge(own_sum.sem, own_sum.value(k, n - 1))
                elif k.older(1):
                    m = max(m for m in range(len(OWN_UNITS)) if m % 2 == n)
                    dve.wait_ge(own_sum.sem, own_sum.value(k.plus(-1), m + 1))
                if unit[0] == "pattern":
                    if n == 0:
                        dve.wait_ge(mixed_ready.sem, mixed_ready.value(k))
                    for part, q, kq in pattern_operands(k, unit[1]):
                        last = dve.tensor_tensor(set_of(slot, part), q, kq, ALU.mult)
                else:
                    dve.wait_ge(amp_ready.sem, amp_ready.value(k))
                    w, v = weighted_operands(k, unit[1])
                    last = dve.tensor_tensor(weighted_slot(slot), w, v, ALU.mult)
                last.then_inc(own_prod.sem, 1)

            def sums(k, unit):
                kind, m = unit
                if unit in POOL_UNITS:
                    n, made, summed, slot = POOL_UNITS.index(unit), pool_prod, pool_sum, 2
                else:
                    n, made, summed = OWN_UNITS.index(unit), own_prod, own_sum
                    slot = n % 2
                dve.wait_ge(made.sem, made.value(k, n + 1))
                if kind == "pattern":
                    (t, _), (t2, _) = PATTERN_SETS[m]
                    dst = pat[:, t, 0:2, :] if t == t2 else pat[:, t:t2 + 1, 2, :]
                    src = prod[:, slot, :].rearrange("p (n g d) -> p n g d", n=2, d=HD)
                else:
                    t, c = m // 2, 2 * (m % 2)
                    dst = u[:, t, c:c + 2, :].rearrange("p c e -> p (c e)")
                    src = prod[:, slot, :].rearrange("p (g j) -> p g j", j=NH)
                dve.tensor_reduce(dst, src, AX_X, ALU.add).then_inc(summed.sem, 1)

            def grown(k, sig, grow_sig, dst_x, dst_y):
                dve.wait_ge(grow_sig.sem, grow_sig.value(k))
                dve.scalar_tensor_tensor(dst_x, zp, 1.0, x1[:, :, HD:C], ALU.add, ALU.mult).then_inc(sig.sem, 1)
                dve.scalar_tensor_tensor(dst_y, zm, 1.0, y1[:, :, HD:C], ALU.add, ALU.mult).then_inc(sig.sem, 1)

            def grown_once(k):
                grown(k, grown1, grow1, x2[:, :, 0:NT * HD], y2[:, :, 0:NT * HD])

            def grown_twice(k):
                if k.older(2):
                    o = k.plus(-2)
                    pattern_summed(dve, o)
                grown(k, grown2, grow2, fx[:, k.slot, :, 0:NT * HD], fy[:, k.slot, :, 0:NT * HD])

            def pattern_power(k):
                pattern_summed(dve, k)
                a, b, c = (pat[:, :, n, :] for n in range(3))
                tt(pr[:, 1], a, b, ALU.subtract, power_step)
                tt(pr[:, 0], a, b, ALU.add, power_step)
                dve.wait_ge(power_step.sem, power_step.value(k, 1))
                tt(pr[:, 2], pr[:, 1], c, ALU.add, power_step)
                dve.wait_ge(power_step.sem, power_step.value(k, 2))
                tt(pr[:, 0], pr[:, 0], pr[:, 0], ALU.mult, power_step)
                dve.wait_ge(power_step.sem, power_step.value(k, 3))
                tt(pr[:, 1], pr[:, 2], pr[:, 2], ALU.mult, power_step)
                dve.wait_ge(power_step.sem, power_step.value(k, 5))
                tt(power, pr[:, 0], pr[:, 1], ALU.add, power_step)
                dve.wait_ge(power_step.sem, power_step.value(k))
                rows = power.rearrange("p t (i j) -> p (t i) j", j=NH)
                dve.tensor_reduce(rowmax[:], rows, AX_X, ALU.max).then_inc(below_step.sem, 1)
                dve.wait_ge(below_step.sem, below_step.value(k, 1))
                tt(below[:].rearrange("p t (i j) -> p (t i) j", j=NH), rows, bc_last(rowmax[:], NH),
                   ALU.subtract, below_step)

            def probabilities(k):
                dve.wait_ge(exp_ready.sem, exp_ready.value(k))
                rows = expo[:].rearrange("p t c (i j) -> p (t c i) j", j=NH)
                dve.tensor_reduce(zsum[:], rows, AX_X, ALU.add).then_inc(probs_step.sem, 1)
                dve.wait_ge(probs_step.sem, probs_step.value(k, 1))
                dve.reciprocal(rz[:], zsum[:]).then_inc(probs_step.sem, 1)
                dve.wait_ge(probs_step.sem, probs_step.value(k, 2))
                tt(rows, rows, bc_last(rz[:], NH), ALU.mult, probs_step)

            def clip_and_mix(k):
                dve.wait_ge(abs_ready.sem, abs_ready.value(k))
                dve.wait_ge(sgn_ready.sem, sgn_ready.value(k))
                dve.tensor_scalar(u[:], u[:], 1e-6, 1.0, ALU.max, ALU.min).then_inc(clip_ready.sem, 1)
                dve.wait_ge(clip_ready.sem, clip_ready.value(k))
                for c in range(NC):
                    dve.scalar_tensor_tensor(u_sgn[:, :, c, :], u[:, :, c, :], sup[:, c:c + 1], u_sgn[:, :, c, :],
                                             ALU.mult, ALU.mult).then_inc(mix_ready.sem, 1)

            def measure(k):
                dve.wait_ge(msum_step.sem, msum_step.value(k))
                dve.wait_ge(phase_ready.sem, phase_ready.value(k))
                if k.older(1):
                    dve.wait_ge(mT_psum.sem, mT_psum.value(k.plus(-1)))
                tt(meas[:].rearrange("p t (i d) -> p t i d", d=HD), msum[:].rearrange("p t (i d) -> p t i d", d=HD),
                   phase[:, k.slot].unsqueeze(2).to_broadcast([P, T, NH, HD]), ALU.mult, meas_ready)

            def add_out(k):
                dve.wait_ge(o_psum.sem, o_psum.value(k))
                dve.wait_ge(y_added.sem, y_added.value(k))
                tt(yacc[:, k.slot], ps_o[:].rearrange("p (t c) -> p t c", t=T), yacc[:, k.slot], ALU.add, out_ready)

            def step(k):
                o, n, far = k.plus(-1), k.plus(1), k.plus(2)
                if n.exists(NB):
                    norm_squares(n)
                if k.exists(NB):
                    products(k, ("pattern", 0))
                if o.exists(NB):
                    clip_and_mix(o)
                if k.exists(NB):
                    sums(k, ("pattern", 1))
                if n.exists(NB):
                    normalise(n)
                if k.exists(NB):
                    sums(k, ("pattern", 0))
                if o.exists(NB):
                    measure(o)
                if k.exists(NB):
                    products(k, ("pattern", 2))
                if n.exists(NB):
                    route(n)
                if k.exists(NB):
                    sums(k, ("pattern", 2))
                    products(k, ("pattern", 3))
                    sums(k, ("pattern", 4))
                    sums(k, ("pattern", 3))
                    products(k, ("pattern", 5))
                if o.exists(NB):
                    add_out(o)
                if k.exists(NB):
                    sums(k, ("pattern", 5))
                    pattern_power(k)
                if n.exists(NB):
                    grown_once(n)
                if far.exists(NB):
                    layer_norm_stats(far)
                if k.exists(NB):
                    probabilities(k)
                if n.exists(NB):
                    route_weights(n)
                    value_phase(n)
                if k.exists(NB):
                    products(k, ("weighted", 0))
                    sums(k, ("weighted", 0))
                    products(k, ("weighted", 2))
                    products(k, ("weighted", 3))
                    sums(k, ("weighted", 2))
                    sums(k, ("weighted", 1))
                    sums(k, ("weighted", 3))
                    products(k, ("weighted", 5))
                if far.exists(NB):
                    layer_norm(far)
                if k.exists(NB):
                    sums(k, ("weighted", 5))
                if n.exists(NB):
                    grown_twice(n)
                if k.exists(NB):
                    sums(k, ("weighted", 4))
                    products(k, ("weighted", 7))
                if n.exists(NB):
                    mix_parts(n)
                if k.exists(NB):
                    sums(k, ("weighted", 7))
                    sums(k, ("weighted", 6))

            run_steps(dve, step)


_INS = ["query", "W_qkv", "b_qkv", "W_out", "b_out", "quantum_weights", "photonic_phases", "entanglement_gates",
        "superposition_logits"]
_FFN = ["Wg", "W1", "b1", "W2", "b2"]


def kernel(**inputs):
    import numpy as _np
    import concourse.bacc as _bacc
    from concourse import mybir as _mybir
    from concourse.bass_utils import run_bass_kernel_spmd as _run

    nc = _bacc.Bacc("TRN2", target_bir_lowering=False, num_devices=1)
    arrays, args = {}, []
    for name in ["L0_attn_" + n for n in _INS] + ["L0_ffn_" + n for n in _FFN]:
        a = _np.ascontiguousarray(inputs[name])
        arrays[f"in_{name}_dram"] = a
        args.append(nc.dram_tensor(f"in_{name}_dram", a.shape, _mybir.dt.from_np(a.dtype), kind="ExternalInput").ap())
    shape = inputs["L0_attn_query"].shape
    args.append(nc.dram_tensor("out_0_dram", shape, _mybir.dt.float32, kind="ExternalOutput").ap())
    build(nc, *args)
    r = _run(nc, [arrays], core_ids=[0])
    return r.results[0]["out_0_dram"]
```

```python
import math
from contextlib import ExitStack

import concourse.bass as bass
from concourse import mybir

ALU = mybir.AluOpType
ACT = mybir.ActivationFunctionType
F32 = mybir.dt.float32
BF16 = mybir.dt.bfloat16
AX_X = mybir.AxisListType.X

P = 128
T = 4
BT = P * T
C = 128
NH = 8
HD = C // NH
NT = NH - 1
NC = 4
DEPTH = 3
E = 8
HID = 512
HC = HID // P
QKV = 3 * C
PROJ = QKV + E
GQ = 2 * T

ANGLES = dict(gamma=(0, 128), eta=(128, 112), theta=(240, 21), turn=(261, 8), twop=(269, 16), p=(285, 16), qw=(301, 4))
NANG = 305
TWO_PI = 2.0 * math.pi
PI_HI = 6.28125
PI_MID = 0.0019350051879882812
PI_LO = TWO_PI - PI_HI - PI_MID
ROUND = 1.5 * 2.0 ** 23
PI_IN = 3.1415925


PATTERN_SETS = [[(0, 0), (0, 1)], [(1, 0), (1, 1)], [(0, 2), (1, 2)], [(2, 0), (2, 1)], [(3, 0), (3, 1)],
                [(2, 2), (3, 2)]]
UNITS = [("pattern", m) for m in range(6)] + [("weighted", m) for m in range(2 * T)]
POOL_UNITS = [("pattern", 1), ("pattern", 4), ("weighted", 1), ("weighted", 4), ("weighted", 6)]
OWN_UNITS = [u for u in UNITS if u not in POOL_UNITS]
PE_UNITS = [("weighted", 0), ("weighted", 1), ("weighted", 5)]
ABS_PARTS = [part for t in range(T)
             for part in ([[2 * t, 2 * t + 1]] if (("weighted", 2 * t) in PE_UNITS) == (("weighted", 2 * t + 1) in PE_UNITS)
                          else [[2 * t], [2 * t + 1]])]
PE_PARTS = [n for n, part in enumerate(ABS_PARTS) if ("weighted", part[0]) in PE_UNITS]


class Blk:

    def __init__(self, pair, slot):
        self.pair, self.slot = pair, slot
        self.value = pair * 2 + slot
        self.number = self.value if type(pair) is int else None

    def plus(self, n):
        return Blk(self.pair + (self.slot + n) // 2, (self.slot + n) % 2)

    def older(self, n):
        return self.number is None or self.number >= n

    def exists(self, nblocks):
        return self.number is None or 0 <= self.number < nblocks


class Signal:

    def __init__(self, sem, per):
        self.sem, self.per = sem, per

    def value(self, k, n=None):
        return k.value * self.per + (self.per if n is None else n)


class SlotSignal:

    def __init__(self, sems):
        self.sems = sems

    def of(self, k):
        return self.sems[k.slot]

    def value(self, k):
        return k.pair * 16 + 16


def bc_mid(ap, n):
    return ap.unsqueeze(1).to_broadcast([ap.shape[0], n, ap.shape[1]])


def bc_last(ap, n):
    return ap.unsqueeze(2).to_broadcast([ap.shape[0], ap.shape[1], n])


def build(nc, query, W_qkv, b_qkv, W_out, b_out, quantum_weights, photonic_phases, entanglement_gates,
          superposition_logits, Wg, W1, b1, W2, b2, out):
    B, S, _ = query.shape
    NB = B * S // BT
    LOOP_FROM, LOOP_TO = 1, NB // 2 - 1

    x_dram = query.rearrange("b s c -> (b s) c")
    out_dram = out.rearrange("b s c -> (b s) c")

    with ExitStack() as ctx:
        def sb(name, shape, dtype=F32):
            return ctx.enter_context(nc.sbuf_tensor(name, shape, dtype))

        def psum(name, shape):
            return ctx.enter_context(nc.psum_tensor(name, shape, F32))

        def sem(name):
            return ctx.enter_context(nc.semaphore(name))

        def signal(name, per=1):
            return Signal(sem(name), per)

        ident = sb("ident", [P, P])
        ones = sb("ones", [P, P])
        w_proj = sb("w_proj", [P, PROJ])
        b_parts = sb("b_parts", [96, PROJ], BF16)
        pick = sb("pick", [96, P], BF16)
        w_outT = sb("w_outT", [P, C])
        w1 = sb("w1", [P, E, HID])
        w2 = sb("w2", [P, E, HC, C])
        b1_cols = sb("b1_cols", [P, E * HC])
        b_rows = sb("b_rows", [E + 1, C])
        prow = sb("prow", [1, 120])
        par = sb("par", [P, 120])
        half = sb("half", [P, 96])
        psi = sb("psi", [P, NH])
        phi_psi = sb("phi_psi", [P, NT])
        fr1 = sb("fr1", [P, NH])
        fr2 = sb("fr2", [P, NH])
        sin_t = sb("sin_t", [P, NANG])
        cos_t = sb("cos_t", [P, NANG])
        alpha = sb("alpha", [P, DEPTH * NT])
        a_plus = sb("a_plus", [P, DEPTH * NT])
        a_minus = sb("a_minus", [P, DEPTH * NT])
        k1x = sb("k1x", [P, NT * HD])
        k1y = sb("k1y", [P, NT * HD])
        ratio = sb("ratio", [P, 2, NC])
        gain = sb("gain", [P, NC])
        sup = sb("sup", [P, NC])
        sup_tmp = sb("sup_tmp", [P, 8])
        eps_ln = sb("eps_ln", [P, 1])
        eps_amp = sb("eps_amp", [P, 1])
        tiny = sb("tiny", [P, 1])
        rank = sb("rank", [P, E])

        x_sb = sb("x_sb", [P, 2, T, C])
        stats = sb("stats", [P, T, 6])
        moments = sb("moments", [P, 3, T])
        sd = sb("sd", [P, T])
        rstd = sb("rstd", [P, T])
        xn = sb("xn", [P, T, C])
        xnT = sb("xnT", [P, 2, BT])
        qkv = sb("qkv", [P, T, PROJ])
        ss = sb("ss", [P, 2, T * 3 * NH])
        norm = sb("norm", [P, T * 3 * NH])
        rnorm = sb("rnorm", [P, T * 3 * NH])
        a0 = sb("a0", [P, GQ, C])
        vT = sb("vT", [P, 2, T, HD, NH])
        vsum = sb("vsum", [P, T, HD])
        f_tmp = sb("f_tmp", [P, 3, T, HD])
        phase = sb("phase", [P, 2, T, HD])
        r_tmp = sb("r_tmp", [P, 4, T, E])
        r_one = sb("r_one", [P, 8, T])
        cw = sb("cw", [P, 2, T, E + 1])
        cwT = sb("cwT", [E + 1, 2, BT])
        sqx = sb("sqx", [P, GQ, NT * HD])
        sqy = sb("sqy", [P, GQ, NT * HD])
        x1 = sb("x1", [P, GQ, C])
        y1 = sb("y1", [P, GQ, C])
        xy2 = sb("xy2", [P, 2, GQ, C])
        x2, y2 = xy2[:, 0], xy2[:, 1]
        sq = xy2.rearrange("p a g c -> p (a g c)")[:, 0:T * QKV].rearrange("p (t c) -> p t c", t=T)
        m1 = sb("m1", [P, GQ, C])
        m2 = sb("m2", [P, GQ, C])
        zp, zm = m1[:, :, 0:NT * HD], m2[:, :, 0:NT * HD]
        fx = sb("fx", [P, 2, GQ, C])
        fy = sb("fy", [P, 2, GQ, C])
        qsum = sb("qsum", [P, T, C])
        kdif = sb("kdif", [P, T, C])
        prod = sb("prod", [P, 3, 2048])
        ang, kk, rem = (prod[:, 0, n * NANG:(n + 1) * NANG] for n in range(3))
        k_tmp = prod[:, 1, 0:4 * NT * HD].rearrange("p (n e) -> p n e", n=4)
        pat = sb("pat", [P, T, 3, NH * NH])
        pr = sb("pr", [P, 3, T, NH * NH])
        power = pr[:, 0]
        rowmax = sb("rowmax", [P, T * NH])
        below = sb("below", [P, T, NH * NH])
        expo = sb("expo", [P, T, NC, NH * NH])
        zsum = sb("zsum", [P, T * NC * NH])
        rz = sb("rz", [P, T * NC * NH])
        u = sb("u", [P, T, NC, C])
        u_sgn = sb("u_sgn", [P, T, NC, C])
        msum = sb("msum", [P, T, C])
        meas = sb("meas", [P, T, C])
        measT = sb("measT", [P, BT])
        hid = sb("hid", [P, 2, HC, BT])
        wqkv_rows = hid[:, 0, 0, 0:QKV].rearrange("p (r c) -> p r c", r=3)
        wout_rows = hid[:, 0, 0, QKV:QKV + C]
        b1_rows = hid[0:E * HC, 0, 1, 0:P]
        b_in = hid[0:96, 0, 2, 0:QKV]
        b_rest = hid[0:96, 0, 3, 0:QKV]
        gated = sb("gated", [P, 2, T, C])
        yacc = sb("yacc", [P, 2, T, C])

        ps_h = psum("ps_h", [P, 4, 512])
        ps_y = psum("ps_y", [P, 2, 512])
        ps_t = psum("ps_t", [P, 512])
        ps_u = psum("ps_u", [P, 2, 256])

        weights_in = sem("weights_in")
        params_in = sem("params_in")
        bias_in = sem("bias_in")
        bias_split = sem("bias_split")
        small_in = sem("small_in")
        experts_in = sem("experts_in")
        ident_made = sem("ident_made")
        ones_made = sem("ones_made")
        setup_psum = sem("setup_psum")
        setup_copied = sem("setup_copied")
        const_step = sem("const_step")
        angles_reduced = sem("angles_reduced")
        angles_folded = sem("angles_folded")
        logits_shifted = sem("logits_shifted")
        const_act = sem("const_act")
        entangle_consts = sem("entangle_consts")
        consts_ready = sem("consts_ready")
        x_loaded = SlotSignal([sem("x_loaded_0"), sem("x_loaded_1")])
        ln_step = signal("ln_step", T + 7)
        sd_ready = signal("sd_ready")
        xn_centred = signal("xn_centred", T)
        xn_ready = signal("xn_ready", T)
        xT_psum = signal("xT_psum")
        xnT_ready = signal("xnT_ready")
        proj_psum = signal("proj_psum", T)
        qkv_ready = signal("qkv_ready", T)
        sq_ready = signal("sq_ready", T)
        ss_step = signal("ss_step", 2)
        norm_ready = signal("norm_ready")
        rnorm_step = signal("rnorm_step", 2)
        a0_ready = signal("a0_ready")
        v_ready = signal("v_ready")
        phase_step = signal("phase_step", 5)
        router_step = signal("router_step", 16)
        phase_ready = signal("phase_ready")
        router_diff = signal("router_diff")
        router_exp = signal("router_exp")
        cw_ready = signal("cw_ready")
        ctrl0_ready = signal("ctrl0_ready")
        depth0 = signal("depth0", 8)
        sq1_ready = signal("sq1_ready", 4)
        grow1 = signal("grow1", 3)
        grown1 = signal("grown1", 2)
        turn_cos = signal("turn_cos", 2)
        turned = signal("turned", 4)
        sq2_ready = signal("sq2_ready", 4)
        grow2 = signal("grow2", 3)
        grown2 = signal("grown2", 2)
        mixed_ready = signal("mixed_ready", 2)
        own_prod = signal("own_prod", len(OWN_UNITS))
        own_sum = signal("own_sum", len([u for u in OWN_UNITS if u not in PE_UNITS]))
        pool_prod = signal("pool_prod", len(POOL_UNITS))
        pool_sum = signal("pool_sum", len([u for u in POOL_UNITS if u not in PE_UNITS]))
        pe_sum = signal("pe_sum", len(PE_UNITS))
        power_step = signal("power_step", 6)
        below_step = signal("below_step", 2)
        exp_ready = signal("exp_ready", NC)
        probs_step = signal("probs_step", 3)
        amp_ready = signal("amp_ready")
        hidden_psum = signal("hidden_psum", E * HC)
        hidden_ready = signal("hidden_ready", E * HC)
        expert_psum = signal("expert_psum", E)
        gated_ready = signal("gated_ready", E)
        y_added = signal("y_added", E)
        cwT_psum = signal("cwT_psum")
        cwT_ready = signal("cwT_ready")
        abs_ready = signal("abs_ready", len(ABS_PARTS))
        sgn_ready = signal("sgn_ready", len(ABS_PARTS))
        clip_ready = signal("clip_ready")
        mix_ready = signal("mix_ready", NC)
        msum_step = signal("msum_step", NC - 1)
        meas_ready = signal("meas_ready")
        mT_psum = signal("mT_psum")
        mT_ready = signal("mT_ready")
        o_psum = signal("o_psum")
        out_ready = signal("out_ready")
        stored = SlotSignal([sem("stored_0"), sem("stored_1")])

        block = ctx.enter_context(nc.Block())

        first = Blk(-1, 0)

        def run_steps(eng, step):
            for n in range(-1, 2 * LOOP_FROM):
                step(Blk(n // 2, n % 2))
            with eng.Fori(LOOP_FROM, LOOP_TO) as pair:
                for slot in range(2):
                    step(Blk(pair, slot))
            for n in range(2 * LOOP_TO, NB + 1):
                step(Blk(n // 2, n % 2))

        def ang_of(table, name):
            at, n = ANGLES[name]
            return table[:, at:at + n]

        def unit_summed(eng, k, unit):
            if unit in PE_UNITS:
                eng.wait_ge(pe_sum.sem, pe_sum.value(k, PE_UNITS.index(unit) + 1))
            else:
                units, summed = (POOL_UNITS, pool_sum) if unit in POOL_UNITS else (OWN_UNITS, own_sum)
                by_dve = [u for u in units if u not in PE_UNITS]
                eng.wait_ge(summed.sem, summed.value(k, by_dve.index(unit) + 1))

        def slot_summed(eng, k, units, slots, n):
            if n >= slots:
                unit_summed(eng, k, units[n - slots])
            elif k.older(1):
                m = max(m for m in range(len(units)) if m % slots == n % slots)
                unit_summed(eng, k.plus(-1), units[m])

        def pattern_summed(eng, k):
            for units in (POOL_UNITS, OWN_UNITS):
                unit_summed(eng, k, [u for u in units if u[0] == "pattern"][-1])

        def pattern_operands(k, m):
            for n, (t, kind) in enumerate(PATTERN_SETS[m]):
                q, kq = ((fx[:, k.slot, 2 * t, :], fx[:, k.slot, 2 * t + 1, :]),
                         (fy[:, k.slot, 2 * t, :], fy[:, k.slot, 2 * t + 1, :]),
                         (qsum[:, t, :], kdif[:, t, :]))[kind]
                yield (n, q.rearrange("p (i d) -> p i d", d=HD).unsqueeze(2).to_broadcast([P, NH, NH, HD]),
                       kq.rearrange("p (j d) -> p j d", d=HD).unsqueeze(1).to_broadcast([P, NH, NH, HD]))

        def weighted_operands(k, m):
            t, c = m // 2, 2 * (m % 2)
            w = expo[:, t, c:c + 2, :].rearrange("p c (i j) -> p (c i) j", j=NH)
            w = w.unsqueeze(2).to_broadcast([P, 2 * NH, HD, NH])
            v = vT[:, k.slot, t].unsqueeze(1).to_broadcast([P, 2 * NH, HD, NH])
            if ("weighted", m) in PE_UNITS:
                w, v = (ap.rearrange("p g d j -> p j g d") for ap in (w, v))
            return w, v

        def set_of(slot, n):
            return prod[:, slot, n * 1024:(n + 1) * 1024].rearrange("p (i j d) -> p i j d", i=NH, j=NH)

        def weighted_slot(slot, m):
            if ("weighted", m) in PE_UNITS:
                return prod[:, slot, :].rearrange("p (j g d) -> p j g d", d=HD, j=NH)
            return prod[:, slot, :].rearrange("p (g d j) -> p g d j", d=HD, j=NH)

        def heads(ap):
            return ap.rearrange("p g (h d) -> p g h d", d=HD)

        def eng_tt(eng, out_, a, b, op, sig):
            eng.tensor_tensor(out_, a, b, op).then_inc(sig.sem, 1)

        def const_hd(ap):
            return bc_mid(ap, GQ)

        def const_h(ap):
            n = ap.shape[1]
            return ap.unsqueeze(1).unsqueeze(3).to_broadcast([P, GQ, n, HD])

        low, high = slice(0, NT * HD), slice(HD, C)

        def entangle0(eng, k):
            if k.number == 0:
                eng.wait_ge(entangle_consts, 1)
            eng.wait_ge(ctrl0_ready.sem, ctrl0_ready.value(k))
            if k.older(1):
                eng.wait_ge(grown2.sem, grown2.value(k.plus(-1)))
            eng_tt(eng, zp, sqx[:], const_hd(k1x[:]), ALU.mult, depth0)
            eng_tt(eng, zm, sqx[:], const_hd(k1y[:]), ALU.mult, depth0)
            gx, gy = ang_of(cos_t, "gamma"), ang_of(sin_t, "gamma")
            eng_tt(eng, x1[:, :, NT * HD:C], a0[:, :, NT * HD:C], const_hd(gx[:, NT * HD:C]), ALU.mult, depth0)
            eng_tt(eng, y1[:, :, NT * HD:C], a0[:, :, NT * HD:C], const_hd(gy[:, NT * HD:C]), ALU.mult, depth0)
            eng.wait_ge(depth0.sem, depth0.value(k, 4))
            eng_tt(eng, zp, zp, const_hd(gx[:, low]), ALU.add, depth0)
            eng_tt(eng, zm, zm, const_hd(gy[:, low]), ALU.add, depth0)
            eng.wait_ge(depth0.sem, depth0.value(k, 6))
            eng_tt(eng, x1[:, :, low], zp, a0[:, :, high], ALU.mult, depth0)
            eng_tt(eng, y1[:, :, low], zm, a0[:, :, high], ALU.mult, depth0)

        def grow(eng, k, sig, depth):
            eng_tt(eng, sqx[:], sqx[:], sqy[:], ALU.add, sig)
            eng.wait_ge(sig.sem, sig.value(k, 1))
            ap, am = a_plus[:, depth * NT:(depth + 1) * NT], a_minus[:, depth * NT:(depth + 1) * NT]
            eng_tt(eng, heads(zp), heads(sqx[:]), const_h(ap), ALU.mult, sig)
            eng_tt(eng, heads(zm), heads(sqx[:]), const_h(am), ALU.mult, sig)

        def entangle1(eng, k):
            eng.wait_ge(depth0.sem, depth0.value(k))
            eng.wait_ge(sq1_ready.sem, sq1_ready.value(k))
            grow(eng, k, grow1, 1)

        def turn(eng, k):
            eng.wait_ge(grown1.sem, grown1.value(k))
            st = const_h(ang_of(sin_t, "turn"))
            eng_tt(eng, heads(m1[:]), heads(y2), st, ALU.mult, turned)
            eng_tt(eng, heads(m2[:]), heads(x2), st, ALU.mult, turned)
            eng.wait_ge(turn_cos.sem, turn_cos.value(k))
            eng.wait_ge(turned.sem, turned.value(k, 2))
            eng_tt(eng, x1[:], x1[:], m1[:], ALU.subtract, turned)
            eng_tt(eng, y1[:], y1[:], m2[:], ALU.add, turned)

        def entangle2(eng, k):
            eng.wait_ge(turned.sem, turned.value(k))
            eng.wait_ge(sq2_ready.sem, sq2_ready.value(k))
            grow(eng, k, grow2, 2)

        @block.sync
        def _(sp):
            def load_x(k):
                if k.older(2):
                    sp.wait_ge(y_added.sem, y_added.value(k.plus(-2), 1))
                src = x_dram[bass.ds(k.value * BT, BT), :].rearrange("(t p) c -> p t c", p=P)
                sp.dma_start(x_sb[:, k.slot], src).then_inc(x_loaded.of(k), 16)

            def store(k):
                sp.wait_ge(out_ready.sem, out_ready.value(k))
                dst = out_dram[bass.ds(k.value * BT, BT), :].rearrange("(t p) c -> p t c", p=P)
                sp.dma_start(dst, yacc[:, k.slot]).then_inc(stored.of(k), 16)

            load_x(Blk(0, 0))
            sp.dma_start(b_in, b_qkv.unsqueeze(0).to_broadcast([96, QKV])).then_inc(bias_in, 16)
            sp.dma_start(wqkv_rows, W_qkv.rearrange("(r p) c -> p r c", p=P)).then_inc(weights_in, 16)
            sp.dma_start(wout_rows, W_out).then_inc(weights_in, 16)
            sp.dma_start(w_proj[:, QKV:PROJ], Wg).then_inc(weights_in, 16)
            flat = photonic_phases.rearrange("a b -> (a b)")
            diag = flat[0:(HD - 1) * (C + 1) + 1:C + 1]
            sp.dma_start(prow[:, 0:16], diag.unsqueeze(0), allow_slow_non_contiguous=True).then_inc(params_in, 16)
            sp.dma_start(prow[:, 16:112],
                         entanglement_gates.rearrange("a b c -> (a b c)").unsqueeze(0)).then_inc(params_in, 16)
            sp.dma_start(prow[:, 112:116], quantum_weights[:, 0, 0].unsqueeze(0),
                         allow_slow_non_contiguous=True).then_inc(params_in, 16)
            sp.dma_start(prow[:, 116:120], superposition_logits.unsqueeze(0)).then_inc(params_in, 16)
            sp.dma_start(b1_rows, b1.rearrange("e (c p) -> (e c) p", p=P)).then_inc(small_in, 16)
            sp.dma_start(b_rows[0:E, :], b2).then_inc(small_in, 16)
            sp.dma_start(b_rows[E:E + 1, :], b_out.unsqueeze(0)).then_inc(small_in, 16)
            sp.dma_start(w1[:], W1.rearrange("e c h -> c e h")).then_inc(experts_in, 16)
            sp.dma_start(w2[:], W2.rearrange("e (c p) n -> p e c n", p=P)).then_inc(experts_in, 16)

            def step(k):
                if k.plus(-2).exists(NB):
                    store(k.plus(-2))
                if k.plus(2).exists(NB) and not (k.number is not None and k.number < -1):
                    load_x(k.plus(2))

            step(first)
            run_steps(sp, step)
            store(Blk((NB - 1) // 2, (NB - 1) % 2))
            for last in (NB - 2, NB - 1):
                sp.wait_ge(stored.of(Blk(last // 2, last % 2)), stored.value(Blk(last // 2, last % 2)))

        @block.tensor
        def _(pe):
            pe.wait_ge(ident_made, 2)
            pe.wait_ge(weights_in, 48)
            for r in range(3):
                last = nc.tensor.transpose(ps_h[:, 0, r * P:(r + 1) * P], wqkv_rows[:, r, :], ident[:])
            last = nc.tensor.transpose(ps_h[:, 0, 3 * P:4 * P], wout_rows, ident[:])
            last.then_inc(setup_psum, 1)
            pe.wait_ge(params_in, 64)
            pe.wait_ge(ones_made, 1)
            nc.tensor.matmul(ps_y[:, 0, 0:120], ones[0:1, :], prow[:], start=True, stop=True).then_inc(setup_psum, 1)
            pe.wait_ge(small_in, 48)
            nc.tensor.transpose(ps_y[:, 1, 0:E * HC], b1_rows, ident[0:E * HC, 0:E * HC]).then_inc(setup_psum, 1)

            def experts(k, e):
                if e == 0:
                    pe.wait_ge(xnT_ready.sem, xnT_ready.value(k))
                    if k.number == 0:
                        pe.wait_ge(experts_in, 32)
                        pe.wait_ge(setup_copied, 3)
                for c in range(HC):
                    n = e * HC + c
                    if e > 0:
                        pe.wait_ge(hidden_ready.sem, hidden_ready.value(k, n - HC + 1))
                    elif k.plus(1).exists(NB):
                        pe.wait_ge(sq_ready.sem, sq_ready.value(k.plus(1), c + 1))
                    else:
                        pe.wait_ge(hidden_ready.sem, hidden_ready.value(k.plus(-1), (E - 1) * HC + c + 1))
                    nc.tensor.matmul(ps_h[:, c, :], w1[:, e, c * P:(c + 1) * P], xnT[:, k.slot, :],
                                     start=True, stop=True).then_inc(hidden_psum.sem, 1)
                    if e > 0:
                        expert_out(k, e - 1, c)

            def expert_out(k, e, t):
                if t == 0:
                    if e >= 2:
                        pe.wait_ge(gated_ready.sem, gated_ready.value(k, e - 1))
                    elif k.older(1):
                        pe.wait_ge(gated_ready.sem, gated_ready.value(k.plus(-1), E + e - 1))
                    elif e == 0:
                        pe.wait_ge(setup_copied, 4)
                    pe.wait_ge(hidden_ready.sem, hidden_ready.value(k, (e + 1) * HC))
                for c in range(HC):
                    last = nc.tensor.matmul(ps_y[:, e % 2, t * P:(t + 1) * P], hid[:, e % 2, c, t * P:(t + 1) * P],
                                            w2[:, e, c, :], start=(c == 0), stop=(c == HC - 1))
                if t == T - 1:
                    last.then_inc(expert_psum.sem, 1)

            def sums(k, unit):
                n = PE_UNITS.index(unit)
                units, made, first_slot, slots = ((POOL_UNITS, pool_prod, 2, 1) if unit in POOL_UNITS else
                                                  (OWN_UNITS, own_prod, 0, 2))
                at = units.index(unit)
                slot = first_slot + at % slots
                pe.wait_ge(made.sem, made.value(k, at + 1))
                part = [p for p in PE_PARTS if unit[1] in ABS_PARTS[p]][0]
                if unit[1] == ABS_PARTS[part][0]:
                    if part != PE_PARTS[0]:
                        pe.wait_ge(abs_ready.sem, abs_ready.value(k, PE_PARTS[PE_PARTS.index(part) - 1] + 1))
                    elif k.older(1):
                        pe.wait_ge(abs_ready.sem, abs_ready.value(k.plus(-1), PE_PARTS[-1] + 1))
                for j in range(NH):
                    last = nc.tensor.matmul(ps_u[:, ABS_PARTS[part].index(unit[1]), :], ident[:], prod[:, slot, j * 256:(j + 1) * 256],
                                            start=(j == 0), stop=(j == NH - 1))
                last.then_inc(pe_sum.sem, 1)

            def last_expert_out(k):
                for t in range(T):
                    expert_out(k, E - 1, t)

            def turn_x(k):
                pe.wait_ge(xn_ready.sem, xn_ready.value(k))
                if k.older(2):
                    pe.wait_ge(cwT_ready.sem, cwT_ready.value(k.plus(-2)))
                elif k.older(1):
                    pe.wait_ge(xnT_ready.sem, xnT_ready.value(k.plus(-1)))
                for t in range(T):
                    last = nc.tensor.transpose(ps_t[:, t * P:(t + 1) * P], xn[:, t, :], ident[:])
                last.then_inc(xT_psum.sem, 1)

            def project(k):
                pe.wait_ge(xnT_ready.sem, xnT_ready.value(k))
                if k.number == 0:
                    pe.wait_ge(setup_copied, 3)
                    pe.wait_ge(bias_split, 11)
                for t in range(T):
                    if k.older(2):
                        pe.wait_ge(hidden_ready.sem, hidden_ready.value(k.plus(-2), (E - 1) * HC + t + 1))
                    elif k.older(1):
                        pe.wait_ge(sq_ready.sem, sq_ready.value(k.plus(-1), t + 1))
                    nc.tensor.matmul(ps_h[:, t, 0:PROJ], xnT[:, k.slot, t * P:(t + 1) * P], w_proj[:],
                                     start=True, stop=False)
                    nc.tensor.matmul(ps_h[:, t, 0:PROJ], pick[:], b_parts[:],
                                     start=False, stop=True).then_inc(proj_psum.sem, 1)

            def turn_cw(k):
                pe.wait_ge(cw_ready.sem, cw_ready.value(k))
                if k.older(1):
                    pe.wait_ge(out_ready.sem, out_ready.value(k.plus(-1)))
                else:
                    pe.wait_ge(xnT_ready.sem, xnT_ready.value(k.plus(1)))
                for t in range(T):
                    last = nc.tensor.transpose(ps_t[0:E + 1, t * P:(t + 1) * P], cw[:, k.slot, t, :], ident[:])
                last.then_inc(cwT_psum.sem, 1)

            def turn_m(k):
                pe.wait_ge(meas_ready.sem, meas_ready.value(k))
                if k.plus(2).exists(NB):
                    pe.wait_ge(xnT_ready.sem, xnT_ready.value(k.plus(2)))
                else:
                    pe.wait_ge(cwT_ready.sem, cwT_ready.value(k))
                for t in range(T):
                    last = nc.tensor.transpose(ps_t[:, t * P:(t + 1) * P], meas[:, t, :], ident[:])
                last.then_inc(mT_psum.sem, 1)

            def project_out(k):
                pe.wait_ge(mT_ready.sem, mT_ready.value(k))
                pe.wait_ge(cwT_ready.sem, cwT_ready.value(k))
                for t in range(T):
                    cols = slice(t * P, (t + 1) * P)
                    nc.tensor.matmul(ps_t[:, cols], measT[:, cols], w_outT[:], start=True, stop=False)
                    last = nc.tensor.matmul(ps_t[:, cols], cwT[:, k.slot, cols], b_rows[:], start=False, stop=True)
                last.then_inc(o_psum.sem, 1)

            def step(k):
                o, n, far = k.plus(-1), k.plus(1), k.plus(2)
                if n.exists(NB):
                    project(n)
                if k.exists(NB):
                    experts(k, 0)
                    experts(k, 1)
                    experts(k, 2)
                if o.exists(NB):
                    turn_m(o)
                if k.exists(NB):
                    experts(k, 3)
                if o.exists(NB):
                    project_out(o)
                if k.exists(NB):
                    experts(k, 4)
                    turn_cw(k)
                    experts(k, 5)
                    sums(k, ("weighted", 0))
                    sums(k, ("weighted", 1))
                    experts(k, 6)
                    sums(k, ("weighted", 5))
                if far.exists(NB):
                    turn_x(far)
                if k.exists(NB):
                    experts(k, 7)
                    last_expert_out(k)

            step(first)
            run_steps(pe, step)

        @block.scalar
        def _(act):
            act.wait_ge(setup_psum, 1)
            act.activation(w_proj[:, 0:QKV], ps_h[:, 0, 0:QKV], ACT.Copy).then_inc(setup_copied, 1)
            act.activation(w_outT[:], ps_h[:, 0, QKV:QKV + C], ACT.Copy).then_inc(setup_copied, 1)
            act.wait_ge(setup_psum, 2)
            act.activation(par[:], ps_y[:, 0, 0:120], ACT.Copy).then_inc(setup_copied, 1)
            act.wait_ge(setup_psum, 3)
            act.activation(b1_cols[:], ps_y[:, 1, 0:E * HC], ACT.Copy).then_inc(setup_copied, 1)

            def angle_tables():
                act.wait_ge(angles_reduced, 1)
                act.activation(sin_t[:], rem, ACT.Sin).then_inc(const_act, 1)
                act.activation(kk, rem, ACT.Abs).then_inc(const_act, 1)
                act.wait_ge(angles_folded, 1)
                act.activation(cos_t[:], kk, ACT.Sin).then_inc(const_act, 1)
                act.wait_ge(logits_shifted, 1)
                act.activation(sup_tmp[:, 4:8], sup_tmp[:, 0:4], ACT.Exp).then_inc(const_act, 1)

            def ln_sd(k):
                act.wait_ge(ln_step.sem, ln_step.value(k, T + 6))
                if k.older(1):
                    act.wait_ge(ln_step.sem, ln_step.value(k.plus(-1)))
                if k.number == 0:
                    act.wait_ge(consts_ready, 1)
                act.activation(sd[:], moments[:, 2], ACT.Sqrt, bias=eps_ln[:, 0:1], scale=1.0 / C).then_inc(sd_ready.sem, 1)

            def layer_norm(k):
                act.wait_ge(ln_step.sem, ln_step.value(k))
                act.wait_ge(x_loaded.of(k), x_loaded.value(k))
                if k.older(1):
                    act.wait_ge(xT_psum.sem, xT_psum.value(k.plus(-1)))
                for t in range(T):
                    act.activation(xn[:, t, :], x_sb[:, k.slot, t, :], ACT.Identity,
                                   bias=moments[:, 0, t:t + 1]).then_inc(xn_centred.sem, 1)
                for t in range(T):
                    act.wait_ge(xn_centred.sem, xn_centred.value(k, t + 1))
                    act.activation(xn[:, t, :], xn[:, t, :], ACT.Copy, scale=rstd[:, t:t + 1]).then_inc(xn_ready.sem, 1)

            def copy_xT(k):
                act.wait_ge(xT_psum.sem, xT_psum.value(k))
                if k.older(2):
                    o = k.plus(-2)
                    act.wait_ge(hidden_psum.sem, hidden_psum.value(o))
                act.activation(xnT[:, k.slot, :], ps_t[:], ACT.Copy).then_inc(xnT_ready.sem, 1)

            def copy_proj(k):
                if k.older(1):
                    o = k.plus(-1)
                    act.wait_ge(v_ready.sem, v_ready.value(o))
                    act.wait_ge(a0_ready.sem, a0_ready.value(o))
                    act.wait_ge(router_step.sem, router_step.value(o, 6))
                    act.wait_ge(ss_step.sem, ss_step.value(o, 1))
                    act.wait_ge(turned.sem, turned.value(o))
                for t in range(T):
                    act.wait_ge(proj_psum.sem, proj_psum.value(k, t + 1))
                    act.activation(qkv[:, t, :], ps_h[:, t, 0:PROJ], ACT.Copy).then_inc(qkv_ready.sem, 1)
                    act.activation(sq[:, t, :], ps_h[:, t, 0:QKV], ACT.Square).then_inc(sq_ready.sem, 1)

            def norm_sqrt(k):
                act.wait_ge(ss_step.sem, ss_step.value(k))
                if k.older(1):
                    act.wait_ge(rnorm_step.sem, rnorm_step.value(k.plus(-1), 1))
                act.activation(norm[:], ss[:, 1, :], ACT.Sqrt).then_inc(norm_ready.sem, 1)

            def control0(k):
                act.wait_ge(a0_ready.sem, a0_ready.value(k))
                if k.older(1):
                    act.wait_ge(grow2.sem, grow2.value(k.plus(-1)))
                act.activation(sqx[:], a0[:, :, 0:NT * HD], ACT.Square).then_inc(ctrl0_ready.sem, 1)

            def control1(k):
                act.wait_ge(depth0.sem, depth0.value(k))
                act.activation(sqx[:], x1[:, :, 0:NT * HD], ACT.Square).then_inc(sq1_ready.sem, 1)
                act.activation(sqy[:], y1[:, :, 0:NT * HD], ACT.Square).then_inc(sq1_ready.sem, 1)
                act.activation(x2[:, :, NT * HD:C], x1[:, :, NT * HD:C], ACT.Copy).then_inc(sq1_ready.sem, 1)
                act.activation(y2[:, :, NT * HD:C], y1[:, :, NT * HD:C], ACT.Copy).then_inc(sq1_ready.sem, 1)

            def control2(k):
                act.wait_ge(turned.sem, turned.value(k))
                if k.older(2):
                    pattern_summed(act, k.plus(-2))
                act.activation(sqx[:], x1[:, :, 0:NT * HD], ACT.Square).then_inc(sq2_ready.sem, 1)
                act.activation(sqy[:], y1[:, :, 0:NT * HD], ACT.Square).then_inc(sq2_ready.sem, 1)
                act.activation(fx[:, k.slot, :, NT * HD:C], x1[:, :, NT * HD:C], ACT.Copy).then_inc(sq2_ready.sem, 1)
                act.activation(fy[:, k.slot, :, NT * HD:C], y1[:, :, NT * HD:C], ACT.Copy).then_inc(sq2_ready.sem, 1)

            def router_softmax(k):
                act.wait_ge(router_diff.sem, router_diff.value(k))
                if k.older(1):
                    act.wait_ge(cw_ready.sem, cw_ready.value(k.plus(-1)))
                act.activation(r_one[:, 3, :], r_one[:, 2, :], ACT.Exp).then_inc(router_exp.sem, 1)

            def score_exp(k):
                act.wait_ge(below_step.sem, below_step.value(k))
                if k.older(1):
                    act.wait_ge(own_prod.sem, own_prod.value(k.plus(-1)))
                    act.wait_ge(pool_prod.sem, pool_prod.value(k.plus(-1)))
                for c in range(NC):
                    act.activation(expo[:, :, c, :], below[:], ACT.Exp,
                                   scale=gain[:, c:c + 1]).then_inc(exp_ready.sem, 1)

            def amplitude(k):
                act.wait_ge(probs_step.sem, probs_step.value(k))
                act.activation(expo[:], expo[:], ACT.Sqrt, bias=eps_amp[:, 0:1]).then_inc(amp_ready.sem, 1)

            def turn_cosines(k):
                act.wait_ge(grown1.sem, grown1.value(k))
                ct = ang_of(cos_t, "turn")
                for src, dst in ((x2, x1), (y2, y1)):
                    for h in range(NH):
                        cols = slice(h * HD, (h + 1) * HD)
                        last = act.activation(dst[:, :, cols], src[:, :, cols], ACT.Copy, scale=ct[:, h:h + 1])
                    last.then_inc(turn_cos.sem, 1)

            def abs_sign(k, n):
                units = ABS_PARTS[n]
                for m in units:
                    unit_summed(act, k, ("weighted", m))
                if k.older(1):
                    act.wait_ge(msum_step.sem, msum_step.value(k.plus(-1)))
                t, c = units[0] // 2, 2 * (units[0] % 2)
                circuits = slice(c, c + 2 * len(units))
                dst = u[:, t, circuits, :]
                src = dst
                if ("weighted", units[0]) in PE_UNITS:
                    src = ps_u[:, 0:len(units), :].rearrange("p m (c e) -> p (m c) e", c=2)
                act.activation(u_sgn[:, t, circuits, :], src, ACT.Sign, bias=tiny[:, 0:1]).then_inc(sgn_ready.sem, 1)
                act.wait_ge(sgn_ready.sem, sgn_ready.value(k, n + 1))
                act.activation(dst, src, ACT.Abs).then_inc(abs_ready.sem, 1)

            def gelu(k, e):
                for c in range(HC):
                    n = e * HC + c
                    act.wait_ge(hidden_psum.sem, hidden_psum.value(k, n + 1))
                    if c == 0:
                        if e >= 2:
                            act.wait_ge(expert_psum.sem, expert_psum.value(k, e - 1))
                        elif k.older(1):
                            act.wait_ge(expert_psum.sem, expert_psum.value(k.plus(-1), E + e - 1))
                    act.activation(hid[:, e % 2, c, :], ps_h[:, c, :], ACT.Gelu,
                                   bias=b1_cols[:, n:n + 1]).then_inc(hidden_ready.sem, 1)

            def gate(k, e):
                act.wait_ge(expert_psum.sem, expert_psum.value(k, e + 1))
                if e == 0:
                    act.wait_ge(cw_ready.sem, cw_ready.value(k))
                if e >= 2:
                    act.wait_ge(y_added.sem, y_added.value(k, e - 1))
                elif k.older(1):
                    act.wait_ge(y_added.sem, y_added.value(k.plus(-1), E + e - 1))
                for t in range(T):
                    last = act.activation(gated[:, e % 2, t, :], ps_y[:, e % 2, t * P:(t + 1) * P], ACT.Copy,
                                          scale=cw[:, k.slot, t, e:e + 1])
                last.then_inc(gated_ready.sem, 1)

            def copy_cwT(k):
                act.wait_ge(cwT_psum.sem, cwT_psum.value(k))
                if k.older(2):
                    act.wait_ge(o_psum.sem, o_psum.value(k.plus(-2)))
                act.activation(cwT[:, k.slot, :], ps_t[0:E + 1, :], ACT.Copy).then_inc(cwT_ready.sem, 1)

            def copy_mT(k):
                act.wait_ge(mT_psum.sem, mT_psum.value(k))
                if k.older(1):
                    act.wait_ge(o_psum.sem, o_psum.value(k.plus(-1)))
                act.activation(measT[:], ps_t[:], ACT.Copy).then_inc(mT_ready.sem, 1)

            def step(k):
                o, n, far = k.plus(-1), k.plus(1), k.plus(2)
                if o.exists(NB):
                    abs_sign(o, 4)
                if n.exists(NB):
                    copy_proj(n)
                if o.exists(NB):
                    gate(o, 6)
                if k.exists(NB):
                    gelu(k, 0)
                if n.exists(NB):
                    norm_sqrt(n)
                if o.exists(NB):
                    gate(o, 7)
                if k.exists(NB):
                    gelu(k, 1)
                if n.exists(NB):
                    control0(n)
                if k.exists(NB):
                    gelu(k, 2)
                    gate(k, 0)
                    gate(k, 1)
                if o.exists(NB):
                    copy_mT(o)
                if k.exists(NB):
                    gelu(k, 3)
                if n.exists(NB):
                    router_softmax(n)
                    control1(n)
                if k.exists(NB):
                    gate(k, 2)
                    score_exp(k)
                    gelu(k, 4)
                    amplitude(k)
                    gate(k, 3)
                if n.exists(NB):
                    turn_cosines(n)
                if k.exists(NB):
                    copy_cwT(k)
                if far.exists(NB):
                    ln_sd(far)
                if k.exists(NB):
                    gelu(k, 5)
                    abs_sign(k, 0)
                if n.exists(NB):
                    control2(n)
                if k.exists(NB):
                    gelu(k, 6)
                    abs_sign(k, 1)
                if far.exists(NB):
                    layer_norm(far)
                if k.exists(NB):
                    gate(k, 4)
                    abs_sign(k, 2)
                    abs_sign(k, 3)
                    gate(k, 5)
                    gelu(k, 7)
                if far.exists(NB):
                    copy_xT(far)

            step(first)
            angle_tables()
            run_steps(act, step)

        @block.gpsimd
        def _(pool):
            pool.memset(ident[:], 0.0).then_inc(ident_made, 1)
            pool.memset(ones[:], 1.0).then_inc(ones_made, 1)
            pool.wait_ge(ident_made, 1)
            pool.affine_select(out=ident[:], in_=ident[:], compare_op=ALU.not_equal, fill=1.0, base=0,
                               pattern=[[-1, P]], channel_multiplier=1).then_inc(ident_made, 1)
            done = [0]

            def split(ins):
                done[0] += 1
                ins.then_inc(bias_split, 1)
                pool.wait_ge(bias_split, done[0])

            split(pool.memset(pick[:], 0.0))
            for row in (0, 32, 64):
                split(pool.memset(pick[row:row + 1, :], 1.0))
            split(pool.memset(b_parts[:, QKV:PROJ], 0.0))
            pool.wait_ge(bias_in, 16)
            split(pool.tensor_copy(b_parts[:, 0:QKV], b_in))
            split(pool.tensor_tensor(b_rest, b_in, b_parts[:, 0:QKV], ALU.subtract))
            split(pool.tensor_copy(b_parts[32:64, 0:QKV], b_rest[32:64, :]))
            split(pool.tensor_copy(b_parts[64:96, 0:QKV], b_rest[64:96, :]))
            split(pool.tensor_tensor(b_rest[64:96, :], b_rest[64:96, :], b_parts[64:96, 0:QKV], ALU.subtract))
            split(pool.tensor_copy(b_parts[64:96, 0:QKV], b_rest[64:96, :]))

            def tt(out_, a, b, op, sig):
                pool.tensor_tensor(out_, a, b, op).then_inc(sig.sem, 1)

            def mix_parts(k):
                pool.wait_ge(grown2.sem, grown2.value(k))
                pool.wait_ge(sq2_ready.sem, sq2_ready.value(k))
                if k.older(1):
                    pool.wait_ge(own_prod.sem, own_prod.value(k.plus(-1), OWN_UNITS.index(("pattern", 5)) + 1))
                vx = fx[:, k.slot].rearrange("p (t q) c -> p t q c", t=T)
                vy = fy[:, k.slot].rearrange("p (t q) c -> p t q c", t=T)
                tt(qsum[:], vx[:, :, 0, :], vy[:, :, 0, :], ALU.add, mixed_ready)
                tt(kdif[:], vy[:, :, 1, :], vx[:, :, 1, :], ALU.subtract, mixed_ready)

            def by_pool(part, k):
                if k.number != 0:
                    part(pool, k)

            def products(k, unit):
                n = POOL_UNITS.index(unit)
                slot_summed(pool, k, POOL_UNITS, 1, n)
                if unit[0] == "pattern":
                    if n == 0:
                        pool.wait_ge(grown2.sem, grown2.value(k))
                        pool.wait_ge(sq2_ready.sem, sq2_ready.value(k))
                    for part, q, kq in pattern_operands(k, unit[1]):
                        last = pool.tensor_tensor(set_of(2, part), q, kq, ALU.mult)
                else:
                    pool.wait_ge(amp_ready.sem, amp_ready.value(k))
                    w, v = weighted_operands(k, unit[1])
                    last = pool.tensor_tensor(weighted_slot(2, unit[1]), w, v, ALU.mult)
                last.then_inc(pool_prod.sem, 1)

            def add_expert(k, e):
                pool.wait_ge(gated_ready.sem, gated_ready.value(k, e + 1))
                if e == 0 and k.older(2):
                    pool.wait_ge(stored.of(k), stored.value(k.plus(-2)))
                if e > 0:
                    pool.wait_ge(y_added.sem, y_added.value(k, e))
                base = x_sb[:, k.slot] if e == 0 else yacc[:, k.slot]
                tt(yacc[:, k.slot], gated[:, e % 2], base, ALU.add, y_added)

            def sum_circuits(k):
                if k.older(1):
                    pool.wait_ge(meas_ready.sem, meas_ready.value(k.plus(-1)))
                for c in range(1, NC):
                    pool.wait_ge(mix_ready.sem, mix_ready.value(k, c + 1))
                    if c > 1:
                        pool.wait_ge(msum_step.sem, msum_step.value(k, c - 1))
                    tt(msum[:], u_sgn[:, :, 0, :] if c == 1 else msum[:], u_sgn[:, :, c, :], ALU.add, msum_step)

            def step(k):
                o, n = k.plus(-1), k.plus(1)
                if k.exists(NB):
                    products(k, ("pattern", 1))
                if o.exists(NB):
                    add_expert(o, 6)
                    sum_circuits(o)
                    add_expert(o, 7)
                if k.exists(NB):
                    products(k, ("pattern", 4))
                if n.exists(NB):
                    by_pool(entangle0, n)
                if k.exists(NB):
                    add_expert(k, 0)
                    add_expert(k, 1)
                if n.exists(NB):
                    by_pool(entangle1, n)
                if k.exists(NB):
                    add_expert(k, 2)
                    products(k, ("weighted", 1))
                if n.exists(NB):
                    by_pool(turn, n)
                if k.exists(NB):
                    products(k, ("weighted", 4))
                if n.exists(NB):
                    by_pool(entangle2, n)
                if k.exists(NB):
                    add_expert(k, 3)
                    products(k, ("weighted", 6))
                if n.exists(NB):
                    mix_parts(n)
                if k.exists(NB):
                    add_expert(k, 4)
                    add_expert(k, 5)

            step(first)
            run_steps(pool, step)

        @block.vector
        def _(dve):
            steps = [0]

            def const(ins, named=None):
                if named is None:
                    steps[0] += 1
                    ins.then_inc(const_step, 1)
                    dve.wait_ge(const_step, steps[0])
                else:
                    ins.then_inc(named, 1)
                    dve.wait_ge(named, 1)

            const(dve.memset(eps_ln[:], 1e-5))
            const(dve.memset(eps_amp[:], 1e-12))
            const(dve.memset(tiny[:], 1e-30))
            for j in range(E):
                const(dve.memset(rank[:, j:j + 1], float(E - j)))
            for slot in range(2):
                const(dve.memset(cw[:, slot, :, E:E + 1], 1.0), None if slot == 0 else consts_ready)

            def angle_constants():
                dve.wait_ge(setup_copied, 3)
                phases = par[:, 0:HD]
                gates = par[:, 16:112].rearrange("p (a h c) -> p a h c", a=DEPTH, h=NH)
                halves = half[:].rearrange("p (a h c) -> p a h c", a=DEPTH, h=NH)
                const(dve.tensor_scalar(half[:], par[:, 16:112], 0.5, None, ALU.mult))
                const(dve.tensor_copy(psi[:, 1:NH], halves[:, 1, 0:NT, 1]))
                const(dve.tensor_copy(psi[:, 0:1], halves[:, 0, 0:1, 1]))
                const(dve.tensor_tensor(phi_psi[:], gates[:, 0, 0:NT, 1], psi[:, 0:NT], ALU.subtract))
                const(dve.tensor_tensor(ang_of(ang, "gamma").rearrange("p (h d) -> p h d", d=HD), bc_mid(phases, NH),
                                        bc_last(psi[:], HD), ALU.subtract))
                const(dve.tensor_tensor(ang_of(ang, "eta").rearrange("p (h d) -> p h d", d=HD), bc_last(phi_psi[:], HD),
                                        bc_mid(phases, NT), ALU.subtract))
                const(dve.tensor_copy(ang_of(ang, "theta").rearrange("p (a h) -> p a h", a=DEPTH), halves[:, :, 0:NT, 0]))
                const(dve.tensor_copy(fr1[:, 0:NT], halves[:, 1, 0:NT, 1]))
                const(dve.tensor_copy(fr1[:, NT:NH], halves[:, 1, NT - 1:NT, 1]))
                const(dve.tensor_copy(fr2[:, 1:NH], halves[:, 2, 0:NT, 1]))
                const(dve.tensor_copy(fr2[:, 0:1], halves[:, 1, 0:1, 1]))
                const(dve.tensor_tensor(ang_of(ang, "turn"), fr1[:], fr2[:], ALU.subtract))
                const(dve.tensor_scalar(ang_of(ang, "twop"), phases, 2.0, None, ALU.mult))
                const(dve.tensor_copy(ang_of(ang, "p"), phases))
                const(dve.tensor_copy(ang_of(ang, "qw"), par[:, 112:116]))
                const(dve.tensor_scalar(kk, ang, 1.0 / TWO_PI, ROUND, ALU.mult, ALU.add))
                const(dve.tensor_scalar(kk, kk, ROUND, None, ALU.subtract))
                const(dve.scalar_tensor_tensor(rem, kk, -PI_HI, ang, ALU.mult, ALU.add))
                const(dve.scalar_tensor_tensor(rem, kk, -PI_MID, rem, ALU.mult, ALU.add))
                const(dve.scalar_tensor_tensor(rem, kk, -PI_LO, rem, ALU.mult, ALU.add))
                const(dve.tensor_scalar(rem, rem, PI_IN, -PI_IN, ALU.min, ALU.max), angles_reduced)
                dve.wait_ge(const_act, 2)
                const(dve.tensor_scalar(kk, kk, -1.0, math.pi / 2, ALU.mult, ALU.add), angles_folded)
                const(dve.tensor_reduce(ratio[:, 0, 0:1], par[:, 116:120], AX_X, ALU.max))
                const(dve.tensor_scalar(sup_tmp[:, 0:4], par[:, 116:120], ratio[:, 0, 0:1], None, ALU.subtract),
                      logits_shifted)
                dve.wait_ge(const_act, 4)
                const(dve.tensor_reduce(ratio[:, 0, 0:1], sup_tmp[:, 4:8], AX_X, ALU.add))
                const(dve.reciprocal(ratio[:, 0, 1:2], ratio[:, 0, 0:1]))
                const(dve.tensor_scalar(sup[:], sup_tmp[:, 4:8], ratio[:, 0, 1:2], None, ALU.mult))
                const(dve.tensor_scalar(ratio[:, 0, :], ang_of(sin_t, "qw"), 0.3, 0.5, ALU.mult, ALU.add))
                const(dve.tensor_scalar(ratio[:, 1, :], ratio[:, 0, :], -1.0, 1.0, ALU.mult, ALU.add))
                const(dve.scalar_tensor_tensor(gain[:], ratio[:, 0, :], HD ** -0.5, ratio[:, 1, :], ALU.mult, ALU.mult))
                const(dve.tensor_scalar(alpha[:], ang_of(cos_t, "theta"), 1.0, None, ALU.subtract))
                const(dve.tensor_tensor(a_plus[:], alpha[:], ang_of(sin_t, "theta"), ALU.add))
                const(dve.tensor_tensor(a_minus[:], alpha[:], ang_of(sin_t, "theta"), ALU.subtract))
                for n, (table, name, factor) in enumerate(((cos_t, "gamma", alpha[:, 0:NT]),
                                                           (cos_t, "eta", ang_of(sin_t, "theta")[:, 0:NT]),
                                                           (sin_t, "gamma", alpha[:, 0:NT]),
                                                           (sin_t, "eta", ang_of(sin_t, "theta")[:, 0:NT]))):
                    const(dve.tensor_tensor(k_tmp[:, n].rearrange("p (h d) -> p h d", d=HD),
                                            ang_of(table, name)[:, 0:NT * HD].rearrange("p (h d) -> p h d", d=HD),
                                            bc_last(factor, HD), ALU.mult))
                const(dve.tensor_tensor(k1x[:], k_tmp[:, 0], k_tmp[:, 1], ALU.add))
                const(dve.tensor_tensor(k1y[:], k_tmp[:, 2], k_tmp[:, 3], ALU.add), entangle_consts)

            def tt(out_, a, b, op, sig):
                dve.tensor_tensor(out_, a, b, op).then_inc(sig.sem, 1)

            def layer_norm_stats(k):
                dve.wait_ge(x_loaded.of(k), x_loaded.value(k))
                if k.older(1):
                    dve.wait_ge(xn_ready.sem, xn_ready.value(k.plus(-1)))
                for t in range(T):
                    dve.bn_stats(stats[:, t, :], x_sb[:, k.slot, t, :]).then_inc(ln_step.sem, 1)
                dve.wait_ge(ln_step.sem, ln_step.value(k, T))
                tt(moments[:, 0], stats[:, :, 1], stats[:, :, 4], ALU.add, ln_step)
                tt(moments[:, 1], stats[:, :, 1], stats[:, :, 4], ALU.subtract, ln_step)
                tt(moments[:, 2], stats[:, :, 2], stats[:, :, 5], ALU.add, ln_step)
                dve.wait_ge(ln_step.sem, ln_step.value(k, T + 3))
                dve.scalar_tensor_tensor(moments[:, 1], moments[:, 1], C / 4.0, moments[:, 1],
                                         ALU.mult, ALU.mult).then_inc(ln_step.sem, 1)
                dve.tensor_scalar(moments[:, 0], moments[:, 0], -0.5, None, ALU.mult).then_inc(ln_step.sem, 1)
                dve.wait_ge(ln_step.sem, ln_step.value(k, T + 4))
                tt(moments[:, 2], moments[:, 1], moments[:, 2], ALU.add, ln_step)

            def invert_sd(k):
                dve.wait_ge(sd_ready.sem, sd_ready.value(k))
                dve.reciprocal(rstd[:], sd[:]).then_inc(ln_step.sem, 1)

            def norm_squares(k):
                dve.wait_ge(sq_ready.sem, sq_ready.value(k))
                dve.tensor_reduce(ss[:, 0, :], sq.rearrange("p t (g d) -> p (t g) d", d=HD), AX_X,
                                  ALU.add).then_inc(ss_step.sem, 1)
                dve.wait_ge(ss_step.sem, ss_step.value(k, 1))
                dve.tensor_scalar(ss[:, 1, :], ss[:, 0, :], 1e-24, None, ALU.max).then_inc(ss_step.sem, 1)

            def normalise(k):
                dve.wait_ge(norm_ready.sem, norm_ready.value(k))
                dve.tensor_scalar(rnorm[:], norm[:], 1e-12, None, ALU.max).then_inc(rnorm_step.sem, 1)
                dve.wait_ge(rnorm_step.sem, rnorm_step.value(k, 1))
                dve.reciprocal(rnorm[:], rnorm[:]).then_inc(rnorm_step.sem, 1)
                dve.wait_ge(rnorm_step.sem, rnorm_step.value(k))
                if k.older(1):
                    dve.wait_ge(depth0.sem, depth0.value(k.plus(-1)))
                if k.older(2):
                    dve.wait_ge(pool_prod.sem, pool_prod.value(k.plus(-2)))
                rn = rnorm[:].rearrange("p (t g) -> p t g", t=T)
                tt(a0[:].rearrange("p (t q) (h d) -> p t (q h) d", t=T, d=HD),
                   qkv[:, :, 0:2 * C].rearrange("p t (g d) -> p t g d", d=HD),
                   rn[:, :, 0:2 * NH].unsqueeze(3).to_broadcast([P, T, 2 * NH, HD]), ALU.mult, a0_ready)
                tt(vT[:, k.slot].rearrange("p t d j -> p t j d"),
                   qkv[:, :, 2 * C:QKV].rearrange("p t (g d) -> p t g d", d=HD),
                   rn[:, :, 2 * NH:3 * NH].unsqueeze(3).to_broadcast([P, T, NH, HD]), ALU.mult, v_ready)
                if k.number == 0:
                    entangle0(dve, k)

            def value_phase(k):
                dve.wait_ge(v_ready.sem, v_ready.value(k))
                dve.tensor_reduce(vsum[:], vT[:, k.slot], AX_X, ALU.add).then_inc(phase_step.sem, 1)
                dve.wait_ge(phase_step.sem, phase_step.value(k, 1))
                dve.tensor_scalar(f_tmp[:, 0], vsum[:], 0.0, None, ALU.is_gt).then_inc(phase_step.sem, 1)
                dve.scalar_tensor_tensor(f_tmp[:, 2], vsum[:], 0.0, bc_mid(ang_of(cos_t, "p"), T),
                                         ALU.is_equal, ALU.mult).then_inc(phase_step.sem, 1)
                dve.wait_ge(phase_step.sem, phase_step.value(k, 2))
                dve.scalar_tensor_tensor(f_tmp[:, 1], vsum[:], 0.0, f_tmp[:, 0],
                                         ALU.is_lt, ALU.subtract).then_inc(phase_step.sem, 1)
                dve.wait_ge(phase_step.sem, phase_step.value(k, 4))
                tt(f_tmp[:, 1], f_tmp[:, 1], bc_mid(ang_of(cos_t, "twop"), T), ALU.mult, phase_step)
                dve.wait_ge(phase_step.sem, phase_step.value(k))
                tt(phase[:, k.slot], f_tmp[:, 2], f_tmp[:, 1], ALU.subtract, phase_ready)

            def route(k):
                done = [0]

                def link(ins):
                    done[0] += 1
                    ins.then_inc(router_step.sem, 1)
                    dve.wait_ge(router_step.sem, router_step.value(k, done[0]))

                def wide(ap):
                    return bc_last(ap, E)

                dve.wait_ge(qkv_ready.sem, qkv_ready.value(k))
                s = qkv[:, :, QKV:PROJ]
                order = bc_mid(rank[:], T)
                best, second, first_at, second_at = (r_one[:, n, :] for n in (0, 4, 1, 5))
                is_first, is_second, rest, tmp = (r_tmp[:, n] for n in range(4))
                link(dve.tensor_reduce(best, s, AX_X, ALU.max))
                link(dve.tensor_tensor(tmp, s, wide(best), ALU.is_equal))
                link(dve.tensor_tensor(tmp, tmp, order, ALU.mult))
                link(dve.tensor_reduce(first_at, tmp, AX_X, ALU.max))
                link(dve.tensor_tensor(is_first, tmp, wide(first_at), ALU.is_equal))
                link(dve.scalar_tensor_tensor(rest, is_first, -3e38, s, ALU.mult, ALU.add))
                link(dve.tensor_reduce(second, rest, AX_X, ALU.max))
                dve.tensor_tensor(r_one[:, 2, :], second, best, ALU.subtract).then_inc(router_diff.sem, 1)
                link(dve.tensor_tensor(tmp, rest, wide(second), ALU.is_equal))
                link(dve.tensor_tensor(tmp, tmp, order, ALU.mult))
                link(dve.tensor_reduce(second_at, tmp, AX_X, ALU.max))
                link(dve.tensor_tensor(is_second, tmp, wide(second_at), ALU.is_equal))

            def route_weights(k):
                done = [11]

                def link(ins):
                    done[0] += 1
                    ins.then_inc(router_step.sem, 1)
                    dve.wait_ge(router_step.sem, router_step.value(k, done[0]))

                dve.wait_ge(router_exp.sem, router_exp.value(k))
                if k.older(2):
                    dve.wait_ge(gated_ready.sem, gated_ready.value(k.plus(-2)))
                    dve.wait_ge(cwT_psum.sem, cwT_psum.value(k.plus(-2)))
                w_one, w_two = r_one[:, 7, :], r_one[:, 6, :]
                link(dve.tensor_scalar(w_two, r_one[:, 3, :], 1.0, None, ALU.add))
                link(dve.reciprocal(w_one, w_two))
                link(dve.tensor_tensor(w_two, r_one[:, 3, :], w_one, ALU.mult))
                link(dve.tensor_tensor(r_tmp[:, 2], r_tmp[:, 0], bc_last(w_one, E), ALU.mult))
                link(dve.tensor_tensor(r_tmp[:, 3], r_tmp[:, 1], bc_last(w_two, E), ALU.mult))
                tt(cw[:, k.slot, :, 0:E], r_tmp[:, 2], r_tmp[:, 3], ALU.add, cw_ready)

            def products(k, unit):
                n = OWN_UNITS.index(unit)
                slot = n % 2
                slot_summed(dve, k, OWN_UNITS, 2, n)
                if unit[0] == "pattern":
                    if n == 0:
                        dve.wait_ge(grown2.sem, grown2.value(k))
                        dve.wait_ge(sq2_ready.sem, sq2_ready.value(k))
                    if unit[1] in (2, 5):
                        dve.wait_ge(mixed_ready.sem, mixed_ready.value(k))
                    for part, q, kq in pattern_operands(k, unit[1]):
                        last = dve.tensor_tensor(set_of(slot, part), q, kq, ALU.mult)
                else:
                    dve.wait_ge(amp_ready.sem, amp_ready.value(k))
                    w, v = weighted_operands(k, unit[1])
                    last = dve.tensor_tensor(weighted_slot(slot, unit[1]), w, v, ALU.mult)
                last.then_inc(own_prod.sem, 1)

            def sums(k, unit):
                kind, m = unit
                if unit in POOL_UNITS:
                    n, made, summed, slot = POOL_UNITS.index(unit), pool_prod, pool_sum, 2
                else:
                    n, made, summed = OWN_UNITS.index(unit), own_prod, own_sum
                    slot = n % 2
                dve.wait_ge(made.sem, made.value(k, n + 1))
                if kind == "pattern":
                    (t, _), (t2, _) = PATTERN_SETS[m]
                    dst = pat[:, t, 0:2, :] if t == t2 else pat[:, t:t2 + 1, 2, :]
                    src = prod[:, slot, :].rearrange("p (n g d) -> p n g d", n=2, d=HD)
                else:
                    t, c = m // 2, 2 * (m % 2)
                    dst = u[:, t, c:c + 2, :].rearrange("p c e -> p (c e)")
                    src = prod[:, slot, :].rearrange("p (g j) -> p g j", j=NH)
                dve.tensor_reduce(dst, src, AX_X, ALU.add).then_inc(summed.sem, 1)

            def grown(k, sig, grow_sig, dst_x, dst_y):
                dve.wait_ge(grow_sig.sem, grow_sig.value(k))
                dve.scalar_tensor_tensor(dst_x, zp, 1.0, x1[:, :, HD:C], ALU.add, ALU.mult).then_inc(sig.sem, 1)
                dve.scalar_tensor_tensor(dst_y, zm, 1.0, y1[:, :, HD:C], ALU.add, ALU.mult).then_inc(sig.sem, 1)

            def grown_once(k):
                if k.number == 0:
                    entangle1(dve, k)
                grown(k, grown1, grow1, x2[:, :, 0:NT * HD], y2[:, :, 0:NT * HD])
                if k.number == 0:
                    turn(dve, k)

            def grown_twice(k):
                if k.number == 0:
                    entangle2(dve, k)
                if k.older(2):
                    o = k.plus(-2)
                    pattern_summed(dve, o)
                grown(k, grown2, grow2, fx[:, k.slot, :, 0:NT * HD], fy[:, k.slot, :, 0:NT * HD])

            def pattern_power(k):
                pattern_summed(dve, k)
                a, b, c = (pat[:, :, n, :] for n in range(3))
                tt(pr[:, 1], a, b, ALU.subtract, power_step)
                tt(pr[:, 0], a, b, ALU.add, power_step)
                dve.wait_ge(power_step.sem, power_step.value(k, 1))
                tt(pr[:, 2], pr[:, 1], c, ALU.add, power_step)
                dve.wait_ge(power_step.sem, power_step.value(k, 2))
                tt(pr[:, 0], pr[:, 0], pr[:, 0], ALU.mult, power_step)
                dve.wait_ge(power_step.sem, power_step.value(k, 3))
                tt(pr[:, 1], pr[:, 2], pr[:, 2], ALU.mult, power_step)
                dve.wait_ge(power_step.sem, power_step.value(k, 5))
                tt(power, pr[:, 0], pr[:, 1], ALU.add, power_step)
                dve.wait_ge(power_step.sem, power_step.value(k))
                rows = power.rearrange("p t (i j) -> p (t i) j", j=NH)
                dve.tensor_reduce(rowmax[:], rows, AX_X, ALU.max).then_inc(below_step.sem, 1)
                dve.wait_ge(below_step.sem, below_step.value(k, 1))
                tt(below[:].rearrange("p t (i j) -> p (t i) j", j=NH), rows, bc_last(rowmax[:], NH),
                   ALU.subtract, below_step)

            def probabilities(k):
                dve.wait_ge(exp_ready.sem, exp_ready.value(k))
                rows = expo[:].rearrange("p t c (i j) -> p (t c i) j", j=NH)
                dve.tensor_reduce(zsum[:], rows, AX_X, ALU.add).then_inc(probs_step.sem, 1)
                dve.wait_ge(probs_step.sem, probs_step.value(k, 1))
                dve.reciprocal(rz[:], zsum[:]).then_inc(probs_step.sem, 1)
                dve.wait_ge(probs_step.sem, probs_step.value(k, 2))
                tt(rows, rows, bc_last(rz[:], NH), ALU.mult, probs_step)

            def clip_and_mix(k):
                dve.wait_ge(abs_ready.sem, abs_ready.value(k))
                dve.wait_ge(sgn_ready.sem, sgn_ready.value(k))
                dve.tensor_scalar(u[:], u[:], 1e-6, 1.0, ALU.max, ALU.min).then_inc(clip_ready.sem, 1)
                dve.wait_ge(clip_ready.sem, clip_ready.value(k))
                for c in range(NC):
                    dve.scalar_tensor_tensor(u_sgn[:, :, c, :], u[:, :, c, :], sup[:, c:c + 1], u_sgn[:, :, c, :],
                                             ALU.mult, ALU.mult).then_inc(mix_ready.sem, 1)

            def measure(k):
                dve.wait_ge(msum_step.sem, msum_step.value(k))
                dve.wait_ge(phase_ready.sem, phase_ready.value(k))
                if k.older(1):
                    dve.wait_ge(mT_psum.sem, mT_psum.value(k.plus(-1)))
                tt(meas[:].rearrange("p t (i d) -> p t i d", d=HD), msum[:].rearrange("p t (i d) -> p t i d", d=HD),
                   phase[:, k.slot].unsqueeze(2).to_broadcast([P, T, NH, HD]), ALU.mult, meas_ready)

            def add_out(k):
                dve.wait_ge(o_psum.sem, o_psum.value(k))
                dve.wait_ge(y_added.sem, y_added.value(k))
                tt(yacc[:, k.slot], ps_t[:].rearrange("p (t c) -> p t c", t=T), yacc[:, k.slot], ALU.add, out_ready)

            def step(k):
                o, n, far = k.plus(-1), k.plus(1), k.plus(2)
                if k.exists(NB):
                    products(k, ("pattern", 0))
                    sums(k, ("pattern", 0))
                if o.exists(NB):
                    sums(o, ("weighted", 6))
                if k.exists(NB):
                    products(k, ("pattern", 2))
                if o.exists(NB):
                    clip_and_mix(o)
                if n.exists(NB):
                    norm_squares(n)
                if k.exists(NB):
                    sums(k, ("pattern", 1))
                if n.exists(NB):
                    normalise(n)
                    route(n)
                if k.exists(NB):
                    sums(k, ("pattern", 2))
                if o.exists(NB):
                    measure(o)
                if k.exists(NB):
                    products(k, ("pattern", 3))
                    sums(k, ("pattern", 3))
                    sums(k, ("pattern", 4))
                    products(k, ("pattern", 5))
                    sums(k, ("pattern", 5))
                    pattern_power(k)
                if o.exists(NB):
                    add_out(o)
                if n.exists(NB):
                    route_weights(n)
                if k.exists(NB):
                    probabilities(k)
                if n.exists(NB):
                    grown_once(n)
                if far.exists(NB):
                    layer_norm_stats(far)
                if k.exists(NB):
                    products(k, ("weighted", 0))
                    products(k, ("weighted", 2))
                    sums(k, ("weighted", 2))
                    products(k, ("weighted", 3))
                    products(k, ("weighted", 5))
                    sums(k, ("weighted", 3))
                if far.exists(NB):
                    invert_sd(far)
                if k.exists(NB):
                    products(k, ("weighted", 7))
                if n.exists(NB):
                    value_phase(n)
                if k.exists(NB):
                    sums(k, ("weighted", 4))
                    sums(k, ("weighted", 7))
                if n.exists(NB):
                    grown_twice(n)

            step(first)
            angle_constants()
            run_steps(dve, step)


_INS = ["query", "W_qkv", "b_qkv", "W_out", "b_out", "quantum_weights", "photonic_phases", "entanglement_gates",
        "superposition_logits"]
_FFN = ["Wg", "W1", "b1", "W2", "b2"]


def kernel(**inputs):
    import numpy as _np
    import concourse.bacc as _bacc
    from concourse import mybir as _mybir
    from concourse.bass_utils import run_bass_kernel_spmd as _run

    nc = _bacc.Bacc("TRN2", target_bir_lowering=False, num_devices=1)
    arrays, args = {}, []
    for name in ["L0_attn_" + n for n in _INS] + ["L0_ffn_" + n for n in _FFN]:
        a = _np.ascontiguousarray(inputs[name])
        arrays[f"in_{name}_dram"] = a
        args.append(nc.dram_tensor(f"in_{name}_dram", a.shape, _mybir.dt.from_np(a.dtype), kind="ExternalInput").ap())
    shape = inputs["L0_attn_query"].shape
    args.append(nc.dram_tensor("out_0_dram", shape, _mybir.dt.float32, kind="ExternalOutput").ap())
    build(nc, *args)
    r = _run(nc, [arrays], core_ids=[0])
    return r.results[0]["out_0_dram"]
```
